# Optimizing a Trainium2 kernel written in Bass

```python
import numpy as np
import jax
import jax.numpy as jnp

def _softmax(x, axis=-1):
    return jax.nn.softmax(x, axis=axis)

def _gelu(x):
    return jax.nn.gelu(x, approximate=True)

def _silu(x):
    return jax.nn.silu(x)

def _sigmoid(x):
    return jax.nn.sigmoid(x)

def _layernorm(x, axis=-1, eps=1e-05):
    m = jnp.mean(x, axis=axis, keepdims=True)
    v = jnp.var(x, axis=axis, keepdims=True)
    return (x - m) / jnp.sqrt(v + eps)

def _scatter_add(tgt, idx, src, axis=0):
    return tgt.at[idx].add(src)

def _segment_sum(src, seg, n):
    return jax.ops.segment_sum(src, seg, n)
kernel_name = 'mk_gnn_ffn_d1_gnn_r8_e05ddd'

def setup_inputs(seed: int=0):
    np.random.seed(seed)
    _w = jnp.asarray

    def _rec_inputs():
        import jax
        import jax.numpy as jnp
        _gk = jax.random.key(seed)
        x = -6.415e-05 + 1 * jax.random.normal(jax.random.fold_in(_gk, 1), (1250, 512), jnp.float32)
        src = jax.random.randint(jax.random.fold_in(_gk, 2), (40000,), 0, 1250, jnp.int32)
        dst = jnp.minimum((1250 * jax.random.uniform(jax.random.fold_in(_gk, 3), (40000,)) ** 2.0).astype(jnp.int32), 9999)
        _o = jnp.argsort(dst, stable=True)
        src = src[_o]
        dst = dst[_o]
        edge_attr_32 = jax.random.uniform(jax.random.fold_in(_gk, 11), (40000, 32), jnp.float32, 0.0, 1)
        edge_attr_4 = 0.000937891 + 0.999965 * jax.random.normal(jax.random.fold_in(_gk, 12), (40000, 4), jnp.float32)
        return (x, src, dst, edge_attr_32, edge_attr_4)
    x, src, dst, edge_attr_32, edge_attr_4 = _rec_inputs()

    def _L0_gnn_setup():
        import jax, jax.numpy as jnp
        import numpy as np
        import math
        N, E = (2500, 25000)
        MUL = 128
        D = MUL + 3 * MUL
        EDGE_ATTR = 32
        HID = 32
        LOG2 = math.log(2.0)

        def ssp(x):
            return jax.nn.softplus(x) - LOG2

        def split_irreps(x):
            return (x[:, :MUL], x[:, MUL:].reshape(x.shape[0], MUL, 3))

        def merge_irreps(x0, x1):
            return jnp.concatenate([x0, x1.reshape(x1.shape[0], MUL * 3)], axis=-1)

        def irrep_linear(x, W0, b0, W1):
            x0, x1 = split_irreps(x)
            y0 = x0 @ W0 + b0
            y1 = jnp.einsum('nuc,uv->nvc', x1, W1)
            return merge_irreps(y0, y1)
        key = jax.random.key(seed)
        ks = iter(jax.random.split(key, 32))

        def randn(shape, scale=1.0):
            return (scale * jax.random.normal(next(ks), shape)).astype(jnp.float32)
        inp = {'x': randn((N, D)), 'edge_sh': randn((E, 4)), 'edge_attr': jax.random.uniform(next(ks), (E, EDGE_ATTR), dtype=jnp.float32), 'edge_index': jax.random.randint(next(ks), (2, E), 0, N, dtype=jnp.int32), 'W_pre0': randn((MUL, MUL), MUL ** (-0.5)), 'b_pre0': jnp.zeros((MUL,), jnp.float32), 'W_pre1': randn((MUL, MUL), MUL ** (-0.5)), 'W_nd0': randn((MUL, MUL), MUL ** (-0.5)), 'b_nd0': jnp.zeros((MUL,), jnp.float32), 'W_nd1': randn((MUL, MUL), MUL ** (-0.5)), 'W_g1': randn((2 * MUL, 2 * MUL), (2 * MUL) ** (-0.5)), 'b_g1': jnp.zeros((2 * MUL,), jnp.float32), 'W_g2': randn((2 * MUL, 2 * MUL), (2 * MUL) ** (-0.5)), 'b_g2': jnp.zeros((2 * MUL,), jnp.float32), 'W_f1': randn((EDGE_ATTR, HID), EDGE_ATTR ** (-0.5)), 'W_f2': randn((HID, 4 * MUL), HID ** (-0.5)), 'W_s1': randn((3 * MUL, HID), (3 * MUL) ** (-0.5)), 'W_s2': randn((HID, 4 * MUL), HID ** (-0.5)), 'W_o0': randn((MUL, MUL), MUL ** (-0.5)), 'b_o0': jnp.zeros((MUL,), jnp.float32), 'W_o1': randn((MUL, MUL), MUL ** (-0.5))}
        return inp
    _L0_gnn_all = _L0_gnn_setup()
    _L0_gnn_in = {k: v for k, v in _L0_gnn_all.items() if k in ('W_pre0', 'b_pre0', 'W_pre1', 'W_nd0', 'b_nd0', 'W_nd1', 'W_g1', 'b_g1', 'W_g2', 'b_g2', 'W_f1', 'W_f2', 'W_s1', 'W_s2', 'W_o0', 'b_o0', 'W_o1')}
    del _L0_gnn_all

    def _L0_ffn_setup():
        import jax, jax.numpy as jnp
        import numpy as np
        TOP_K = 2
        key = jax.random.key(seed)
        ks = jax.random.split(key, 4)
        b, t, d, e, h = (2, 256, 512, 8, 1024)
        scale = 0.02
        return {'x': jax.random.normal(ks[0], (b, t, d), dtype=jnp.float32), 'router_w': jax.random.normal(ks[1], (e, d), dtype=jnp.float32) * scale, 'router_b': jnp.zeros((e,), dtype=jnp.float32), 'fc1_w': jax.random.normal(ks[2], (e, 2 * h, d), dtype=jnp.float32) * scale, 'fc1_b': jnp.zeros((e, 2 * h), dtype=jnp.float32), 'fc2_w': jax.random.normal(ks[3], (e, d, h), dtype=jnp.float32) * scale, 'fc2_b': jnp.zeros((e, d), dtype=jnp.float32)}
    _L0_ffn_all = _L0_ffn_setup()
    _L0_ffn_in = {k: v for k, v in _L0_ffn_all.items() if k in ('router_w', 'router_b', 'fc1_w', 'fc1_b', 'fc2_w', 'fc2_b')}
    del _L0_ffn_all
    return {'x': x, 'src': src, 'dst': dst, 'edge_attr_32': edge_attr_32, 'edge_attr_4': edge_attr_4, 'L0_gnn_W_pre0': _L0_gnn_in['W_pre0'], 'L0_gnn_b_pre0': _L0_gnn_in['b_pre0'], 'L0_gnn_W_pre1': _L0_gnn_in['W_pre1'], 'L0_gnn_W_nd0': _L0_gnn_in['W_nd0'], 'L0_gnn_b_nd0': _L0_gnn_in['b_nd0'], 'L0_gnn_W_nd1': _L0_gnn_in['W_nd1'], 'L0_gnn_W_g1': _L0_gnn_in['W_g1'], 'L0_gnn_b_g1': _L0_gnn_in['b_g1'], 'L0_gnn_W_g2': _L0_gnn_in['W_g2'], 'L0_gnn_b_g2': _L0_gnn_in['b_g2'], 'L0_gnn_W_f1': _L0_gnn_in['W_f1'], 'L0_gnn_W_f2': _L0_gnn_in['W_f2'], 'L0_gnn_W_s1': _L0_gnn_in['W_s1'], 'L0_gnn_W_s2': _L0_gnn_in['W_s2'], 'L0_gnn_W_o0': _L0_gnn_in['W_o0'], 'L0_gnn_b_o0': _L0_gnn_in['b_o0'], 'L0_gnn_W_o1': _L0_gnn_in['W_o1'], 'L0_ffn_router_w': _L0_ffn_in['router_w'], 'L0_ffn_router_b': _L0_ffn_in['router_b'], 'L0_ffn_fc1_w': _L0_ffn_in['fc1_w'], 'L0_ffn_fc1_b': _L0_ffn_in['fc1_b'], 'L0_ffn_fc2_w': _L0_ffn_in['fc2_w'], 'L0_ffn_fc2_b': _L0_ffn_in['fc2_b']}

def reference(x, src, dst, edge_attr_32, edge_attr_4, L0_gnn_W_pre0, L0_gnn_b_pre0, L0_gnn_W_pre1, L0_gnn_W_nd0, L0_gnn_b_nd0, L0_gnn_W_nd1, L0_gnn_W_g1, L0_gnn_b_g1, L0_gnn_W_g2, L0_gnn_b_g2, L0_gnn_W_f1, L0_gnn_W_f2, L0_gnn_W_s1, L0_gnn_W_s2, L0_gnn_W_o0, L0_gnn_b_o0, L0_gnn_W_o1, L0_ffn_router_w, L0_ffn_router_b, L0_ffn_fc1_w, L0_ffn_fc1_b, L0_ffn_fc2_w, L0_ffn_fc2_b):
    import jax
    import jax.numpy as jnp

    def _L0_gnn_ref(x, edge_sh, edge_attr, edge_index, W_pre0, b_pre0, W_pre1, W_nd0, b_nd0, W_nd1, W_g1, b_g1, W_g2, b_g2, W_f1, W_f2, W_s1, W_s2, W_o0, b_o0, W_o1):
        import jax, jax.numpy as jnp
        import numpy as np
        import math
        N, E = (2500, 25000)
        MUL = 128
        D = MUL + 3 * MUL
        EDGE_ATTR = 32
        HID = 32
        LOG2 = math.log(2.0)

        def ssp(x):
            return jax.nn.softplus(x) - LOG2

        def split_irreps(x):
            return (x[:, :MUL], x[:, MUL:].reshape(x.shape[0], MUL, 3))

        def merge_irreps(x0, x1):
            return jnp.concatenate([x0, x1.reshape(x1.shape[0], MUL * 3)], axis=-1)

        def irrep_linear(x, W0, b0, W1):
            x0, x1 = split_irreps(x)
            y0 = x0 @ W0 + b0
            y1 = jnp.einsum('nuc,uv->nvc', x1, W1)
            return merge_irreps(y0, y1)
        edge_dst, edge_src = (edge_index[0], edge_index[1])
        old_x = x
        pre = irrep_linear(x, W_pre0, b_pre0, W_pre1)
        p0, p1 = split_irreps(pre)
        pd0 = p0[edge_dst]
        ip1 = jnp.einsum('eum,eum->eu', p1[edge_dst], p1[edge_src]) / 3.0
        s0 = jnp.concatenate([pd0, pd0, ip1], axis=-1)
        x0, x1 = split_irreps(x)
        n1 = jnp.sqrt(jnp.sum(x1 * x1, axis=-1) / 3.0)
        g = jax.nn.silu(jnp.concatenate([x0, n1], -1) @ W_g1 + b_g1) @ W_g2 + b_g2
        xg = merge_irreps(g[:, :MUL], x1 * g[:, MUL:, None])
        x = irrep_linear(xg, W_nd0, b_nd0, W_nd1)
        self_x = x
        w = ssp(edge_attr @ W_f1) @ W_f2 * (ssp(s0 @ W_s1) @ W_s2)
        w1, w2, w3, w4 = jnp.split(w, 4, axis=-1)
        x0e, x1e = split_irreps(x[edge_src])
        sh0, sh1 = (edge_sh[:, 0], edge_sh[:, 1:4])
        out0 = w1 * x0e * sh0[:, None] + w4 * (jnp.einsum('eum,em->eu', x1e, sh1) / jnp.sqrt(3.0))
        out1 = w2[:, :, None] * x0e[:, :, None] * sh1[:, None, :] + w3[:, :, None] * x1e * sh0[:, None, None]
        edge_feat = merge_irreps(out0, out1)
        out = jax.ops.segment_sum(edge_feat, edge_dst, num_segments=old_x.shape[0])
        out = out + self_x
        out = irrep_linear(out, W_o0, b_o0, W_o1)
        return out + old_x

    def _L0_ffn_ref(x, router_w, router_b, fc1_w, fc1_b, fc2_w, fc2_b):
        import jax, jax.numpy as jnp
        import numpy as np
        TOP_K = 2
        n_experts = router_w.shape[0]
        temp = 1.0
        logits = (jnp.einsum('btd,ed->bte', x, router_w) + router_b) / temp
        topk_val, topk_idx = jax.lax.top_k(logits, TOP_K)
        weights = jax.nn.softmax(topk_val, axis=-1)
        onehot = jax.nn.one_hot(topk_idx, n_experts, dtype=x.dtype)
        cw = jnp.einsum('btk,btke->bte', weights, onehot)
        h = jnp.einsum('btd,efd->btef', x, fc1_w) + fc1_b
        h1, h2 = jnp.split(h, 2, axis=-1)
        a = jax.nn.silu(h1) * h2
        y = jnp.einsum('bteh,edh->bted', a, fc2_w) + fc2_b
        out = jnp.einsum('bted,bte->btd', y, cw)
        return out
    edge_index = jnp.stack([src, dst])
    x = x + _L0_gnn_ref(_layernorm(x, axis=-1), edge_attr_4, edge_attr_32, edge_index, L0_gnn_W_pre0, L0_gnn_b_pre0, L0_gnn_W_pre1, L0_gnn_W_nd0, L0_gnn_b_nd0, L0_gnn_W_nd1, L0_gnn_W_g1, L0_gnn_b_g1, L0_gnn_W_g2, L0_gnn_b_g2, L0_gnn_W_f1, L0_gnn_W_f2, L0_gnn_W_s1, L0_gnn_W_s2, L0_gnn_W_o0, L0_gnn_b_o0, L0_gnn_W_o1)
    x = x + _L0_ffn_ref(_layernorm(x, axis=-1)[None], L0_ffn_router_w, L0_ffn_router_b, L0_ffn_fc1_w, L0_ffn_fc1_b, L0_ffn_fc2_w, L0_ffn_fc2_b)[0]
    return x

_drawn_inputs = setup_inputs


def setup_inputs(seed=0):
    import zlib

    import numpy as np

    out = dict(_drawn_inputs(seed))
    spreads = {'L0_gnn_b_pre0': (0.0, 0.311),
     'L0_gnn_b_nd0': (0.0, 0.1),
     'L0_gnn_b_g1': (0.0, 0.1),
     'L0_gnn_b_g2': (0.0, 0.1),
     'L0_gnn_b_o0': (0.0, 0.352),
     'L0_ffn_router_b': (0.0, 0.521),
     'L0_ffn_fc1_b': (0.0, 0.8),
     'L0_ffn_fc2_b': (0.0, 0.1)}
    factors = {}
    for name, (base, spread) in spreads.items():
        noise = np.random.default_rng([zlib.crc32(name.encode()), seed]).standard_normal(out[name].shape)
        drawn = base * np.exp(spread * noise) if base else spread * noise
        out[name] = jnp.asarray(drawn.astype(out[name].dtype))
    for name, factor in factors.items():
        out[name] = (out[name] * factor).astype(out[name].dtype)
    return out
```

```python
from contextlib import ExitStack

import numpy as np
import concourse.bass as bass
from concourse import mybir

F32 = mybir.dt.float32
F32R = mybir.dt.float32r
I32 = mybir.dt.int32
ALU = mybir.AluOpType
ACT = mybir.ActivationFunctionType

N, D, E = 1250, 512, 40000
MUL = 128
G = 10
NG = N // G
EP = 125
EC = E // EP
STEP = 256
STEPS = (E - G) // STEP + G
REC = 38
A_LOC, B_ID, SH, ATTR = 0, 1, 2, 6
RECK = ATTR + 32
HID = 32
ROW = 3 * MUL + 4 * MUL
CH = 8
FILLS = 4
NEXP = 8
FF = 1024
EPS = 1e-5
TOK = 250
CHUNKS = N // TOK


def wait(eng, sem, value):
    if isinstance(value, int) and value <= 0:
        return
    eng.wait_ge(sem, value)


def prepare(nc, a, keep, scratch):
    with ExitStack() as ctx:
        def sb(name, shape, dt=F32):
            return ctx.enter_context(nc.sbuf_tensor(name, shape, dt))

        def ps(name, shape, dt=F32):
            return ctx.enter_context(nc.psum_tensor(name, shape, dt))

        def sem(name):
            return ctx.enter_context(nc.semaphore(name))

        rec_all = sb("rec_all", [EP, EC, REC])
        stage = [sb(f"stage{i}", [EP, CH, REC]) for i in range(2)]
        stage_pos = [sb(f"stage_pos{i}", [EP, CH], I32) for i in range(2)]
        a_int = sb("a_int", [EP, EC], I32)
        b_int = sb("b_int", [EP, EC], I32)
        a_f = sb("a_f", [EP, EC])
        grp = sb("grp", [EP, EC])
        mask = sb("mask", [EP, EC])
        zeros_e = sb("zeros_e", [EP, EC])
        rank = sb("rank", [EP, G, EC])
        picked = sb("picked", [EP, EC])
        pos = a_f
        pos_i = sb("pos_i", [EP, EC], I32)
        small = sb("small", [EP, 5, G])
        cnt_i = sb("cnt_i", [EP, 2, G], I32)
        step_no = sb("step_no", [1, STEPS])
        step_f = sb("step_f", [1, STEPS])
        zero_fill = sb("zero_fill", [128, STEPS * STEP * REC // (FILLS * 128)])
        tri = sb("tri", [EP, EP])
        onesq = sb("onesq", [EP, EP])
        stats = sb("stats", [NG, G, 6])
        mv = sb("mv", [NG, G, 2])
        std = sb("std", [NG, G])
        rstd = sb("rstd", [NG, G])
        eps_t = sb("eps_t", [NG, 1])
        wpre0 = sb("wpre0", [128, MUL])
        wpre1 = sb("wpre1", [128, MUL])
        wnd0 = sb("wnd0", [128, MUL])
        wnd1 = sb("wnd1", [128, MUL])
        wg1 = sb("wg1", [128, 2, 2 * MUL])
        wg2 = sb("wg2", [128, 2, 2 * MUL])
        bpre0 = sb("bpre0", [128, 1])
        bg1 = sb("bg1", [128, 2])
        bg2 = sb("bg2", [128, 2])
        bnd0 = sb("bnd0", [1, MUL])
        ones_row = sb("ones_row", [1, NG])
        ws1ab = sb("ws1ab", [128, 2, 4, HID])
        xs = sb("xs", [NG, 4, MUL])
        xT = sb("xT", [128, 4, NG])
        sq = sb("sq", [128, 3, NG])
        n1s = sb("n1s", [128, 2, NG])
        n1T = sb("n1T", [128, NG])
        p0T = sb("p0T", [128, NG])
        hT = sb("hT", [128, 2, NG])
        gT = sb("gT", [128, 2, NG])
        xgT = sb("xgT", [128, 3, NG])
        brow = sb("brow", [NG, ROW])
        ps_prefix = ps("ps_prefix", [EP, 2, G])
        ps_xT = ps("ps_xT", [128, 4, NG])
        ps_p0 = ps("ps_p0", [128, NG])
        ps_pre = ps("ps_pre", [NG, 4, MUL])
        ps_g1 = ps("ps_g1", [128, 2, NG])
        ps_g2 = ps("ps_g2", [128, 2, NG])
        ps_nd = ps("ps_nd", [NG, 4, MUL])

        rec_in = sem("rec_in")
        ab_in = sem("ab_in")
        x_in = sem("x_in")
        w_in = sem("w_in")
        w4_in = sem("w4_in")
        zeros_set = sem("zeros_set")
        filled = sem("filled")
        consts = sem("consts")
        wide_consts = sem("wide_consts")
        dve_step = sem("dve_step")
        rec_done = sem("rec_done")
        totals = sem("totals")
        prefixed = sem("prefixed")
        pos_done = sem("pos_done")
        stage_seen = sem("stage_seen")
        staged = [sem(f"staged{i}") for i in range(2)]
        scattered = [sem(f"scattered{i}") for i in range(2)]
        var_done = sem("var_done")
        std_done = sem("std_done")
        split_hi = sem("split_hi")
        xs_ready = sem("xs_ready")
        xT_ps = sem("xT_ps")
        xT_ready = sem("xT_ready")
        sq_ready = sem("sq_ready")
        sq_sum = sem("sq_sum")
        n1_sum = sem("n1_sum")
        n1_ready = sem("n1_ready")
        p0_ps = sem("p0_ps")
        p0_ready = sem("p0_ready")
        pre_ps = sem("pre_ps")
        tab_hi = sem("tab_hi")
        tab_done = sem("tab_done")
        g1_ps = sem("g1_ps")
        h_ready = sem("h_ready")
        g2_ps = sem("g2_ps")
        g_ready = sem("g_ready")
        xg_ready = sem("xg_ready")
        nd_ps = sem("nd_ps")
        acc_ready = sem("acc_ready")
        row_pre = sem("row_pre")
        row_ready = sem("row_ready")
        row_out = sem("row_out")
        block = ctx.enter_context(nc.Block())

        WDMA = 16 * 19

        @block.sync
        def _(sp):
            sp.dma_start(a_int[:, :], a["src"].rearrange("(p c) -> p c", p=EP)).then_inc(ab_in, 16)
            sp.dma_start(b_int[:, :], a["dst"].rearrange("(p c) -> p c", p=EP)).then_inc(ab_in, 16)
            sp.dma_start(rec_all[:, :, :], a["rec"].rearrange("(p c) r -> p c r", p=EP)).then_inc(rec_in, 16)
            sp.dma_start(keep["x"][:, :, :], a["x"].rearrange("(g p) d -> p g d", p=NG)).then_inc(x_in, 16)
            sp.wait_ge(zeros_set, 1)
            fill = scratch["sorted"].rearrange("(k p f) r -> k p (f r)", k=FILLS, p=128)
            for i in range(FILLS):
                sp.dma_start(fill[i], zero_fill[:, :]).then_inc(filled, 16)
            sp.wait_ge(rec_done, 2)
            sp.wait_ge(pos_done, 1)

            def stage_pair(r):
                for i in range(2):
                    wait(sp, scattered[i], r * 16 * CH)
                    col = (2 * r + i) * CH
                    sp.dma_start(stage[i][:, :, :], rec_all[:, bass.ds(col, CH), :]).then_inc(staged[i], 16)
                    sp.dma_start(stage_pos[i][:, :], pos_i[:, bass.ds(col, CH)]).then_inc(staged[i], 16)
            stage_pair(0)
            with sp.Fori(1, EC // (2 * CH)) as r:
                stage_pair(r)

        @block.gpsimd
        def _(pool):
            pool.memset(zero_fill[:, :], 0.0).then_inc(zeros_set, 1)
            pool.memset(keep["half"][:, :], 0.5).then_inc(zeros_set, 1)
            pool.memset(keep["ident"][:, :], 0.0).then_inc(wide_consts, 1)
            pool.memset(onesq[:, :], 1.0).then_inc(wide_consts, 1)
            pool.memset(zeros_e[:, :], 0.0).then_inc(wide_consts, 1)
            pool.memset(ones_row[:, :], 1.0).then_inc(wide_consts, 1)
            pool.memset(eps_t[:, :], EPS).then_inc(wide_consts, 1)
            pool.memset(keep["wf1"][:, :, :], 0.0).then_inc(wide_consts, 1)
            pool.iota(keep["iota"][:, :], [[1, NG]], base=0, channel_multiplier=0,
                      allow_small_or_imprecise_dtypes=True).then_inc(wide_consts, 1)
            pool.iota(step_no[:, :], [[STEP, STEPS]], base=0, channel_multiplier=0,
                      allow_small_or_imprecise_dtypes=True).then_inc(wide_consts, 1)
            pool.wait_ge(wide_consts, 8)
            pool.affine_select(out=keep["ident"][:, :], in_=keep["ident"][:, :], compare_op=ALU.not_equal,
                               fill=1.0, base=0, pattern=[[-1, 128]], channel_multiplier=1).then_inc(consts, 1)
            pool.affine_select(out=tri[:, :], in_=onesq[:, :], compare_op=ALU.is_ge,
                               fill=0.0, base=-1, pattern=[[1, EP]], channel_multiplier=-1).then_inc(consts, 1)
            pool.wait_ge(filled, 16 * FILLS)

            def scatter_pair(r):
                for i in range(2):
                    pool.wait_ge(staged[i], 32 * (r + 1))
                    pool.sem_inc(stage_seen, 1)
                    for c in range(CH):
                        pool.indirect_dma_start(
                            out=scratch["sorted"], out_offset=bass.IndirectOffsetOnAxis(ap=stage_pos[i][:, c:c + 1], axis=0),
                            in_=stage[i][:, c, :], in_offset=None).then_inc(scattered[i], 16)
            with pool.Fori(0, EC // (2 * CH)) as r:
                scatter_pair(r)
            for i in range(2):
                pool.wait_ge(scattered[i], 8 * EC)

        @block.vector
        def _(dve):
            done = [0]

            def link(ins):
                done[0] += 1
                ins.then_inc(dve_step, 1)
                dve.wait_ge(dve_step, done[0])

            dve.wait_ge(ab_in, 32)
            link(dve.tensor_copy(a_f[:, :], a_int[:, :]))
            link(dve.tensor_scalar(grp[:, :], a_f[:, :], float(NG), None, ALU.is_ge))
            for g in range(2, G):
                link(dve.scalar_tensor_tensor(grp[:, :], a_f[:, :], float(NG * g), grp[:, :], ALU.is_ge, ALU.add))
            dve.wait_ge(rec_in, 16)
            dve.scalar_tensor_tensor(rec_all[:, :, A_LOC], grp[:, :], float(-NG), a_f[:, :],
                                     ALU.mult, ALU.add).then_inc(rec_done, 1)
            dve.tensor_copy(rec_all[:, :, B_ID], b_int[:, :]).then_inc(rec_done, 1)
            dve.wait_ge(wide_consts, 8)
            dve.wait_ge(rec_done, 2)
            for g in range(G):
                link(dve.tensor_scalar(mask[:, :], grp[:, :], float(g), None, ALU.is_equal))
                link(dve.tensor_tensor_scan(rank[:, g, :], mask[:, :], zeros_e[:, :], 0.0, ALU.add, ALU.add))
            dve.tensor_copy(small[:, 0, :], rank[:, :, EC - 1]).then_inc(totals, 1)
            dve.wait_ge(prefixed, 1)
            link(dve.tensor_scalar(cnt_i[:, 0, :], ps_prefix[:, 1, :], float(STEP - 1), None, ALU.add))
            link(dve.tensor_scalar(cnt_i[:, 1, :], cnt_i[:, 0, :], 8, 8, ALU.logical_shift_right, ALU.logical_shift_left))
            link(dve.tensor_copy(small[:, 1, :], cnt_i[:, 1, :]))
            link(dve.tensor_tensor_scan(small[:, 2, :], small[:, 1, :], zeros_e[:, 0:G], 0.0, ALU.add, ALU.add))
            link(dve.tensor_tensor(small[:, 3, :], small[:, 2, :], small[:, 1, :], ALU.subtract))
            link(dve.scalar_tensor_tensor(small[:, 4, :], small[:, 3, :], -1.0, ps_prefix[:, 0, :], ALU.add, ALU.add))
            for g in range(G):
                dve.scalar_tensor_tensor(rank[:, g, :], rank[:, g, :], small[:, 4, g:g + 1],
                                         zeros_e[:, :], ALU.add, ALU.add).then_inc(dve_step, 1)
                done[0] += 1
                link(dve.tensor_scalar(mask[:, :], grp[:, :], float(g), None, ALU.is_equal))
                if g == 0:
                    link(dve.tensor_tensor(pos[:, :], mask[:, :], rank[:, g, :], ALU.mult))
                else:
                    link(dve.tensor_tensor(picked[:, :], mask[:, :], rank[:, g, :], ALU.mult))
                    link(dve.tensor_tensor(pos[:, :], pos[:, :], picked[:, :], ALU.add))
            dve.tensor_copy(pos_i[:, :], pos[:, :]).then_inc(pos_done, 1)
            link(dve.tensor_scalar(step_f[:, :], step_no[:, :], small[0:1, 3, 1:2], None, ALU.is_ge))
            for g in range(2, G):
                link(dve.scalar_tensor_tensor(step_f[:, :], step_no[:, :], small[0:1, 3, g:g + 1], step_f[:, :],
                                              ALU.is_ge, ALU.add))
            link(dve.tensor_copy(keep["step_group"][:, :], step_f[:, :]))
            dve.wait_ge(w4_in, 16 * 8)
            for w in ("wf2", "ws2"):
                dve.tensor_copy(keep[w][:, :], keep[w + "_raw"][:, :]).then_inc(split_hi, 1)
            dve.wait_ge(split_hi, 2)
            for w in ("wf2", "ws2"):
                for q in (32, 96):
                    link(dve.tensor_tensor(keep[w][q:q + 32, :], keep[w + "_raw"][q:q + 32, :],
                                           keep[w][q:q + 32, :].bitcast(F32), ALU.subtract))
            dve.wait_ge(x_in, 16)
            for t in range(G):
                ins = dve.bn_stats(stats[:, t, :], keep["x"][:, t, :])
            link(ins)
            for t in range(G):
                ins = dve.bn_aggr(mv[:, t, :], stats[:, t, :])
            ins.then_inc(var_done, 1)
            dve.wait_ge(std_done, 1)
            link(dve.reciprocal(rstd[:, :], std[:, :]))
            for t in range(G):
                ins = dve.tensor_scalar(keep["acc"][:, t, :], keep["x"][:, t, :], mv[:, t, 0:1], rstd[:, t:t + 1],
                                        ALU.subtract, ALU.mult)
            link(ins)
            link(dve.tensor_tensor(keep["x"][:, :, :], keep["x"][:, :, :], keep["acc"][:, :, :], ALU.add))

            def tile(t):
                xn_t = keep["acc"][:, bass.ds(t, 1), :]
                wait(dve, xT_ps, t)
                dve.tensor_scalar(xs[:, 0:1, :], xn_t[:, :, 0:MUL], 1.0, None, ALU.mult).then_inc(xs_ready, 1)
                dve.tensor_scalar(xs[:, 1:4, :], xn_t[:, :, MUL:D].rearrange("p g (u m) -> p (g m) u", m=3),
                                  1.0, None, ALU.mult).then_inc(xs_ready, 1)
                dve.wait_ge(sq_ready, t + 1)
                dve.tensor_tensor(n1s[:, 0, :], sq[:, 0, :], sq[:, 1, :], ALU.add).then_inc(sq_sum, 1)
                dve.wait_ge(sq_sum, t + 1)
                dve.tensor_tensor(n1s[:, 1, :], n1s[:, 0, :], sq[:, 2, :], ALU.add).then_inc(n1_sum, 1)
                dve.wait_ge(pre_ps, t + 1)
                dve.tensor_scalar(keep["tab_hi"][:, bass.ds(t, 1), :], ps_pre[:, :, :].rearrange("p a b -> p (a b)").unsqueeze(1),
                                  1.0, None, ALU.mult).then_inc(tab_hi, 1)
                dve.wait_ge(tab_hi, t + 1)
                dve.tensor_tensor(keep["tab_lo"][:, bass.ds(t, 1), :], ps_pre[:, :, :].rearrange("p a b -> p (a b)").unsqueeze(1),
                                  keep["tab_hi"][:, bass.ds(t, 1), :].bitcast(F32), ALU.subtract).then_inc(tab_done, 1)
                dve.wait_ge(g_ready, 2 * t + 2)
                dve.tensor_tensor(xgT[:, :, :], xT[:, 1:4, :], gT[:, 1:2, :].to_broadcast([128, 3, NG]),
                                  ALU.mult).then_inc(xg_ready, 1)
                dve.wait_ge(nd_ps, t + 1)
                dve.tensor_scalar(keep["acc"][:, bass.ds(t, 1), :], ps_nd[:, :, :].rearrange("p a b -> p (a b)").unsqueeze(1),
                                  1.0, None, ALU.mult).then_inc(acc_ready, 1)
            tile(0)
            with dve.Fori(1, G) as t:
                tile(t)

        @block.scalar
        def _(act):
            for dst, src in ((wpre0[:, :], a["L0_gnn_W_pre0"]), (wpre1[:, :], a["L0_gnn_W_pre1"]),
                             (wnd0[:, :], a["L0_gnn_W_nd0"]), (wnd1[:, :], a["L0_gnn_W_nd1"]),
                             (wg1[:, :, :], a["L0_gnn_W_g1"].rearrange("(c p) j -> p c j", p=128)),
                             (wg2[:, :, :], a["L0_gnn_W_g2"].rearrange("(c p) j -> p c j", p=128)),
                             (bpre0[:, :], a["L0_gnn_b_pre0"].rearrange("(p c) -> p c", c=1)),
                             (bg1[:, :], a["bg1"]),
                             (bg2[:, :], a["bg2"]),
                             (bnd0[:, :], a["L0_gnn_b_nd0"].rearrange("(c p) -> c p", c=1))):
                act.dma_start(dst, src).then_inc(w_in, 16)
            w_s1 = a["L0_gnn_W_s1"].rearrange("(c p) k -> c p k", p=MUL)
            act.wait_ge(wide_consts, 8)
            for q in range(4):
                for c in range(2):
                    act.dma_start(ws1ab[:, c, q, :], w_s1[c]).then_inc(w_in, 16)
                act.dma_start(keep["ws1c"][:, q, :], w_s1[2]).then_inc(w_in, 16)
                act.dma_start(keep["wf1"][ATTR:RECK, q, :], a["L0_gnn_W_f1"]).then_inc(w_in, 16)
                act.dma_start(keep["wf2_raw"][32 * q:32 * q + 32, :], a["wf2"]).then_inc(w4_in, 16)
                act.dma_start(keep["ws2_raw"][32 * q:32 * q + 32, :], a["ws2"]).then_inc(w4_in, 16)
            act.wait_ge(var_done, 1)
            act.activation(std[:, :], mv[:, :, 1], ACT.Sqrt, bias=eps_t[:, :]).then_inc(std_done, 1)
            act.wait_ge(w_in, 16 * 26)

            def tile(t):
                act.wait_ge(xT_ps, t + 1)
                wait(act, nd_ps, t)
                act.activation(xT[:, :, :], ps_xT[:, :, :], ACT.Copy).then_inc(xT_ready, 1)
                act.activation(sq[:, :, :], ps_xT[:, 1:4, :], ACT.Square).then_inc(sq_ready, 1)
                act.wait_ge(n1_sum, t + 1)
                act.activation(n1T[:, :], n1s[:, 1, :], ACT.Sqrt, scale=1.0 / 3.0).then_inc(n1_ready, 1)
                act.wait_ge(p0_ps, t + 1)
                act.activation(p0T[:, :], ps_p0[:, :], ACT.Identity, bias=bpre0[:, :]).then_inc(p0_ready, 1)
                act.wait_ge(g1_ps, t + 1)
                for c in range(2):
                    act.activation(hT[:, c, :], ps_g1[:, c, :], ACT.Silu, bias=bg1[:, c:c + 1]).then_inc(h_ready, 1)
                act.wait_ge(tab_done, t + 1)
                wait(act, row_out, 16 * t)
                act.activation(brow[:, 0:3 * MUL], ps_pre[:, 0:3, :].rearrange("p a b -> p (a b)"), ACT.Copy).then_inc(row_pre, 1)
                act.wait_ge(g2_ps, t + 1)
                for c in range(2):
                    act.activation(gT[:, c, :], ps_g2[:, c, :], ACT.Identity, bias=bg2[:, c:c + 1]).then_inc(g_ready, 1)
                act.wait_ge(acc_ready, t + 1)
                act.activation(brow[:, 3 * MUL:ROW], ps_nd[:, :, :].rearrange("p a b -> p (a b)"), ACT.Copy).then_inc(row_ready, 1)
                act.wait_ge(row_ready, t + 1)
                act.wait_ge(row_pre, t + 1)
                act.dma_start(scratch["rows"][bass.ds(t * NG, NG), :], brow[:, :]).then_inc(row_out, 16)
            tile(0)
            with act.Fori(1, G) as t:
                tile(t)
            act.wait_ge(row_out, 16 * G)

        @block.tensor
        def _(pe):
            pe.wait_ge(consts, 2)
            pe.wait_ge(totals, 1)
            pe.matmul(ps_prefix[:, 0, :], tri[:, :], small[:, 0, :], start=True, stop=True)
            pe.matmul(ps_prefix[:, 1, :], onesq[:, :], small[:, 0, :], start=True, stop=True).then_inc(prefixed, 1)
            pe.wait_ge(w_in, 16 * 26)

            def tile(t):
                pe.wait_ge(xs_ready, 2 * t + 2)
                wait(pe, xT_ready, t)
                wait(pe, sq_ready, t)
                for c in range(4):
                    ins = pe.transpose(ps_xT[:, c, :], xs[:, c, :], keep["ident"][0:NG, 0:NG])
                ins.then_inc(xT_ps, 1)
                pe.wait_ge(xT_ready, t + 1)
                wait(pe, p0_ready, t)
                pe.matmul(ps_p0[:, :], wpre0[:, :], xT[:, 0, :], start=True, stop=True).then_inc(p0_ps, 1)
                wait(pe, tab_done, t)
                wait(pe, row_pre, t)
                for m in range(3):
                    pe.matmul(ps_pre[:, m, :], xT[:, 1 + m, :], wpre1[:, :], start=True, stop=True)
                pe.wait_ge(p0_ready, t + 1)
                for c in range(2):
                    ins = pe.matmul(ps_pre[:, 3, :], p0T[:, :], ws1ab[:, c, :, :].rearrange("p q k -> p (q k)"),
                                    start=(c == 0), stop=(c == 1))
                ins.then_inc(pre_ps, 1)
                pe.wait_ge(n1_ready, t + 1)
                for c in range(2):
                    pe.matmul(ps_g1[:, c, :], wg1[:, 0, c * 128:(c + 1) * 128], xT[:, 0, :], start=True, stop=False)
                    ins = pe.matmul(ps_g1[:, c, :], wg1[:, 1, c * 128:(c + 1) * 128], n1T[:, :], start=False, stop=True)
                ins.then_inc(g1_ps, 1)
                pe.wait_ge(h_ready, 2 * t + 2)
                for c in range(2):
                    for k in range(2):
                        ins = pe.matmul(ps_g2[:, c, :], wg2[:, k, c * 128:(c + 1) * 128], hT[:, k, :],
                                        start=(k == 0), stop=(k == 1))
                ins.then_inc(g2_ps, 1)
                pe.wait_ge(g_ready, 2 * t + 2)
                wait(pe, acc_ready, t)
                wait(pe, row_ready, t)
                pe.matmul(ps_nd[:, 0, :], gT[:, 0, :], wnd0[:, :], start=True, stop=False)
                pe.matmul(ps_nd[:, 0, :], ones_row[:, :], bnd0[:, :], start=False, stop=True)
                pe.wait_ge(xg_ready, t + 1)
                for m in range(3):
                    ins = pe.matmul(ps_nd[:, 1 + m, :], xgT[:, m, :], wnd1[:, :], start=True, stop=True)
                ins.then_inc(nd_ps, 1)
            tile(0)
            with pe.Fori(1, G) as t:
                tile(t)


def edges(nc, keep, scratch):
    U = 3
    with ExitStack() as ctx:
        def sb(name, shape, dt=F32):
            return ctx.enter_context(nc.sbuf_tensor(name, shape, dt))

        def ps(name, shape, dt=F32):
            return ctx.enter_context(nc.psum_tensor(name, shape, dt))

        def sem(name):
            return ctx.enter_context(nc.semaphore(name))

        rec = [sb(f"rec{k}", [128, 2, REC]) for k in range(U)]
        rows = [sb(f"rows{k}", [128, 2, ROW]) for k in range(U)]
        bidx = [sb(f"bidx{k}", [128, 2], I32) for k in range(U)]
        shs = [sb(f"shs{k}", [128, 2, 4]) for k in range(U)]
        sht = [sb(f"sht{k}", [128, 2, 3]) for k in range(U)]
        oh = [sb(f"oh{k}", [128, 2, NG]) for k in range(U)]
        q0s = [sb(f"q0s{k}", [NG, 2, MUL], F32R) for k in range(U)]
        recT = [sb(f"recT{k}", [RECK, 2, 128]) for k in range(U)]
        ohT = [sb(f"ohT{k}", [NG, 2, 128], F32R) for k in range(U)]
        prod = sb("prod", [128, 2, 3 * MUL])
        ipT = sb("ipT", [128, 2, 128])
        soft = sb("soft", [128, 512])
        ssp = sb("ssp", [128, 512])
        z = [sb(f"z{k}", [128, 4, 128], F32R) for k in range(U)]
        fs = sb("fs", [128, 2, 4 * MUL])
        w = sb("w", [128, 2, 4 * MUL])
        u = sb("u", [128, 2, 2, MUL])
        dot = sb("dot", [128, 2, 3, MUL])
        v3 = sb("v3", [128, 2, 3, MUL])
        feat = sb("feat", [128, 2, 4 * MUL])
        ps_tr = ps("ps_tr", [128, 4, 128])
        ps_a = [ps(f"ps_a{t}", [128, 3 * MUL]) for t in range(2)]
        ps_ip = ps("ps_ip", [128, 2, 128])
        ps_hid = ps("ps_hid", [128, 512])
        ps_f = ps("ps_f", [128, 4 * MUL])
        ps_s = ps("ps_s", [128, 4 * MUL])
        ps_sum = ps("ps_sum", [NG, 4 * MUL])

        rec_landed = [sem(f"rec_landed{k}") for k in range(U)]
        rows_landed = [[sem(f"rows_landed{k}_{t}") for t in range(2)] for k in range(U)]
        names = ("const_set bidx_ready sh_ready oh_ready q0_ready v3_ready z_lo tr_done recT_ready ohT_ready a_ready prod_ready "
                 "ip_ps ip_ready hid_f hid_done abs_ready exp_ready ln_ready ssp_ready z_hi f_ps fs_ready s_ps "
                 "w_ready u_ready x0s_ready dot1_ready dot2_ready w4_ready out1_done feat_ready tile_summed acc_done")
        S = {n: sem(n) for n in names.split()}
        block = ctx.enter_context(nc.Block())
        sqrt3 = sb("inv_sqrt3", [128, 3])
        one4 = sb("one4", [128, 4])

        @block.sync
        def _(sp):
            def load(s, k):
                wait(sp, S["tr_done"], s - U + 1)
                sp.dma_start(rec[k][:, :, :],
                             scratch["sorted"][bass.ds(s * STEP, STEP), :].rearrange("(t p) r -> p t r", p=128)
                             ).then_inc(rec_landed[k], 16)
            for k in range(U):
                load(k, k)
            assert STEPS % U == 1
            with sp.Fori(1, STEPS // U) as r:
                for k in range(U):
                    load(r * U + k, k)
            load(STEPS - 1, 0)

        @block.gpsimd
        def _(pool):
            pool.memset(sqrt3[:, :], 3.0 ** -0.5).then_inc(S["const_set"], 1)
            pool.memset(one4[:, :], 1.0).then_inc(S["const_set"], 1)
            pool.wait_ge(S["const_set"], 2)

            def first(s, k, rnd):
                pool.wait_ge(rec_landed[k], 16 * (rnd + 1))
                wait(pool, S["feat_ready"], 2 * (s - U + 1))
                wait(pool, S["tile_summed"], 2 * (s - U + 1))
                pool.tensor_tensor(shs[k][:, :, :], rec[k][:, :, SH:SH + 4],
                                   one4[:, :].unsqueeze(1).to_broadcast([128, 2, 4]), ALU.mult).then_inc(S["sh_ready"], 1)
                pool.tensor_copy(bidx[k][:, :], rec[k][:, :, B_ID]).then_inc(S["bidx_ready"], 1)
                pool.wait_ge(S["bidx_ready"], s + 1)
                pool.tensor_tensor(sht[k][:, :, :], rec[k][:, :, SH + 1:SH + 4],
                                   sqrt3[:, :].unsqueeze(1).to_broadcast([128, 2, 3]), ALU.mult).then_inc(S["sh_ready"], 1)
                for t in range(2):
                    pool.tensor_scalar(oh[k][:, t, :], keep["iota"][:, :], rec[k][:, t, A_LOC:A_LOC + 1], None,
                                       ALU.is_equal).then_inc(S["oh_ready"], 1)
                    pool.indirect_dma_start(
                        out=rows[k][:, t, :], out_offset=None, in_=scratch["rows"],
                        in_offset=bass.IndirectOffsetOnAxis(ap=bidx[k][:, t:t + 1], axis=0)
                    ).then_inc(rows_landed[k][t], 16)
                g = pool.value_load(keep["step_group"][0:1, bass.ds(s, 1)], min_val=0, max_val=G - 1)
                for i, tab in enumerate(("tab_hi", "tab_lo")):
                    pool.tensor_copy(q0s[k][:, i:i + 1, :], keep[tab][:, bass.ds(g, 1), 3 * MUL:4 * MUL]
                                     ).then_inc(S["q0_ready"], 1)

            def vectors(s, k, t):
                pool.wait_ge(S["w_ready"], 2 * s + t + 1)
                wait(pool, S["feat_ready"], 2 * s + t - 1)
                pool.tensor_tensor(v3[:, t, :, :], rows[k][:, t, 4 * MUL:ROW].rearrange("p (m u) -> p m u", m=3),
                                   w[:, t, MUL:2 * MUL].unsqueeze(1).to_broadcast([128, 3, MUL]),
                                   ALU.mult).then_inc(S["v3_ready"], 1)

            def low(s, k):
                pool.wait_ge(S["z_hi"], s + 1)
                pool.tensor_tensor(z[k][0:64, :, :].rearrange("p a b -> p (a b)"), ssp[0:64, :],
                                   z[k][0:64, :, :].bitcast(F32).rearrange("p a b -> p (a b)"),
                                   ALU.subtract).then_inc(S["z_lo"], 1)

            first(0, 0, 0)
            first(1, 1, 0)
            low(0, 0)
            for k in range(U):
                first(k + 2, (k + 2) % U, (k + 2) // U)
                vectors(k, k, 0)
                low(k + 1, (k + 1) % U)
                vectors(k, k, 1)
            with pool.Fori(1, STEPS // U - 1) as r:
                for k in range(U):
                    s = r * U + k
                    first(s + 2, (k + 2) % U, r + (k + 2) // U)
                    vectors(s, k, 0)
                    low(s + 1, (k + 1) % U)
                    vectors(s, k, 1)
            for s in range(STEPS - 1 - U, STEPS):
                if s + 2 < STEPS:
                    first(s + 2, (s + 2) % U, (s + 2) // U)
                vectors(s, s % U, 0)
                if s + 1 < STEPS:
                    low(s + 1, (s + 1) % U)
                vectors(s, s % U, 1)

        @block.vector
        def _(dve):
            dve.wait_ge(S["const_set"], 2)

            def products(s, k, rnd):
                for t in range(2):
                    dve.wait_ge(rows_landed[k][t], 16 * (rnd + 1))
                    dve.wait_ge(S["a_ready"], 2 * s + t + 1)
                    wait(dve, S["ip_ps"], 2 * s + t - 1)
                    dve.tensor_tensor(prod[:, t, :], ps_a[t][:, :], rows[k][:, t, 0:3 * MUL],
                                      ALU.mult).then_inc(S["prod_ready"], 1)

            def softplus(s):
                dve.wait_ge(S["ln_ready"], s + 1)
                wait(dve, S["z_lo"], s)
                dve.scalar_tensor_tensor(ssp[:, :], ps_hid[:, :], 0.0, soft[:, :], ALU.max, ALU.add
                                         ).then_inc(S["ssp_ready"], 1)

            def message(s, k, t):
                n = 2 * s + t
                x0 = rows[k][:, t, 3 * MUL:4 * MUL]
                x1 = rows[k][:, t, 4 * MUL:ROW].rearrange("p (m u) -> p m u", m=3)
                dve.wait_ge(S["fs_ready"], 2 * n + 2)
                dve.wait_ge(S["s_ps"], n + 1)
                dve.tensor_tensor(w[:, t, :], ps_s[:, :], fs[:, t, :], ALU.mult).then_inc(S["w_ready"], 1)
                dve.wait_ge(S["x0s_ready"], n + 1)
                dve.scalar_tensor_tensor(dot[:, t, 1, :], x1[:, 1, :], sht[k][:, t, 1:2], dot[:, t, 0, :],
                                         ALU.mult, ALU.add).then_inc(S["dot1_ready"], 1)
                dve.wait_ge(S["w_ready"], n + 1)
                wv = w[:, t, :].rearrange("p (a b u) -> p a b u", a=2, b=2)[:, :, 0, :]
                dve.tensor_tensor(u[:, t, :, :], wv, x0.unsqueeze(1).to_broadcast([128, 2, MUL]),
                                  ALU.mult).then_inc(S["u_ready"], 1)
                dve.wait_ge(S["dot1_ready"], n + 1)
                dve.scalar_tensor_tensor(dot[:, t, 2, :], x1[:, 2, :], sht[k][:, t, 2:3], dot[:, t, 1, :],
                                         ALU.mult, ALU.add).then_inc(S["dot2_ready"], 1)
                wait(dve, S["tile_summed"], n - 1)
                dve.wait_ge(S["v3_ready"], n + 1)
                dve.wait_ge(S["u_ready"], n + 1)
                for m in range(3):
                    dve.scalar_tensor_tensor(feat[:, t, (1 + m) * MUL:(2 + m) * MUL], u[:, t, 1, :],
                                             shs[k][:, t, 1 + m:2 + m], v3[:, t, m, :], ALU.mult, ALU.add
                                             ).then_inc(S["out1_done"], 1)
                    if m == 0:
                        dve.wait_ge(S["dot2_ready"], n + 1)
                        dve.tensor_tensor(dot[:, t, 0, :], dot[:, t, 2, :], w[:, t, 3 * MUL:4 * MUL],
                                          ALU.mult).then_inc(S["w4_ready"], 1)
                dve.wait_ge(S["w4_ready"], n + 1)
                dve.wait_ge(S["out1_done"], 3 * n + 3)
                dve.tensor_tensor(feat[:, t, 0:MUL], u[:, t, 0, :], dot[:, t, 0, :], ALU.add
                                  ).then_inc(S["feat_ready"], 1)

            def total(s):
                g = dve.value_load(keep["step_group"][0:1, bass.ds(s, 1)], min_val=0, max_val=G - 1)
                dve.wait_ge(S["tile_summed"], 2 * s + 2)
                dve.tensor_tensor(keep["acc"][:, bass.ds(g, 1), :], ps_sum[:, :].unsqueeze(1),
                                  keep["acc"][:, bass.ds(g, 1), :], ALU.add).then_inc(S["acc_done"], 1)

            def before():
                products(0, 0, 0)
                softplus(0)

            def last():
                dve.wait_ge(S["acc_done"], STEPS - 2)
                total(STEPS - 2)
                message(STEPS - 1, 0, 0)
                message(STEPS - 1, 0, 1)
                dve.wait_ge(S["acc_done"], STEPS - 1)
                total(STEPS - 1)
            def both(s, k, rnd):
                products(s + 1, (k + 1) % U, rnd)
                if not (isinstance(s, int) and s == 0):
                    wait(dve, S["acc_done"], s - 1)
                    total(s - 1)
                message(s, k, 0)
                softplus(s + 1)
                message(s, k, 1)
            before()
            for k in range(U):
                both(k, k, (k + 1) // U)
            with dve.Fori(1, STEPS // U) as r:
                for k in range(U):
                    both(r * U + k, k, r + (k + 1) // U)
            last()

        @block.scalar
        def _(act):
            def transposed(s, k):
                act.wait_ge(S["tr_done"], s + 1)
                wait(act, S["hid_done"], s - U + 1)
                act.activation(recT[k][:, :, :], ps_tr[0:RECK, 0:2, :], ACT.Copy).then_inc(S["recT_ready"], 1)
                act.activation(ohT[k][:, :, :], ps_tr[0:NG, 2:4, :], ACT.Copy).then_inc(S["ohT_ready"], 1)

            def inner(s):
                act.wait_ge(S["ip_ps"], 2 * s + 2)
                wait(act, S["hid_done"], s)
                act.activation(ipT[:, :, :], ps_ip[:, :, :], ACT.Copy, scale=1.0 / 3.0).then_inc(S["ip_ready"], 1)

            def softplus(s):
                act.wait_ge(S["hid_done"], s + 1)
                wait(act, S["ssp_ready"], s)
                act.activation(soft[:, :], ps_hid[:, :], ACT.Abs).then_inc(S["abs_ready"], 1)
                act.wait_ge(S["abs_ready"], s + 1)
                act.activation(soft[:, :], soft[:, :], ACT.Exp, scale=-1.0).then_inc(S["exp_ready"], 1)
                act.wait_ge(S["exp_ready"], s + 1)
                act.activation(soft[:, :], soft[:, :], ACT.Ln, bias=keep["half"][:, :], scale=0.5).then_inc(S["ln_ready"], 1)

            def high(s, k):
                act.wait_ge(S["ssp_ready"], s + 1)
                wait(act, S["s_ps"], 2 * (s - U + 1))
                act.activation(z[k][:, :, :], ssp[:, :].rearrange("p (a b) -> p a b", a=4), ACT.Copy).then_inc(S["z_hi"], 1)

            def filters(s, k, t, rnd):
                n = 2 * s + t
                act.wait_ge(S["sh_ready"], 2 * s + 2)
                wait(act, S["feat_ready"], n - 1)
                act.wait_ge(rows_landed[k][t], 16 * (rnd + 1))
                act.activation(dot[:, t, 0, :], rows[k][:, t, 4 * MUL:5 * MUL], ACT.Copy,
                               scale=sht[k][:, t, 0:1]).then_inc(S["x0s_ready"], 1)
                act.wait_ge(S["f_ps"], n + 1)
                act.activation(fs[:, t, 0:2 * MUL], ps_f[:, 0:2 * MUL], ACT.Copy,
                               scale=shs[k][:, t, 0:1]).then_inc(S["fs_ready"], 1)
                act.activation(fs[:, t, 2 * MUL:4 * MUL], ps_f[:, 2 * MUL:4 * MUL], ACT.Copy).then_inc(S["fs_ready"], 1)

            def both(s, k, nxt, rnd):
                transposed(s + 1, nxt)
                filters(s, k, 0, rnd)
                inner(s + 1)
                softplus(s + 1)
                filters(s, k, 1, rnd)
                high(s + 1, nxt)
            transposed(0, 0)
            inner(0)
            softplus(0)
            high(0, 0)
            for k in range(U):
                both(k, k, (k + 1) % U, 0)
            with act.Fori(1, STEPS // U) as r:
                for k in range(U):
                    both(r * U + k, k, (k + 1) % U, r)
            filters(STEPS - 1, 0, 0, STEPS // U)
            filters(STEPS - 1, 0, 1, STEPS // U)

        @block.tensor
        def _(pe):
            def transposes(s, k, rnd):
                pe.wait_ge(rec_landed[k], 16 * (rnd + 1))
                pe.wait_ge(S["oh_ready"], 2 * s + 2)
                wait(pe, S["ohT_ready"], s)
                wait(pe, S["recT_ready"], s)
                for t in range(2):
                    pe.transpose(ps_tr[0:NG, 2 + t, :], oh[k][:, t, :], keep["ident"][:, :])
                for t in range(2):
                    ins = pe.transpose(ps_tr[0:RECK, t, :], rec[k][:, t, 0:RECK], keep["ident"][:, :])
                ins.then_inc(S["tr_done"], 1)

            def gathers(s, k):
                g = pe.value_load(keep["step_group"][0:1, bass.ds(s, 1)], min_val=0, max_val=G - 1)
                pe.wait_ge(S["recT_ready"], s + 1)
                wait(pe, S["ssp_ready"], s)
                pe.matmul(ps_hid[:, 0:256], keep["wf1"][:, :, :].rearrange("p q k -> p (q k)"),
                          recT[k][:, :, :].rearrange("p a b -> p (a b)"), start=True, stop=True)
                pe.wait_ge(S["ohT_ready"], s + 1)
                for t in range(2):
                    wait(pe, S["prod_ready"], 2 * s + t - 1)
                    for i, tab in enumerate(("tab_hi", "tab_lo")):
                        ins = pe.matmul(ps_a[t][:, :].unsqueeze(1), ohT[k][:, t, :],
                                        keep[tab][:, bass.ds(g, 1), 0:3 * MUL], start=(i == 0), stop=(i == 1))
                    ins.then_inc(S["a_ready"], 1)

            def inner(s, k):
                for t in range(2):
                    pe.wait_ge(S["prod_ready"], 2 * s + t + 1)
                    if t == 0:
                        wait(pe, S["ip_ready"], s)
                    for m in range(3):
                        ins = pe.matmul(ps_ip[:, t, :], prod[:, t, m * MUL:(m + 1) * MUL], keep["ident"][:, :],
                                        start=(m == 0), stop=(m == 2))
                    ins.then_inc(S["ip_ps"], 1)

            def hidden(s, k):
                pe.wait_ge(S["q0_ready"], 2 * s + 2)
                for i in range(2):
                    pe.matmul(ps_hid[:, 256:512], q0s[k][:, i, :], ohT[k][:, :, :].rearrange("p a b -> p (a b)"),
                              start=(i == 0), stop=False)
                pe.wait_ge(S["ip_ready"], s + 1)
                pe.matmul(ps_hid[:, 256:512], keep["ws1c"][:, :, :].rearrange("p q k -> p (q k)"),
                          ipT[:, :, :].rearrange("p a b -> p (a b)"), start=False, stop=True).then_inc(S["hid_done"], 1)

            def weights(s, k, t):
                n = 2 * s + t
                pe.wait_ge(S["z_lo"], s + 1)
                wait(pe, S["fs_ready"], 2 * n)
                pe.matmul(ps_f[:, :], z[k][:, t, :], keep["wf2"][:, :], start=True, stop=True).then_inc(S["f_ps"], 1)
                wait(pe, S["w_ready"], n)
                pe.matmul(ps_s[:, :], z[k][:, 2 + t, :], keep["ws2"][:, :], start=True, stop=True).then_inc(S["s_ps"], 1)

            def sums(s, k, t):
                if t == 0:
                    wait(pe, S["acc_done"], s)
                pe.wait_ge(S["feat_ready"], 2 * s + t + 1)
                pe.matmul(ps_sum[:, :], oh[k][:, t, :], feat[:, t, :], start=(t == 0), stop=(t == 1)
                          ).then_inc(S["tile_summed"], 1)

            def both(s, k, nxt, rnd):
                transposes(s + 1, nxt, rnd)
                gathers(s + 1, nxt)
                weights(s, k, 0)
                inner(s + 1, nxt)
                hidden(s + 1, nxt)
                weights(s, k, 1)
                sums(s, k, 0)
                sums(s, k, 1)
            transposes(0, 0, 0)
            gathers(0, 0)
            inner(0, 0)
            hidden(0, 0)
            for k in range(U):
                both(k, k, (k + 1) % U, (k + 1) // U)
            with pe.Fori(1, STEPS // U) as r:
                for k in range(U):
                    both(r * U + k, k, (k + 1) % U, r + (k + 1) // U)
            weights(STEPS - 1, 0, 0)
            weights(STEPS - 1, 0, 1)
            sums(STEPS - 1, 0, 0)
            sums(STEPS - 1, 0, 1)


def ffn(nc, a, keep, scratch, out):
    with ExitStack() as ctx:
        def sb(name, shape, dt=F32):
            return ctx.enter_context(nc.sbuf_tensor(name, shape, dt))

        def sem(name):
            return ctx.enter_context(nc.semaphore(name))

        x3T = sb("x3T", [128, 4, N])
        cw = sb("cw", [NG, G, NEXP])
        cwT = sb("cwT", [NEXP, N])
        fb2 = sb("fb2", [NEXP, D])
        with ExitStack() as inner:
            route(nc, a, keep, inner, x3T, cw, cwT, fb2)
        experts(nc, a, keep, x3T, cw, cwT, fb2, out)


def route(nc, a, keep, ctx, x3T, cw, cwT, fb2):
    def sb(name, shape, dt=F32):
        return ctx.enter_context(nc.sbuf_tensor(name, shape, dt))

    def ps(name, shape, dt=F32):
        return ctx.enter_context(nc.psum_tensor(name, shape, dt))

    def sem(name):
        return ctx.enter_context(nc.semaphore(name))
    wo0 = sb("wo0", [128, MUL])
    wo1 = sb("wo1", [128, MUL])
    bo0 = sb("bo0", [1, MUL])
    ones_row = sb("ones_row2", [1, NG])
    rw = sb("rw_s", [128, 4, NEXP])
    rb = sb("rb_s", [1, NEXP])
    eps_t = sb("eps_t2", [NG, 1])
    iota8 = sb("iota8", [NG, NEXP])
    s1 = sb("s1", [NG, D])
    accT = sb("accT", [128, 4, NG])
    x3 = sb("x3", [NG, G, D])
    stats = sb("stats2", [NG, G, 6])
    mv = sb("mv2", [NG, G, 2])
    std = sb("std2", [NG, G])
    rstd = sb("rstd2", [NG, G])
    x3s = sb("x3s", [NG, D])
    x3Ts = sb("x3Ts", [128, 4, NG])
    logit = sb("logit", [NG, G, NEXP])
    top = sb("top", [NG, G, 8])
    topi = sb("topi", [NG, G, 8], mybir.dt.uint32)
    topf = sb("topf", [NG, G, 8])
    gap = sb("gap", [NG, 4, G])
    hit = sb("hit", [NG, 2, G, NEXP])
    ps_T = ps("ps_T", [128, 4, NG])
    ps_o = ps("ps_o", [NG, 4, MUL])
    ps_T3 = ps("ps_T3", [128, 4, NG])
    ps_l = ps("ps_l", [NG, NEXP])
    ps_cs = [ps(f"ps_c{h}", [NEXP, 4, NG]) for h in range(3)]
    names = ("w2_in set2 dve2_step s1_ready accT_ps accT_ready o_ps x2_ready var2 std2_done x3s_ready x3T_ps "
             "x3T_ready x3T_kept l_ps l_ready gap_ready exp_ready2 cw_ready cwT_ps")
    S = {n: sem(n) for n in names.split()}
    block = ctx.enter_context(nc.Block())

    @block.sync
    def _(sp):
        for dst, src in ((wo0[:, :], a["L0_gnn_W_o0"]), (wo1[:, :], a["L0_gnn_W_o1"]),
                         (bo0[:, :], a["L0_gnn_b_o0"].rearrange("(c p) -> c p", c=1)),
                         (rw[:, :, :], a["rw"].rearrange("(c p) e -> p c e", p=128)),
                         (rb[:, :], a["L0_ffn_router_b"].rearrange("(c p) -> c p", c=1)),
                         (fb2[:, :], a["L0_ffn_fc2_b"])):
            sp.dma_start(dst, src).then_inc(S["w2_in"], 16)

    @block.gpsimd
    def _(pool):
        pool.memset(ones_row[:, :], 1.0).then_inc(S["set2"], 1)
        pool.memset(eps_t[:, :], EPS).then_inc(S["set2"], 1)
        pool.iota(iota8[:, :], [[1, NEXP]], base=0, channel_multiplier=0,
                  allow_small_or_imprecise_dtypes=True).then_inc(S["set2"], 1)

    @block.vector
    def _(dve):
        done = [0]

        def link(ins):
            done[0] += 1
            ins.then_inc(S["dve2_step"], 1)
            dve.wait_ge(S["dve2_step"], done[0])

        def linear(t):
            x_t = keep["x"][:, bass.ds(t, 1), :]
            wait(dve, S["accT_ps"], t)
            dve.tensor_scalar(s1[:, :].unsqueeze(1), keep["acc"][:, bass.ds(t, 1), :], 1.0, None, ALU.mult
                              ).then_inc(S["s1_ready"], 1)
            dve.wait_ge(S["o_ps"], t + 1)
            dve.tensor_tensor(x_t[:, :, 0:MUL], ps_o[:, 0:1, :], x_t[:, :, 0:MUL], ALU.add).then_inc(S["x2_ready"], 1)
            x_v = x_t[:, :, MUL:D].rearrange("p g (u m) -> p (g m) u", m=3)
            dve.tensor_tensor(x_v, ps_o[:, 1:4, :], x_v, ALU.add).then_inc(S["x2_ready"], 1)
        linear(0)
        with dve.Fori(1, G) as t:
            linear(t)
        dve.wait_ge(S["x2_ready"], 2 * G)
        for t in range(G):
            ins = dve.bn_stats(stats[:, t, :], keep["x"][:, t, :])
        link(ins)
        for t in range(G):
            ins = dve.bn_aggr(mv[:, t, :], stats[:, t, :])
        ins.then_inc(S["var2"], 1)
        dve.wait_ge(S["std2_done"], 1)
        link(dve.reciprocal(rstd[:, :], std[:, :]))
        for t in range(G):
            ins = dve.tensor_scalar(x3[:, t, :], keep["x"][:, t, :], mv[:, t, 0:1], rstd[:, t:t + 1],
                                    ALU.subtract, ALU.mult)
        link(ins)

        def router(t):
            wait(dve, S["x3T_ps"], t)
            dve.tensor_scalar(x3s[:, :].unsqueeze(1), x3[:, bass.ds(t, 1), :], 1.0, None, ALU.mult
                              ).then_inc(S["x3s_ready"], 1)
            dve.wait_ge(S["x3T_ready"], t + 1)
            dve.tensor_scalar(x3T[:, :, bass.ds(t * NG, NG)], ps_T3[:, :, :], 1.0, None, ALU.mult
                              ).then_inc(S["x3T_kept"], 1)
            dve.wait_ge(S["l_ps"], t + 1)
            dve.tensor_scalar(logit[:, bass.ds(t, 1), :], ps_l[:, :].unsqueeze(1), 1.0, None, ALU.mult
                              ).then_inc(S["l_ready"], 1)
        router(0)
        with dve.Fori(1, G) as t:
            router(t)
        dve.wait_ge(S["l_ready"], G)
        for t in range(G):
            ins = dve.max(top[:, t, :], logit[:, t, :])
        link(ins)
        for t in range(G):
            ins = dve.max_index(topi[:, t, :], top[:, t, :], logit[:, t, :])
        link(ins)
        link(dve.tensor_copy(topf[:, :, :], topi[:, :, :]))
        dve.tensor_tensor(gap[:, 0, :], top[:, :, 1], top[:, :, 0], ALU.subtract).then_inc(S["gap_ready"], 1)
        dve.wait_ge(S["exp_ready2"], 1)
        link(dve.tensor_scalar(gap[:, 2, :], gap[:, 1, :], 1.0, None, ALU.add))
        link(dve.reciprocal(gap[:, 3, :], gap[:, 2, :]))
        link(dve.tensor_tensor(gap[:, 2, :], gap[:, 1, :], gap[:, 3, :], ALU.mult))
        dve.wait_ge(S["set2"], 3)
        for i, wgt in enumerate((3, 2)):
            link(dve.tensor_tensor(hit[:, i, :, :], iota8[:, :].unsqueeze(1).to_broadcast([NG, G, NEXP]),
                                   topf[:, :, i:i + 1].to_broadcast([NG, G, NEXP]), ALU.is_equal))
            link(dve.tensor_tensor(hit[:, i, :, :], hit[:, i, :, :],
                                   gap[:, wgt, :].unsqueeze(2).to_broadcast([NG, G, NEXP]), ALU.mult))
        dve.tensor_tensor(cw[:, :, :], hit[:, 0, :, :], hit[:, 1, :, :], ALU.add).then_inc(S["cw_ready"], 1)
        dve.wait_ge(S["cwT_ps"], 1)
        for h in range(3):
            n = min(4, G - 4 * h)
            dve.tensor_copy(cwT[:, 4 * h * NG:(4 * h + n) * NG].rearrange("e (g p) -> e g p", p=NG),
                            ps_cs[h][:, 0:n, :])

    @block.scalar
    def _(act):
        def linear(t):
            act.wait_ge(S["accT_ps"], t + 1)
            wait(act, S["o_ps"], t)
            act.activation(accT[:, :, :], ps_T[:, :, :], ACT.Copy).then_inc(S["accT_ready"], 1)
        linear(0)
        with act.Fori(1, G) as t:
            linear(t)
        act.wait_ge(S["set2"], 2)
        act.wait_ge(S["var2"], 1)
        act.activation(std[:, :], mv[:, :, 1], ACT.Sqrt, bias=eps_t[:, :]).then_inc(S["std2_done"], 1)

        def router(t):
            act.wait_ge(S["x3T_ps"], t + 1)
            wait(act, S["l_ps"], t)
            act.activation(x3Ts[:, :, :], ps_T3[:, :, :], ACT.Copy).then_inc(S["x3T_ready"], 1)
        router(0)
        with act.Fori(1, G) as t:
            router(t)
        act.wait_ge(S["gap_ready"], 1)
        act.activation(gap[:, 1, :], gap[:, 0, :], ACT.Exp).then_inc(S["exp_ready2"], 1)

    @block.tensor
    def _(pe):
        pe.wait_ge(S["w2_in"], 16 * 6)
        pe.wait_ge(S["set2"], 1)

        def linear(t):
            pe.wait_ge(S["s1_ready"], t + 1)
            wait(pe, S["accT_ready"], t)
            for c in range(4):
                ins = pe.transpose(ps_T[:, c, :], s1[:, c * 128:(c + 1) * 128], keep["ident"][0:NG, 0:NG])
            ins.then_inc(S["accT_ps"], 1)
            pe.wait_ge(S["accT_ready"], t + 1)
            wait(pe, S["x2_ready"], 2 * t)
            pe.matmul(ps_o[:, 0, :], accT[:, 0, :], wo0[:, :], start=True, stop=False)
            pe.matmul(ps_o[:, 0, :], ones_row[:, :], bo0[:, :], start=False, stop=True)
            for m in range(3):
                ins = pe.matmul(ps_o[:, 1 + m, :], accT[:, 1 + m, :], wo1[:, :], start=True, stop=True)
            ins.then_inc(S["o_ps"], 1)
        linear(0)
        with pe.Fori(1, G) as t:
            linear(t)

        def router(t):
            pe.wait_ge(S["x3s_ready"], t + 1)
            wait(pe, S["x3T_ready"], t)
            wait(pe, S["x3T_kept"], t)
            for c in range(4):
                ins = pe.transpose(ps_T3[:, c, :], x3s[:, c * 128:(c + 1) * 128], keep["ident"][0:NG, 0:NG])
            ins.then_inc(S["x3T_ps"], 1)
            pe.wait_ge(S["x3T_ready"], t + 1)
            wait(pe, S["l_ready"], t)
            for c in range(4):
                pe.matmul(ps_l[:, :], x3Ts[:, c, :], rw[:, c, :], start=(c == 0), stop=False)
            pe.matmul(ps_l[:, :], ones_row[:, :], rb[:, :], start=False, stop=True).then_inc(S["l_ps"], 1)
        router(0)
        with pe.Fori(1, G) as t:
            router(t)
        pe.wait_ge(S["cw_ready"], 1)
        for t in range(G):
            ins = pe.transpose(ps_cs[t // 4][:, t % 4, :], cw[:, t, :], keep["ident"][0:NG, 0:NG])
        ins.then_inc(S["cwT_ps"], 1)


def experts(nc, a, keep, x3T, cw, cwT, fb2, out):
    FC = FF // 128
    SUB = TOK // NG
    with ExitStack() as ctx:
        def sb(name, shape, dt=F32):
            return ctx.enter_context(nc.sbuf_tensor(name, shape, dt))

        def ps(name, shape, dt=F32):
            return ctx.enter_context(nc.psum_tensor(name, shape, dt))

        def sem(name):
            return ctx.enter_context(nc.semaphore(name))

        w1 = [sb(f"w1_{i}", [128, 4, 2 * FF]) for i in range(2)]
        w2 = [sb(f"w2_{i}", [128, FC, D]) for i in range(2)]
        b1 = [sb(f"b1_{i}", [128, 2 * FC]) for i in range(2)]
        gate = sb("gate", [128, 2, TOK])
        act_a = sb("act_a", [128, FC, TOK])
        cws = sb("cws", [NG, SUB, 1])
        ps_h = [ps(f"ps_h{i}", [128, 2, TOK]) for i in range(4)]
        ps_y = [ps(f"ps_y{i}", [NG, D]) for i in range(SUB)]
        names = ("bias_ps bias_done gate_ready h_ps a_ready y_ps y_done stored")
        S = {n: sem(n) for n in names.split()}
        w1_in = [sem(f"w1_in{i}") for i in range(2)]
        w2_in = [sem(f"w2_in{i}") for i in range(2)]
        block = ctx.enter_context(nc.Block())

        @block.sync
        def _(sp):
            def load(e, i):
                wait(sp, S["y_done"], (e - 1) * CHUNKS * SUB)
                sp.dma_start(w1[i][:, :, :], a["w1t"][bass.ds(e, 1)].rearrange("e (c p) f -> p (e c) f", p=128)).then_inc(w1_in[i], 16)
                sp.dma_start(b1[i][:, :], a["b1"][bass.ds(e, 1)].rearrange("e p f -> p (e f)")).then_inc(w1_in[i], 16)
                sp.dma_start(w2[i][:, :, :], a["w2t"][bass.ds(e, 1)].rearrange("e (c p) d -> p (e c) d", p=128)).then_inc(w2_in[i], 16)
            load(0, 0)
            load(1, 1)
            with sp.Fori(1, NEXP // 2) as r:
                load(r * 2, 0)
                load(r * 2 + 1, 1)
            sp.wait_ge(S["y_done"], NEXP * CHUNKS * SUB)
            sp.dma_start(out.rearrange("(g p) d -> p g d", p=NG), keep["x"][:, :, :]).then_inc(S["stored"], 16)
            sp.wait_ge(S["stored"], 16)

        def loop(eng, body):
            body(0, 0, 0, 0, 0)
            with eng.Fori(1, CHUNKS) as c:
                body(0, 0, 0, c, c)
            with eng.Fori(0, CHUNKS) as c:
                body(1, 1, 0, c, c + CHUNKS)
            with eng.Fori(1, NEXP // 2) as r:
                for i in range(2):
                    with eng.Fori(0, CHUNKS) as c:
                        body(r * 2 + i, i, r, c, (r * 2 + i) * CHUNKS + c)

        @block.scalar
        def _(act):
            def body(e, i, r, c, g):
                for f in range(FC):
                    act.wait_ge(S["h_ps"], g * FC + f + 1)
                    wait(act, S["a_ready"], g * FC + f - 1)
                    if f == 0:
                        act.wait_ge(w1_in[i], 32 * r + 32)
                    act.activation(gate[:, f % 2, :], ps_h[f % 4][:, 0, :], ACT.Silu, bias=b1[i][:, f:f + 1]
                                   ).then_inc(S["gate_ready"], 1)
            loop(act, body)

        @block.vector
        def _(dve):
            for t in range(G):
                dve.wait_ge(S["bias_ps"], t + 1)
                dve.tensor_tensor(keep["x"][:, t, :], ps_y[t % SUB][:, :], keep["x"][:, t, :], ALU.add
                                  ).then_inc(S["bias_done"], 1)

            def body(e, i, r, c, g):
                for f in range(FC):
                    dve.wait_ge(S["gate_ready"], g * FC + f + 1)
                    wait(dve, S["y_ps"], g * SUB)
                    dve.scalar_tensor_tensor(act_a[:, f, :], ps_h[f % 4][:, 1, :], b1[i][:, FC + f:FC + f + 1],
                                             gate[:, f % 2, :], ALU.add, ALU.mult).then_inc(S["a_ready"], 1)
                for t in range(SUB):
                    dve.wait_ge(S["y_ps"], g * SUB + t + 1)
                    if t == 0:
                        wait(dve, S["y_done"], g * SUB)
                        dve.wait_ge(S["bias_done"], G)
                    x_t = keep["x"][:, bass.ds(c * SUB + t, 1), :].rearrange("p a d -> p (a d)")
                    dve.scalar_tensor_tensor(x_t, ps_y[t][:, :], cw[:, bass.ds(c * SUB + t, 1), bass.ds(e, 1)].rearrange("p a b -> p (a b)"),
                                             x_t, ALU.mult, ALU.add).then_inc(S["y_done"], 1)
            loop(dve, body)

        @block.tensor
        def _(pe):
            for t in range(G):
                wait(pe, S["bias_done"], t - 1)
                pe.matmul(ps_y[t % SUB][:, :], cwT[:, t * NG:(t + 1) * NG], fb2[:, :], start=True, stop=True
                          ).then_inc(S["bias_ps"], 1)
            pe.wait_ge(S["bias_done"], G)

            def body(e, i, r, c, g):
                pe.wait_ge(w1_in[i], 32 * r + 32)
                for f in range(FC):
                    wait(pe, S["a_ready"], g * FC + f - 3)
                    for h in range(2):
                        for k in range(4):
                            col = h * FF + f * 128
                            ins = pe.matmul(ps_h[f % 4][:, h, :].unsqueeze(1), w1[i][:, k, col:col + 128],
                                            x3T[:, k:k + 1, bass.ds(c * TOK, TOK)], start=(k == 0), stop=(k == 3))
                    ins.then_inc(S["h_ps"], 1)
                pe.wait_ge(w2_in[i], 16 * r + 16)
                pe.wait_ge(S["a_ready"], g * FC + FC)
                for t in range(SUB):
                    wait(pe, S["y_done"], g * SUB + t - 1)
                    for f in range(FC):
                        ins = pe.matmul(ps_y[t][:, :], act_a[:, f, t * NG:(t + 1) * NG], w2[i][:, f, :],
                                        start=(f == 0), stop=(f == FC - 1))
                    ins.then_inc(S["y_ps"], 1)
            loop(pe, body)

_INS = ["x", "src", "dst", "rec", "L0_gnn_W_pre0", "L0_gnn_b_pre0", "L0_gnn_W_pre1", "L0_gnn_W_nd0", "L0_gnn_b_nd0",
        "L0_gnn_W_nd1", "L0_gnn_W_g1", "bg1", "L0_gnn_W_g2", "bg2", "L0_gnn_W_f1", "wf2",
        "L0_gnn_W_s1", "ws2", "L0_gnn_W_o0", "L0_gnn_b_o0", "L0_gnn_W_o1", "rw", "L0_ffn_router_b", "w1t", "b1",
        "w2t", "L0_ffn_fc2_b"]


def program(nc, a, out):
    with ExitStack() as ctx:
        keep = {}

        def sb(name, shape, dt=F32):
            keep[name] = ctx.enter_context(nc.sbuf_tensor(name, shape, dt))
        scratch = {"sorted": nc.dram_tensor("sorted_recs", (STEPS * STEP, REC), F32, kind="Internal").ap(),
                   "rows": nc.dram_tensor("node_rows", (N, ROW), F32, kind="Internal").ap()}
        sb("x", [NG, G, D])
        sb("acc", [NG, G, D])
        sb("ident", [128, 128])
        sb("half", [128, 1])
        with ExitStack() as gnn:
            ctx_, ctx = ctx, gnn
            sb("iota", [128, NG])
            sb("step_group", [1, STEPS], I32)
            sb("tab_hi", [NG, G, 4 * MUL], F32R)
            sb("tab_lo", [NG, G, 4 * MUL], F32R)
            sb("wf1", [RECK, 4, HID])
            sb("ws1c", [128, 4, HID])
            for n in ("wf2", "ws2"):
                sb(n, [128, 4 * MUL], F32R)
                sb(n + "_raw", [128, 4 * MUL])
            prepare(nc, a, keep, scratch)
            edges(nc, keep, scratch)
            ctx = ctx_
        ffn(nc, a, keep, scratch, out)


def kernel(**inputs):
    import concourse.bacc as _bacc
    from concourse.bass_utils import run_bass_kernel_spmd as _run

    i = {k: np.ascontiguousarray(v) for k, v in inputs.items()}
    rec = np.zeros((E, REC), np.float32)
    rec[:, SH:SH + 4] = i["edge_attr_4"]
    rec[:, ATTR:RECK] = i["edge_attr_32"]
    i["rec"] = rec

    def by_path(w):
        return np.ascontiguousarray(w.reshape(HID, 4, MUL)[:, [0, 2, 1, 3], :].reshape(HID, 4 * MUL))
    i["wf2"], i["ws2"] = by_path(i["L0_gnn_W_f2"]), by_path(i["L0_gnn_W_s2"])
    for n in ("1", "2"):
        i["bg" + n] = np.ascontiguousarray(i["L0_gnn_b_g" + n].reshape(2, 128).T)
    i["rw"] = np.ascontiguousarray(i["L0_ffn_router_w"].T)
    i["w1t"] = np.ascontiguousarray(i["L0_ffn_fc1_w"].transpose(0, 2, 1))
    i["b1"] = np.ascontiguousarray(i["L0_ffn_fc1_b"].reshape(NEXP, 2 * FF // 128, 128).transpose(0, 2, 1))
    i["w2t"] = np.ascontiguousarray(i["L0_ffn_fc2_w"].transpose(0, 2, 1))
    nc = _bacc.Bacc("TRN2", target_bir_lowering=False, num_devices=1)
    arrays = {"in_" + n: i[n] for n in _INS}
    a = {n: nc.dram_tensor("in_" + n, i[n].shape, mybir.dt.from_np(i[n].dtype), kind="ExternalInput").ap() for n in _INS}
    out = nc.dram_tensor("out_x", (N, D), F32, kind="ExternalOutput").ap()
    program(nc, a, out)
    return _run(nc, [arrays], core_ids=[0]).results[0]["out_x"]
```

```python
from contextlib import ExitStack

import numpy as np
import concourse.bass as bass
from concourse import mybir

F32 = mybir.dt.float32
F32R = mybir.dt.float32r
I32 = mybir.dt.int32
ALU = mybir.AluOpType
ACT = mybir.ActivationFunctionType

N, D, E = 1250, 512, 40000
MUL = 128
G = 10
NG = N // G
EP = 125
EC = E // EP
STEP = 256
STEPS = (E - G) // STEP + G
REC = 38
A_LOC, B_ID, SH, ATTR = 0, 1, 2, 6
RECK = ATTR + 32
HID = 32
ROW = 3 * MUL + 4 * MUL
CH = 8
FILLS = 4
NEXP = 8
FF = 1024
EPS = 1e-5
TILE = 256
TILE_BITS = 8
TILES = (2 * N - NEXP) // TILE + NEXP


def wait(eng, sem, value):
    if isinstance(value, int) and value <= 0:
        return
    eng.wait_ge(sem, value)


def prepare(nc, a, keep, scratch):
    with ExitStack() as ctx:
        def sb(name, shape, dt=F32):
            return ctx.enter_context(nc.sbuf_tensor(name, shape, dt))

        def ps(name, shape, dt=F32):
            return ctx.enter_context(nc.psum_tensor(name, shape, dt))

        def sem(name):
            return ctx.enter_context(nc.semaphore(name))

        rec_all = sb("rec_all", [EP, EC, REC])
        stage = [sb(f"stage{i}", [EP, CH, REC]) for i in range(2)]
        stage_pos = [sb(f"stage_pos{i}", [EP, CH], I32) for i in range(2)]
        a_int = sb("a_int", [EP, EC], I32)
        b_int = sb("b_int", [EP, EC], I32)
        a_f = sb("a_f", [EP, EC])
        grp = sb("grp", [EP, EC])
        mask = sb("mask", [EP, EC])
        zeros_e = sb("zeros_e", [EP, EC])
        rank = sb("rank", [EP, G, EC])
        picked = sb("picked", [EP, EC])
        pos = a_f
        pos_i = sb("pos_i", [EP, EC], I32)
        small = sb("small", [EP, 5, G])
        cnt_i = sb("cnt_i", [EP, 2, G], I32)
        step_no = sb("step_no", [1, STEPS])
        step_f = sb("step_f", [1, STEPS])
        zero_fill = sb("zero_fill", [128, STEPS * STEP * REC // (FILLS * 128)])
        tri = sb("tri", [EP, EP])
        onesq = sb("onesq", [EP, EP])
        stats = sb("stats", [NG, G, 6])
        mv = sb("mv", [NG, G, 2])
        std = sb("std", [NG, G])
        rstd = sb("rstd", [NG, G])
        eps_t = sb("eps_t", [NG, 1])
        wpre0 = sb("wpre0", [128, MUL])
        wpre1 = sb("wpre1", [128, MUL])
        wnd0 = sb("wnd0", [128, MUL])
        wnd1 = sb("wnd1", [128, MUL])
        wg1 = sb("wg1", [128, 2, 2 * MUL])
        wg2 = sb("wg2", [128, 2, 2 * MUL])
        bpre0 = sb("bpre0", [128, 1])
        bg1 = sb("bg1", [128, 2])
        bg2 = sb("bg2", [128, 2])
        bnd0 = sb("bnd0", [1, MUL])
        ones_row = sb("ones_row", [1, NG])
        ws1ab = sb("ws1ab", [128, 2, 4, HID])
        w2_raw = sb("w2_raw", [128, 4 * MUL])
        xs = sb("xs", [NG, 4, MUL])
        xT = sb("xT", [128, 4, NG])
        sq = sb("sq", [128, 3, NG])
        n1s = sb("n1s", [128, 2, NG])
        n1T = sb("n1T", [128, NG])
        p0T = sb("p0T", [128, NG])
        hT = sb("hT", [128, 2, NG])
        gT = sb("gT", [128, 2, NG])
        xgT = sb("xgT", [128, 3, NG])
        brow = sb("brow", [NG, ROW])
        ps_prefix = ps("ps_prefix", [EP, 2, G])
        ps_xT = ps("ps_xT", [128, 4, NG])
        ps_p0 = ps("ps_p0", [128, NG])
        ps_pre = ps("ps_pre", [NG, 4, MUL])
        ps_g1 = ps("ps_g1", [128, 2, NG])
        ps_g2 = ps("ps_g2", [128, 2, NG])
        ps_nd = ps("ps_nd", [NG, 4, MUL])

        rec_in = sem("rec_in")
        ab_in = sem("ab_in")
        x_in = sem("x_in")
        w_in = sem("w_in")
        w4_in = sem("w4_in")
        zeros_set = sem("zeros_set")
        filled = sem("filled")
        spare_filled = sem("spare_filled")
        consts = sem("consts")
        wide_consts = sem("wide_consts")
        dve_step = sem("dve_step")
        rec_done = sem("rec_done")
        totals = sem("totals")
        prefixed = sem("prefixed")
        pos_done = sem("pos_done")
        stage_seen = sem("stage_seen")
        staged = [sem(f"staged{i}") for i in range(2)]
        scattered = [sem(f"scattered{i}") for i in range(2)]
        var_done = sem("var_done")
        std_done = sem("std_done")
        split_hi = sem("split_hi")
        xs_ready = sem("xs_ready")
        xT_ps = sem("xT_ps")
        xT_ready = sem("xT_ready")
        sq_ready = sem("sq_ready")
        sq_sum = sem("sq_sum")
        n1_sum = sem("n1_sum")
        n1_ready = sem("n1_ready")
        p0_ps = sem("p0_ps")
        p0_ready = sem("p0_ready")
        pre_ps = sem("pre_ps")
        tab_hi = sem("tab_hi")
        tab_done = sem("tab_done")
        g1_ps = sem("g1_ps")
        h_ready = sem("h_ready")
        g2_ps = sem("g2_ps")
        g_ready = sem("g_ready")
        xg_ready = sem("xg_ready")
        nd_ps = sem("nd_ps")
        acc_ready = sem("acc_ready")
        row_pre = sem("row_pre")
        row_ready = sem("row_ready")
        row_out = sem("row_out")
        block = ctx.enter_context(nc.Block())

        WDMA = 16 * 19

        @block.sync
        def _(sp):
            sp.dma_start(a_int[:, :], a["src"].rearrange("(p c) -> p c", p=EP)).then_inc(ab_in, 16)
            sp.dma_start(b_int[:, :], a["dst"].rearrange("(p c) -> p c", p=EP)).then_inc(ab_in, 16)
            sp.dma_start(rec_all[:, :, :], a["rec"].rearrange("(p c) r -> p c r", p=EP)).then_inc(rec_in, 16)
            sp.dma_start(keep["x"][:, :, :], a["x"].rearrange("(g p) d -> p g d", p=NG)).then_inc(x_in, 16)
            sp.wait_ge(zeros_set, 1)
            fill = scratch["sorted"].rearrange("(k p f) r -> k p (f r)", k=FILLS, p=128)
            for i in range(FILLS):
                sp.dma_start(fill[i], zero_fill[:, :]).then_inc(filled, 16)
            spare = scratch["x_slots"].rearrange("(k p f) d -> k p (f d)", p=128, k=TILES)
            for i in range(TILES):
                sp.dma_start(spare[i], zero_fill[:, 0:TILE * D // 128]).then_inc(spare_filled, 16)
            sp.wait_ge(rec_done, 2)
            sp.wait_ge(pos_done, 1)

            def stage_pair(r):
                for i in range(2):
                    wait(sp, scattered[i], r * 16 * CH)
                    col = (2 * r + i) * CH
                    sp.dma_start(stage[i][:, :, :], rec_all[:, bass.ds(col, CH), :]).then_inc(staged[i], 16)
                    sp.dma_start(stage_pos[i][:, :], pos_i[:, bass.ds(col, CH)]).then_inc(staged[i], 16)
            stage_pair(0)
            with sp.Fori(1, EC // (2 * CH)) as r:
                stage_pair(r)
            sp.wait_ge(spare_filled, 16 * TILES)

        @block.gpsimd
        def _(pool):
            pool.memset(zero_fill[:, :], 0.0).then_inc(zeros_set, 1)
            pool.memset(keep["half"][:, :], 0.5).then_inc(zeros_set, 1)
            pool.memset(keep["ident"][:, :], 0.0).then_inc(wide_consts, 1)
            pool.memset(onesq[:, :], 1.0).then_inc(wide_consts, 1)
            pool.memset(zeros_e[:, :], 0.0).then_inc(wide_consts, 1)
            pool.memset(ones_row[:, :], 1.0).then_inc(wide_consts, 1)
            pool.memset(eps_t[:, :], EPS).then_inc(wide_consts, 1)
            pool.memset(keep["wf1"][:, :, :], 0.0).then_inc(wide_consts, 1)
            pool.memset(keep["ws1c"][:, :, :], 0.0).then_inc(wide_consts, 1)
            pool.memset(ws1ab[:, :, :, :], 0.0).then_inc(wide_consts, 1)
            pool.iota(keep["iota"][:, :], [[1, NG]], base=0, channel_multiplier=0,
                      allow_small_or_imprecise_dtypes=True).then_inc(wide_consts, 1)
            pool.iota(step_no[:, :], [[STEP, STEPS]], base=0, channel_multiplier=0,
                      allow_small_or_imprecise_dtypes=True).then_inc(wide_consts, 1)
            pool.wait_ge(wide_consts, 10)
            pool.affine_select(out=keep["ident"][:, :], in_=keep["ident"][:, :], compare_op=ALU.not_equal,
                               fill=1.0, base=0, pattern=[[-1, 128]], channel_multiplier=1).then_inc(consts, 1)
            pool.affine_select(out=tri[:, :], in_=onesq[:, :], compare_op=ALU.is_ge,
                               fill=0.0, base=-1, pattern=[[1, EP]], channel_multiplier=-1).then_inc(consts, 1)
            pool.wait_ge(filled, 16 * FILLS)

            def scatter_pair(r):
                for i in range(2):
                    pool.wait_ge(staged[i], 32 * (r + 1))
                    pool.sem_inc(stage_seen, 1)
                    for c in range(CH):
                        pool.indirect_dma_start(
                            out=scratch["sorted"], out_offset=bass.IndirectOffsetOnAxis(ap=stage_pos[i][:, c:c + 1], axis=0),
                            in_=stage[i][:, c, :], in_offset=None).then_inc(scattered[i], 16)
            with pool.Fori(0, EC // (2 * CH)) as r:
                scatter_pair(r)
            for i in range(2):
                pool.wait_ge(scattered[i], 8 * EC)

        @block.vector
        def _(dve):
            done = [0]

            def link(ins):
                done[0] += 1
                ins.then_inc(dve_step, 1)
                dve.wait_ge(dve_step, done[0])

            dve.wait_ge(ab_in, 32)
            link(dve.tensor_copy(a_f[:, :], a_int[:, :]))
            link(dve.tensor_scalar(grp[:, :], a_f[:, :], float(NG), None, ALU.is_ge))
            for g in range(2, G):
                link(dve.scalar_tensor_tensor(grp[:, :], a_f[:, :], float(NG * g), grp[:, :], ALU.is_ge, ALU.add))
            dve.wait_ge(rec_in, 16)
            dve.scalar_tensor_tensor(rec_all[:, :, A_LOC], grp[:, :], float(-NG), a_f[:, :],
                                     ALU.mult, ALU.add).then_inc(rec_done, 1)
            dve.tensor_copy(rec_all[:, :, B_ID], b_int[:, :]).then_inc(rec_done, 1)
            dve.wait_ge(wide_consts, 10)
            dve.wait_ge(rec_done, 2)
            for g in range(G):
                link(dve.tensor_scalar(mask[:, :], grp[:, :], float(g), None, ALU.is_equal))
                link(dve.tensor_tensor_scan(rank[:, g, :], mask[:, :], zeros_e[:, :], 0.0, ALU.add, ALU.add))
            dve.tensor_copy(small[:, 0, :], rank[:, :, EC - 1]).then_inc(totals, 1)
            dve.wait_ge(prefixed, 1)
            link(dve.tensor_scalar(cnt_i[:, 0, :], ps_prefix[:, 1, :], float(STEP - 1), None, ALU.add))
            link(dve.tensor_scalar(cnt_i[:, 1, :], cnt_i[:, 0, :], 8, 8, ALU.logical_shift_right, ALU.logical_shift_left))
            link(dve.tensor_copy(small[:, 1, :], cnt_i[:, 1, :]))
            link(dve.tensor_tensor_scan(small[:, 2, :], small[:, 1, :], zeros_e[:, 0:G], 0.0, ALU.add, ALU.add))
            link(dve.tensor_tensor(small[:, 3, :], small[:, 2, :], small[:, 1, :], ALU.subtract))
            link(dve.scalar_tensor_tensor(small[:, 4, :], small[:, 3, :], -1.0, ps_prefix[:, 0, :], ALU.add, ALU.add))
            for g in range(G):
                dve.scalar_tensor_tensor(rank[:, g, :], rank[:, g, :], small[:, 4, g:g + 1],
                                         zeros_e[:, :], ALU.add, ALU.add).then_inc(dve_step, 1)
                done[0] += 1
                link(dve.tensor_scalar(mask[:, :], grp[:, :], float(g), None, ALU.is_equal))
                if g == 0:
                    link(dve.tensor_tensor(pos[:, :], mask[:, :], rank[:, g, :], ALU.mult))
                else:
                    link(dve.tensor_tensor(picked[:, :], mask[:, :], rank[:, g, :], ALU.mult))
                    link(dve.tensor_tensor(pos[:, :], pos[:, :], picked[:, :], ALU.add))
            dve.tensor_copy(pos_i[:, :], pos[:, :]).then_inc(pos_done, 1)
            link(dve.tensor_scalar(step_f[:, :], step_no[:, :], small[0:1, 3, 1:2], None, ALU.is_ge))
            for g in range(2, G):
                link(dve.scalar_tensor_tensor(step_f[:, :], step_no[:, :], small[0:1, 3, g:g + 1], step_f[:, :],
                                              ALU.is_ge, ALU.add))
            link(dve.tensor_copy(keep["step_group"][:, :], step_f[:, :]))
            dve.wait_ge(w4_in, 16 * 4)
            dve.tensor_copy(keep["w2"][:, 0, :], w2_raw[:, :]).then_inc(split_hi, 1)
            dve.wait_ge(split_hi, 1)
            link(dve.tensor_tensor(keep["w2"][:, 1, :], w2_raw[:, :], keep["w2"][:, 0, :].bitcast(F32), ALU.subtract))
            dve.wait_ge(x_in, 16)
            for t in range(G):
                ins = dve.bn_stats(stats[:, t, :], keep["x"][:, t, :])
            link(ins)
            for t in range(G):
                ins = dve.bn_aggr(mv[:, t, :], stats[:, t, :])
            ins.then_inc(var_done, 1)
            dve.wait_ge(std_done, 1)
            link(dve.reciprocal(rstd[:, :], std[:, :]))
            for t in range(G):
                ins = dve.tensor_scalar(keep["acc"][:, t, :], keep["x"][:, t, :], mv[:, t, 0:1], rstd[:, t:t + 1],
                                        ALU.subtract, ALU.mult)
            link(ins)
            link(dve.tensor_tensor(keep["x"][:, :, :], keep["x"][:, :, :], keep["acc"][:, :, :], ALU.add))

            def tile(t):
                xn_t = keep["acc"][:, bass.ds(t, 1), :]
                wait(dve, xT_ps, t)
                dve.tensor_scalar(xs[:, 0:1, :], xn_t[:, :, 0:MUL], 1.0, None, ALU.mult).then_inc(xs_ready, 1)
                dve.tensor_scalar(xs[:, 1:4, :], xn_t[:, :, MUL:D].rearrange("p g (u m) -> p (g m) u", m=3),
                                  1.0, None, ALU.mult).then_inc(xs_ready, 1)
                dve.wait_ge(sq_ready, t + 1)
                dve.tensor_tensor(n1s[:, 0, :], sq[:, 0, :], sq[:, 1, :], ALU.add).then_inc(sq_sum, 1)
                dve.wait_ge(sq_sum, t + 1)
                dve.tensor_tensor(n1s[:, 1, :], n1s[:, 0, :], sq[:, 2, :], ALU.add).then_inc(n1_sum, 1)
                dve.wait_ge(pre_ps, t + 1)
                pre = ps_pre[:, :, :].rearrange("p a b -> p (a b)").unsqueeze(1)
                tab_t = keep["tab"][:, bass.ds(t, 1), :, :]
                dve.tensor_scalar(tab_t[:, :, 0, :], pre, 1.0, None, ALU.mult).then_inc(tab_hi, 1)
                dve.wait_ge(tab_hi, t + 1)
                dve.tensor_tensor(tab_t[:, :, 1, :], pre, tab_t[:, :, 0, :].bitcast(F32), ALU.subtract).then_inc(tab_done, 1)
                dve.wait_ge(g_ready, 2 * t + 2)
                dve.tensor_tensor(xgT[:, :, :], xT[:, 1:4, :], gT[:, 1:2, :].to_broadcast([128, 3, NG]),
                                  ALU.mult).then_inc(xg_ready, 1)
                dve.wait_ge(nd_ps, t + 1)
                dve.tensor_scalar(keep["acc"][:, bass.ds(t, 1), :], ps_nd[:, :, :].rearrange("p a b -> p (a b)").unsqueeze(1),
                                  1.0, None, ALU.mult).then_inc(acc_ready, 1)
            tile(0)
            with dve.Fori(1, G) as t:
                tile(t)

        @block.scalar
        def _(act):
            for dst, src in ((wpre0[:, :], a["L0_gnn_W_pre0"]), (wpre1[:, :], a["L0_gnn_W_pre1"]),
                             (wnd0[:, :], a["L0_gnn_W_nd0"]), (wnd1[:, :], a["L0_gnn_W_nd1"]),
                             (wg1[:, :, :], a["L0_gnn_W_g1"].rearrange("(c p) j -> p c j", p=128)),
                             (wg2[:, :, :], a["L0_gnn_W_g2"].rearrange("(c p) j -> p c j", p=128)),
                             (bpre0[:, :], a["L0_gnn_b_pre0"].rearrange("(p c) -> p c", c=1)),
                             (bg1[:, :], a["bg1"]),
                             (bg2[:, :], a["bg2"]),
                             (bnd0[:, :], a["L0_gnn_b_nd0"].rearrange("(c p) -> c p", c=1))):
                act.dma_start(dst, src).then_inc(w_in, 16)
            w_s1 = a["L0_gnn_W_s1"].rearrange("(c p) k -> c p k", p=MUL)
            act.wait_ge(wide_consts, 10)
            for q in range(2):
                for c in range(2):
                    act.dma_start(ws1ab[:, c, 2 + q, :], w_s1[c]).then_inc(w_in, 16)
                act.dma_start(keep["ws1c"][:, 2 + q, :], w_s1[2]).then_inc(w_in, 16)
                act.dma_start(keep["wf1"][ATTR:RECK, q, :], a["L0_gnn_W_f1"]).then_inc(w_in, 16)
                act.dma_start(w2_raw[32 * q:32 * q + 32, :], a["wf2"]).then_inc(w4_in, 16)
                act.dma_start(w2_raw[64 + 32 * q:96 + 32 * q, :], a["ws2"]).then_inc(w4_in, 16)
            act.wait_ge(var_done, 1)
            act.activation(std[:, :], mv[:, :, 1], ACT.Sqrt, bias=eps_t[:, :]).then_inc(std_done, 1)
            act.wait_ge(w_in, 16 * 18)

            def tile(t):
                act.wait_ge(xT_ps, t + 1)
                wait(act, nd_ps, t)
                act.activation(xT[:, :, :], ps_xT[:, :, :], ACT.Copy).then_inc(xT_ready, 1)
                act.activation(sq[:, :, :], ps_xT[:, 1:4, :], ACT.Square).then_inc(sq_ready, 1)
                act.wait_ge(n1_sum, t + 1)
                act.activation(n1T[:, :], n1s[:, 1, :], ACT.Sqrt, scale=1.0 / 3.0).then_inc(n1_ready, 1)
                act.wait_ge(p0_ps, t + 1)
                act.activation(p0T[:, :], ps_p0[:, :], ACT.Identity, bias=bpre0[:, :]).then_inc(p0_ready, 1)
                act.wait_ge(g1_ps, t + 1)
                for c in range(2):
                    act.activation(hT[:, c, :], ps_g1[:, c, :], ACT.Silu, bias=bg1[:, c:c + 1]).then_inc(h_ready, 1)
                act.wait_ge(tab_done, t + 1)
                wait(act, row_out, 16 * t)
                act.activation(brow[:, 0:3 * MUL], ps_pre[:, 0:3, :].rearrange("p a b -> p (a b)"), ACT.Copy).then_inc(row_pre, 1)
                act.wait_ge(g2_ps, t + 1)
                for c in range(2):
                    act.activation(gT[:, c, :], ps_g2[:, c, :], ACT.Identity, bias=bg2[:, c:c + 1]).then_inc(g_ready, 1)
                act.wait_ge(acc_ready, t + 1)
                act.activation(brow[:, 3 * MUL:ROW], ps_nd[:, :, :].rearrange("p a b -> p (a b)"), ACT.Copy).then_inc(row_ready, 1)
                act.wait_ge(row_ready, t + 1)
                act.wait_ge(row_pre, t + 1)
                act.dma_start(scratch["rows"][bass.ds(t * NG, NG), :], brow[:, :]).then_inc(row_out, 16)
            tile(0)
            with act.Fori(1, G) as t:
                tile(t)
            act.wait_ge(row_out, 16 * G)

        @block.tensor
        def _(pe):
            pe.wait_ge(consts, 2)
            pe.wait_ge(totals, 1)
            pe.matmul(ps_prefix[:, 0, :], tri[:, :], small[:, 0, :], start=True, stop=True)
            pe.matmul(ps_prefix[:, 1, :], onesq[:, :], small[:, 0, :], start=True, stop=True).then_inc(prefixed, 1)
            pe.wait_ge(w_in, 16 * 18)

            def tile(t):
                pe.wait_ge(xs_ready, 2 * t + 2)
                wait(pe, xT_ready, t)
                wait(pe, sq_ready, t)
                for c in range(4):
                    ins = pe.transpose(ps_xT[:, c, :], xs[:, c, :], keep["ident"][0:NG, 0:NG])
                ins.then_inc(xT_ps, 1)
                pe.wait_ge(xT_ready, t + 1)
                wait(pe, p0_ready, t)
                pe.matmul(ps_p0[:, :], wpre0[:, :], xT[:, 0, :], start=True, stop=True).then_inc(p0_ps, 1)
                wait(pe, tab_done, t)
                wait(pe, row_pre, t)
                for m in range(3):
                    pe.matmul(ps_pre[:, m, :], xT[:, 1 + m, :], wpre1[:, :], start=True, stop=True)
                pe.wait_ge(p0_ready, t + 1)
                for c in range(2):
                    ins = pe.matmul(ps_pre[:, 3, :], p0T[:, :], ws1ab[:, c, :, :].rearrange("p q k -> p (q k)"),
                                    start=(c == 0), stop=(c == 1))
                ins.then_inc(pre_ps, 1)
                pe.wait_ge(n1_ready, t + 1)
                for c in range(2):
                    pe.matmul(ps_g1[:, c, :], wg1[:, 0, c * 128:(c + 1) * 128], xT[:, 0, :], start=True, stop=False)
                    ins = pe.matmul(ps_g1[:, c, :], wg1[:, 1, c * 128:(c + 1) * 128], n1T[:, :], start=False, stop=True)
                ins.then_inc(g1_ps, 1)
                pe.wait_ge(h_ready, 2 * t + 2)
                for c in range(2):
                    for k in range(2):
                        ins = pe.matmul(ps_g2[:, c, :], wg2[:, k, c * 128:(c + 1) * 128], hT[:, k, :],
                                        start=(k == 0), stop=(k == 1))
                ins.then_inc(g2_ps, 1)
                pe.wait_ge(g_ready, 2 * t + 2)
                wait(pe, acc_ready, t)
                wait(pe, row_ready, t)
                pe.matmul(ps_nd[:, 0, :], gT[:, 0, :], wnd0[:, :], start=True, stop=False)
                pe.matmul(ps_nd[:, 0, :], ones_row[:, :], bnd0[:, :], start=False, stop=True)
                pe.wait_ge(xg_ready, t + 1)
                for m in range(3):
                    ins = pe.matmul(ps_nd[:, 1 + m, :], xgT[:, m, :], wnd1[:, :], start=True, stop=True)
                ins.then_inc(nd_ps, 1)
            tile(0)
            with pe.Fori(1, G) as t:
                tile(t)


def edges(nc, keep, scratch):
    U = 5
    ROUNDS = (STEPS - 4) // U
    with ExitStack() as ctx:
        def sb(name, shape, dt=F32):
            return ctx.enter_context(nc.sbuf_tensor(name, shape, dt))

        def ps(name, shape, dt=F32):
            return ctx.enter_context(nc.psum_tensor(name, shape, dt))

        def sem(name):
            return ctx.enter_context(nc.semaphore(name))

        rec = [sb(f"rec{k}", [128, 2, REC]) for k in range(U)]
        rows = [sb(f"rows{k}", [128, 2, ROW]) for k in range(U)]
        bidx = [sb(f"bidx{k}", [128, 2], I32) for k in range(U)]
        shs = [sb(f"shs{k}", [128, 2, 4]) for k in range(U)]
        sht = [sb(f"sht{k}", [128, 2, 3]) for k in range(U)]
        oh = [sb(f"oh{k}", [128, 2, NG]) for k in range(U)]
        q0s = [sb(f"q0s{k}", [NG, 2, MUL], F32R) for k in range(U)]
        recT = [sb(f"recT{k}", [RECK, 2, 128]) for k in range(U)]
        ohT = [sb(f"ohT{k}", [NG, 2, 128], F32R) for k in range(U)]
        z = [sb(f"z{k}", [128, 2, 128], F32R) for k in range(U)]
        prod = sb("prod", [128, 2, 3 * MUL])
        ipT = sb("ipT", [128, 3, 2, 128])
        soft = sb("soft", [128, 256])
        ssp = sb("ssp", [128, 256])
        zc = sb("zc", [128, 256], F32R)
        fs = sb("fs", [128, 2, 4 * MUL])
        w = sb("w", [128, 2, 4 * MUL])
        u = sb("u", [128, 2, 2, MUL])
        dot = sb("dot", [128, 2, 3, MUL])
        v3 = sb("v3", [128, 2, 3, MUL])
        feat = sb("feat", [128, 2, 4 * MUL])
        sqrt3 = sb("inv_sqrt3", [128, 3])
        one4 = sb("one4", [128, 4])
        is_lo = sb("is_lo", [128, 1])
        sign = sb("sign", [128, 1])
        ps_tr = ps("ps_tr", [128, 4, 128])
        ps_a = [ps(f"ps_a{t}", [128, 3 * MUL]) for t in range(2)]
        ps_ip = ps("ps_ip", [128, 3, 128])
        ps_hid = ps("ps_hid", [128, 256])
        ps_f = ps("ps_f", [128, 4 * MUL])
        ps_s = ps("ps_s", [128, 4 * MUL])
        ps_sum = ps("ps_sum", [NG, 4 * MUL])

        rec_landed = [sem(f"rec_landed{k}") for k in range(U)]
        rows_landed = [[sem(f"rows_landed{k}_{t}") for t in range(2)] for k in range(U)]
        names = ("const_set rows_set bidx_ready sh_ready oh_ready q0_ready v3_ready z_ready tr_done recT_ready ohT_ready "
                 "a_ready prod_ready ip_ps ip_ready hid_done abs_ready exp_ready ln_ready ssp_ready zc_ready f_ps "
                 "fs_ready s_ps w_ready u_ready x0s_ready dot1_ready dot2_ready w4_ready out1_done feat_ready "
                 "tile_summed acc_done")
        S = {n: sem(n) for n in names.split()}
        block = ctx.enter_context(nc.Block())

        def has(s):
            return not isinstance(s, int) or 0 <= s < STEPS

        def steps(eng, body):
            for s in range(U):
                body(s, s, 0)
            with eng.Fori(1, ROUNDS) as r:
                for k in range(U):
                    body(r * U + k, k, r)
            for s in range(ROUNDS * U, STEPS):
                body(s, s % U, s // U)

        def ahead(k, rnd, n):
            return (k + n) % U, rnd + (k + n) // U

        @block.sync
        def _(sp):
            def load(s, k, rnd):
                wait(sp, S["tr_done"], s - U + 1)
                sp.dma_start(rec[k][:, :, :],
                             scratch["sorted"][bass.ds(s * STEP, STEP), :].rearrange("(t p) r -> p t r", p=128)
                             ).then_inc(rec_landed[k], 16)
            steps(sp, load)

        @block.gpsimd
        def _(pool):
            pool.memset(sqrt3[:, :], 3.0 ** -0.5).then_inc(S["const_set"], 1)
            pool.memset(one4[:, :], 1.0).then_inc(S["const_set"], 1)
            pool.wait_ge(S["const_set"], 2)

            def first(s, k, rnd):
                pool.wait_ge(rec_landed[k], 16 * (rnd + 1))
                wait(pool, S["feat_ready"], 2 * (s - U + 1))
                wait(pool, S["tile_summed"], 2 * (s - U + 1))
                pool.tensor_tensor(shs[k][:, :, :], rec[k][:, :, SH:SH + 4],
                                   one4[:, :].unsqueeze(1).to_broadcast([128, 2, 4]), ALU.mult).then_inc(S["sh_ready"], 1)
                pool.tensor_copy(bidx[k][:, :], rec[k][:, :, B_ID]).then_inc(S["bidx_ready"], 1)
                pool.wait_ge(S["bidx_ready"], s + 1)
                pool.tensor_tensor(sht[k][:, :, :], rec[k][:, :, SH + 1:SH + 4],
                                   sqrt3[:, :].unsqueeze(1).to_broadcast([128, 2, 3]), ALU.mult).then_inc(S["sh_ready"], 1)
                gather(k, 0)

            def gather(k, t):
                pool.indirect_dma_start(
                    out=rows[k][:, t, :], out_offset=None, in_=scratch["rows"],
                    in_offset=bass.IndirectOffsetOnAxis(ap=bidx[k][:, t:t + 1], axis=0)
                ).then_inc(rows_landed[k][t], 16)

            def second(k):
                gather(k, 1)
                for t in range(2):
                    pool.tensor_scalar(oh[k][:, t, :], keep["iota"][:, :], rec[k][:, t, A_LOC:A_LOC + 1], None,
                                       ALU.is_equal).then_inc(S["oh_ready"], 1)

            def vectors(s, k, t):
                pool.wait_ge(S["w_ready"], 2 * s + t + 1)
                wait(pool, S["feat_ready"], 2 * s + t - 1)
                pool.tensor_tensor(v3[:, t, :, :], rows[k][:, t, 4 * MUL:ROW].rearrange("p (m u) -> p m u", m=3),
                                   w[:, t, MUL:2 * MUL].unsqueeze(1).to_broadcast([128, 3, MUL]),
                                   ALU.mult).then_inc(S["v3_ready"], 1)

            def body(s, k, rnd):
                vectors(s, k, 0)
                if has(s + 4):
                    first(s + 4, *ahead(k, rnd, 4))
                vectors(s, k, 1)
                if has(s + 4):
                    second(ahead(k, rnd, 4)[0])
            for s in range(4):
                first(s, s, 0)
                second(s)
            steps(pool, body)

        @block.vector
        def _(dve):
            for q in range(4):
                lo = q % 2 == 0
                dve.memset(is_lo[32 * q:32 * q + 32, :], 1.0 if lo else 0.0).then_inc(S["rows_set"], 1)
                dve.memset(sign[32 * q:32 * q + 32, :], -1.0 if lo else 1.0).then_inc(S["rows_set"], 1)
            dve.wait_ge(S["rows_set"], 8)

            def products(s, k, rnd):
                for t in range(2):
                    dve.wait_ge(rows_landed[k][t], 16 * (rnd + 1))
                    dve.wait_ge(S["a_ready"], 2 * s + t + 1)
                    wait(dve, S["ip_ps"], 2 * s + t - 1)
                    dve.tensor_tensor(prod[:, t, :], ps_a[t][:, :], rows[k][:, t, 0:3 * MUL],
                                      ALU.mult).then_inc(S["prod_ready"], 1)

            def softplus(s):
                dve.wait_ge(S["ln_ready"], s + 1)
                wait(dve, S["z_ready"], s)
                dve.scalar_tensor_tensor(ssp[:, :], ps_hid[:, :], 0.0, soft[:, :], ALU.max, ALU.add
                                         ).then_inc(S["ssp_ready"], 1)

            def split(s, k):
                dve.wait_ge(S["zc_ready"], s + 1)
                wait(dve, S["s_ps"], 2 * (s - U + 1))
                dve.scalar_tensor_tensor(z[k][:, :, :].rearrange("p a b -> p (a b)"), ssp[:, :], is_lo[:, :],
                                         zc[:, :].bitcast(F32), ALU.mult, ALU.add).then_inc(S["z_ready"], 1)

            def head(s, k, t):
                n = 2 * s + t
                x0 = rows[k][:, t, 3 * MUL:4 * MUL]
                x1 = rows[k][:, t, 4 * MUL:ROW].rearrange("p (m u) -> p m u", m=3)
                dve.wait_ge(S["fs_ready"], 2 * n + 2)
                dve.wait_ge(S["s_ps"], n + 1)
                dve.tensor_tensor(w[:, t, :], ps_s[:, :], fs[:, t, :], ALU.mult).then_inc(S["w_ready"], 1)
                dve.wait_ge(S["x0s_ready"], n + 1)
                dve.scalar_tensor_tensor(dot[:, t, 1, :], x1[:, 1, :], sht[k][:, t, 1:2], dot[:, t, 0, :],
                                         ALU.mult, ALU.add).then_inc(S["dot1_ready"], 1)
                dve.wait_ge(S["w_ready"], n + 1)
                wv = w[:, t, :].rearrange("p (a b u) -> p a b u", a=2, b=2)[:, :, 0, :]
                dve.tensor_tensor(u[:, t, :, :], wv, x0.unsqueeze(1).to_broadcast([128, 2, MUL]),
                                  ALU.mult).then_inc(S["u_ready"], 1)
                dve.wait_ge(S["dot1_ready"], n + 1)
                dve.scalar_tensor_tensor(dot[:, t, 2, :], x1[:, 2, :], sht[k][:, t, 2:3], dot[:, t, 1, :],
                                         ALU.mult, ALU.add).then_inc(S["dot2_ready"], 1)

            def tail(s, k, t):
                n = 2 * s + t
                wait(dve, S["tile_summed"], n - 1)
                dve.wait_ge(S["dot2_ready"], n + 1)
                dve.tensor_tensor(dot[:, t, 0, :], dot[:, t, 2, :], w[:, t, 3 * MUL:4 * MUL],
                                  ALU.mult).then_inc(S["w4_ready"], 1)
                dve.wait_ge(S["v3_ready"], n + 1)
                for m in range(3):
                    dve.scalar_tensor_tensor(feat[:, t, (1 + m) * MUL:(2 + m) * MUL], u[:, t, 1, :],
                                             shs[k][:, t, 1 + m:2 + m], v3[:, t, m, :], ALU.mult, ALU.add
                                             ).then_inc(S["out1_done"], 1)
                dve.wait_ge(S["w4_ready"], n + 1)
                dve.wait_ge(S["out1_done"], 3 * n + 3)
                dve.tensor_tensor(feat[:, t, 0:MUL], u[:, t, 0, :], dot[:, t, 0, :], ALU.add
                                  ).then_inc(S["feat_ready"], 1)

            def total(s):
                g = dve.value_load(keep["step_group"][0:1, bass.ds(s, 1)], min_val=0, max_val=G - 1)
                dve.wait_ge(S["tile_summed"], 2 * s + 2)
                wait(dve, S["acc_done"], s)
                dve.tensor_tensor(keep["acc"][:, bass.ds(g, 1), :], ps_sum[:, :].unsqueeze(1),
                                  keep["acc"][:, bass.ds(g, 1), :], ALU.add).then_inc(S["acc_done"], 1)

            def body(s, k, rnd):
                if has(s + 2):
                    products(s + 2, *ahead(k, rnd, 2))
                head(s, k, 0)
                if has(s + 1):
                    softplus(s + 1)
                tail(s, k, 0)
                if has(s - 1):
                    total(s - 1)
                head(s, k, 1)
                if has(s + 1):
                    split(s + 1, ahead(k, rnd, 1)[0])
                tail(s, k, 1)
            products(0, 0, 0)
            softplus(0)
            split(0, 0)
            products(1, 1, 0)
            steps(dve, body)
            total(STEPS - 1)

        @block.scalar
        def _(act):
            act.preload_act_table_set("natural_log_exp_and_others")
            act.wait_ge(S["rows_set"], 8)

            def transposed(s, k):
                g = act.value_load(keep["step_group"][0:1, bass.ds(s, 1)], min_val=0, max_val=G - 1)
                act.wait_ge(S["tr_done"], s + 1)
                wait(act, S["hid_done"], s - U + 1)
                act.activation(recT[k][:, :, :], ps_tr[0:RECK, 0:2, :], ACT.Copy).then_inc(S["recT_ready"], 1)
                act.activation(ohT[k][:, :, :], ps_tr[0:NG, 2:4, :], ACT.Copy).then_inc(S["ohT_ready"], 1)
                act.activation(q0s[k][:, :, :].unsqueeze(1),
                               keep["tab"][:, bass.ds(g, 1), :, 3 * MUL:4 * MUL].bitcast(F32), ACT.Copy
                               ).then_inc(S["q0_ready"], 1)

            def inner(s, t):
                act.wait_ge(S["ip_ps"], 2 * s + t + 1)
                wait(act, S["hid_done"], s)
                act.activation(ipT[:, :, t, :], ps_ip[:, :, :], ACT.Copy, scale=1.0 / 3.0).then_inc(S["ip_ready"], 1)

            def softplus(s):
                act.wait_ge(S["hid_done"], s + 1)
                wait(act, S["ssp_ready"], s)
                act.activation(soft[:, :], ps_hid[:, :], ACT.Abs).then_inc(S["abs_ready"], 1)
                act.wait_ge(S["abs_ready"], s + 1)
                act.activation(soft[:, :], soft[:, :], ACT.Exp, scale=-1.0).then_inc(S["exp_ready"], 1)
                act.wait_ge(S["exp_ready"], s + 1)
                act.activation(soft[:, :], soft[:, :], ACT.Ln, bias=keep["half"][:, :], scale=0.5).then_inc(S["ln_ready"], 1)

            def rounded(s):
                act.wait_ge(S["ssp_ready"], s + 1)
                wait(act, S["z_ready"], s)
                act.activation(zc[:, :], ssp[:, :], ACT.Copy, scale=sign[:, :]).then_inc(S["zc_ready"], 1)

            def filters(s, k, rnd, t):
                n = 2 * s + t
                act.wait_ge(S["sh_ready"], 2 * s + 2)
                wait(act, S["feat_ready"], n - 1)
                act.wait_ge(S["f_ps"], n + 1)
                act.activation(fs[:, t, 0:2 * MUL], ps_f[:, 0:2 * MUL], ACT.Copy,
                               scale=shs[k][:, t, 0:1]).then_inc(S["fs_ready"], 1)
                act.activation(fs[:, t, 2 * MUL:4 * MUL], ps_f[:, 2 * MUL:4 * MUL], ACT.Copy).then_inc(S["fs_ready"], 1)
                act.wait_ge(rows_landed[k][t], 16 * (rnd + 1))
                act.activation(dot[:, t, 0, :], rows[k][:, t, 4 * MUL:5 * MUL], ACT.Copy,
                               scale=sht[k][:, t, 0:1]).then_inc(S["x0s_ready"], 1)

            def body(s, k, rnd):
                filters(s, k, rnd, 0)
                if has(s + 1):
                    softplus(s + 1)
                if has(s + 2):
                    inner(s + 2, 0)
                filters(s, k, rnd, 1)
                if has(s + 1):
                    rounded(s + 1)
                if has(s + 2):
                    inner(s + 2, 1)
                if has(s + 3):
                    transposed(s + 3, ahead(k, rnd, 3)[0])
            for s in range(2):
                transposed(s, s)
                inner(s, 0)
                inner(s, 1)
                if s == 0:
                    softplus(0)
                    rounded(0)
            transposed(2, 2)
            steps(act, body)

        @block.tensor
        def _(pe):
            def transposes(s, k, rnd):
                pe.wait_ge(rec_landed[k], 16 * (rnd + 1))
                pe.wait_ge(S["oh_ready"], 2 * s + 2)
                wait(pe, S["ohT_ready"], s)
                for t in range(2):
                    pe.transpose(ps_tr[0:NG, 2 + t, :], oh[k][:, t, :], keep["ident"][:, :])
                for t in range(2):
                    ins = pe.transpose(ps_tr[0:RECK, t, :], rec[k][:, t, 0:RECK], keep["ident"][:, :])
                ins.then_inc(S["tr_done"], 1)

            def gathers(s, k):
                g = pe.value_load(keep["step_group"][0:1, bass.ds(s, 1)], min_val=0, max_val=G - 1)
                pe.wait_ge(S["ohT_ready"], s + 1)
                for t in range(2):
                    wait(pe, S["prod_ready"], 2 * s + t - 1)
                    for i in range(2):
                        ins = pe.matmul(ps_a[t][:, :].unsqueeze(1).unsqueeze(1), ohT[k][:, t, :],
                                        keep["tab"][:, bass.ds(g, 1), i:i + 1, 0:3 * MUL], start=(i == 0), stop=(i == 1))
                    ins.then_inc(S["a_ready"], 1)

            def inner(s, t):
                pe.wait_ge(S["prod_ready"], 2 * s + t + 1)
                wait(pe, S["ip_ready"], 2 * s + t)
                for m in range(3):
                    ins = pe.transpose(ps_ip[:, m, :], prod[:, t, m * MUL:(m + 1) * MUL], keep["ident"][:, :])
                ins.then_inc(S["ip_ps"], 1)

            def hidden(s, k):
                pe.wait_ge(S["recT_ready"], s + 1)
                wait(pe, S["ssp_ready"], s)
                pe.matmul(ps_hid[:, :], keep["wf1"][:, :, :].rearrange("p q k -> p (q k)"),
                          recT[k][:, :, :].rearrange("p a b -> p (a b)"), start=True, stop=False)
                pe.wait_ge(S["q0_ready"], s + 1)
                for i in range(2):
                    pe.matmul(ps_hid[:, :], q0s[k][:, i, :], ohT[k][:, :, :].rearrange("p a b -> p (a b)"),
                              start=False, stop=False)
                pe.wait_ge(S["ip_ready"], 2 * s + 2)
                for m in range(3):
                    ins = pe.matmul(ps_hid[:, :], keep["ws1c"][:, :, :].rearrange("p q k -> p (q k)"),
                                    ipT[:, m, :, :].rearrange("p a b -> p (a b)"), start=False, stop=(m == 2))
                ins.then_inc(S["hid_done"], 1)

            def weights(s, k, t):
                n = 2 * s + t
                pe.wait_ge(S["z_ready"], s + 1)
                wait(pe, S["fs_ready"], 2 * n)
                wait(pe, S["w_ready"], n)
                for i in range(2):
                    f = pe.matmul(ps_f[:, :], z[k][0:64, t, :], keep["w2"][0:64, i, :], start=(i == 0), stop=(i == 1))
                    if i == 1:
                        f.then_inc(S["f_ps"], 1)
                    g = pe.matmul(ps_s[:, :], z[k][64:128, t, :], keep["w2"][64:128, i, :], start=(i == 0), stop=(i == 1))
                g.then_inc(S["s_ps"], 1)

            def sums(s, k, t):
                if t == 0:
                    wait(pe, S["acc_done"], s)
                pe.wait_ge(S["feat_ready"], 2 * s + t + 1)
                pe.matmul(ps_sum[:, :], oh[k][:, t, :], feat[:, t, :], start=(t == 0), stop=(t == 1)
                          ).then_inc(S["tile_summed"], 1)

            def body(s, k, rnd):
                weights(s, k, 0)
                if has(s + 2):
                    inner(s + 2, 0)
                if has(s - 1):
                    sums(s - 1, (k - 1) % U, 1)
                weights(s, k, 1)
                if has(s + 2):
                    inner(s + 2, 1)
                if has(s + 3):
                    transposes(s + 3, *ahead(k, rnd, 3))
                if has(s + 2):
                    hidden(s + 2, ahead(k, rnd, 2)[0])
                if has(s + 3):
                    gathers(s + 3, ahead(k, rnd, 3)[0])
                sums(s, k, 0)
            for s in range(2):
                transposes(s, s, 0)
                gathers(s, s)
                inner(s, 0)
                inner(s, 1)
                hidden(s, s)
            transposes(2, 2, 0)
            gathers(2, 2)
            steps(pe, body)
            sums(STEPS - 1, (STEPS - 1) % U, 1)


def ffn(nc, a, keep, scratch, out):
    with ExitStack() as ctx:
        def sb(name, shape, dt=F32):
            return ctx.enter_context(nc.sbuf_tensor(name, shape, dt))
        plan = {"weight": sb("weight", [NG, 2, G]),
                "slot": sb("slot", [NG, 2, G], I32),
                "tile_expert": sb("tile_expert", [1, TILES], I32)}
        route(nc, a, keep, scratch, plan)
        experts(nc, a, keep, scratch, plan, out)


def route(nc, a, keep, scratch, plan):
    with ExitStack() as ctx:
        def sb(name, shape, dt=F32):
            return ctx.enter_context(nc.sbuf_tensor(name, shape, dt))

        def ps(name, shape, dt=F32):
            return ctx.enter_context(nc.psum_tensor(name, shape, dt))

        wo0 = sb("wo0", [128, MUL])
        wo1 = sb("wo1", [128, MUL])
        bo0 = sb("bo0", [1, MUL])
        ones_row = sb("ones_row2", [1, NG])
        rw = sb("rw_s", [128, 4, NEXP])
        rb = sb("rb_s", [1, NEXP])
        eps_t = sb("eps_t2", [NG, 1])
        tri = sb("tri2", [NG, NG])
        onesq = sb("onesq2", [NG, NG])
        tile_no = sb("tile_no", [1, TILES])
        tile_f = sb("tile_f", [1, TILES])
        s1 = sb("s1", [NG, D])
        accT = sb("accT", [128, 4, NG])
        x3 = sb("x3", [NG, G, D])
        stats = sb("stats2", [NG, G, 6])
        mv = sb("mv2", [NG, G, 2])
        std = sb("std2", [NG, G])
        rstd = sb("rstd2", [NG, G])
        x3s = sb("x3s", [NG, D])
        x3Ts = sb("x3Ts", [128, 4, NG])
        logit = sb("logit", [NG, G, NEXP])
        top = sb("top", [NG, G, 8])
        topi = sb("topi", [NG, G, 8], mybir.dt.uint32)
        choice = sb("choice", [NG, 2, G])
        gap = sb("gap", [NG, 3, G])
        hit = sb("hit", [NG, NEXP, 2 * G])
        rank = sb("rank2", [NG, NEXP, 2 * G])
        small = sb("small2", [NG, 5, NEXP])
        zeros = sb("zeros2", [NG, 2 * G])
        cnt_i = sb("cnt_i2", [NG, 2, NEXP], I32)
        pos = sb("pos2", [NG, 2 * G])
        ps_T = ps("ps_T", [128, 4, NG])
        ps_o = ps("ps_o", [NG, 4, MUL])
        ps_T3 = ps("ps_T3", [128, 4, NG])
        ps_l = ps("ps_l", [NG, NEXP])
        ps_cnt = ps("ps_cnt", [NG, 2, NEXP])
        names = ("params_in set2 tri_set dve2_step s1_ready accT_ps accT_ready o_ps x2_ready var2 std2_done x3s_ready "
                 "x3_done x3T_ps x3T_ready l_ps l_ready gap_ready exp2_ready totals2 prefixed2 slots_ready sent")
        S = {n: ctx.enter_context(nc.semaphore(n)) for n in names.split()}
        block = ctx.enter_context(nc.Block())

        @block.sync
        def _(sp):
            for dst, src in ((wo0[:, :], a["L0_gnn_W_o0"]), (wo1[:, :], a["L0_gnn_W_o1"]),
                             (bo0[:, :], a["L0_gnn_b_o0"].rearrange("(c p) -> c p", c=1)),
                             (rw[:, :, :], a["rw"].rearrange("(c p) e -> p c e", p=128)),
                             (rb[:, :], a["L0_ffn_router_b"].rearrange("(c p) -> c p", c=1))):
                sp.dma_start(dst, src).then_inc(S["params_in"], 16)

        @block.gpsimd
        def _(pool):
            pool.memset(ones_row[:, :], 1.0).then_inc(S["set2"], 1)
            pool.memset(eps_t[:, :], EPS).then_inc(S["set2"], 1)
            pool.memset(onesq[:, :], 1.0).then_inc(S["set2"], 1)
            pool.memset(zeros[:, :], 0.0).then_inc(S["set2"], 1)
            pool.iota(tile_no[:, :], [[TILE, TILES]], base=0, channel_multiplier=0,
                      allow_small_or_imprecise_dtypes=True).then_inc(S["set2"], 1)
            pool.wait_ge(S["set2"], 5)
            pool.affine_select(out=tri[:, :], in_=onesq[:, :], compare_op=ALU.is_ge,
                               fill=0.0, base=-1, pattern=[[1, NG]], channel_multiplier=-1).then_inc(S["tri_set"], 1)
            pool.wait_ge(S["x3_done"], 1)
            pool.wait_ge(S["slots_ready"], 1)
            for i in range(2):
                for t in range(G):
                    pool.indirect_dma_start(
                        out=scratch["x_slots"], out_offset=bass.IndirectOffsetOnAxis(ap=plan["slot"][:, i, t:t + 1], axis=0),
                        in_=x3[:, t, :], in_offset=None).then_inc(S["sent"], 16)
            pool.wait_ge(S["sent"], 16 * 2 * G)

        @block.vector
        def _(dve):
            done = [0]

            def link(ins):
                done[0] += 1
                ins.then_inc(S["dve2_step"], 1)
                dve.wait_ge(S["dve2_step"], done[0])

            def linear(t):
                x_t = keep["x"][:, bass.ds(t, 1), :]
                wait(dve, S["accT_ps"], t)
                dve.tensor_scalar(s1[:, :].unsqueeze(1), keep["acc"][:, bass.ds(t, 1), :], 1.0, None, ALU.mult
                                  ).then_inc(S["s1_ready"], 1)
                dve.wait_ge(S["o_ps"], t + 1)
                dve.tensor_tensor(x_t[:, :, 0:MUL], ps_o[:, 0:1, :], x_t[:, :, 0:MUL], ALU.add).then_inc(S["x2_ready"], 1)
                x_v = x_t[:, :, MUL:D].rearrange("p g (u m) -> p (g m) u", m=3)
                dve.tensor_tensor(x_v, ps_o[:, 1:4, :], x_v, ALU.add).then_inc(S["x2_ready"], 1)
            linear(0)
            with dve.Fori(1, G) as t:
                linear(t)
            dve.wait_ge(S["x2_ready"], 2 * G)
            for t in range(G):
                ins = dve.bn_stats(stats[:, t, :], keep["x"][:, t, :])
            link(ins)
            for t in range(G):
                ins = dve.bn_aggr(mv[:, t, :], stats[:, t, :])
            ins.then_inc(S["var2"], 1)
            dve.wait_ge(S["std2_done"], 1)
            link(dve.reciprocal(rstd[:, :], std[:, :]))
            for t in range(G):
                ins = dve.tensor_scalar(x3[:, t, :], keep["x"][:, t, :], mv[:, t, 0:1], rstd[:, t:t + 1],
                                        ALU.subtract, ALU.mult)
            ins.then_inc(S["x3_done"], 1)
            dve.wait_ge(S["x3_done"], 1)

            def router(t):
                wait(dve, S["x3T_ps"], t)
                dve.tensor_scalar(x3s[:, :].unsqueeze(1), x3[:, bass.ds(t, 1), :], 1.0, None, ALU.mult
                                  ).then_inc(S["x3s_ready"], 1)
                dve.wait_ge(S["l_ps"], t + 1)
                dve.tensor_scalar(logit[:, bass.ds(t, 1), :], ps_l[:, :].unsqueeze(1), 1.0, None, ALU.mult
                                  ).then_inc(S["l_ready"], 1)
            router(0)
            with dve.Fori(1, G) as t:
                router(t)
            dve.wait_ge(S["l_ready"], G)
            for t in range(G):
                ins = dve.max(top[:, t, :], logit[:, t, :])
            link(ins)
            dve.tensor_tensor(gap[:, 0, :], top[:, :, 1], top[:, :, 0], ALU.subtract).then_inc(S["gap_ready"], 1)
            for t in range(G):
                ins = dve.max_index(topi[:, t, :], top[:, t, :], logit[:, t, :])
            link(ins)
            link(dve.tensor_copy(choice[:, :, :], topi[:, :, 0:2].rearrange("p g i -> p i g")))
            dve.wait_ge(S["set2"], 5)
            chosen = choice[:, :, :].rearrange("p i g -> p (i g)")
            for e in range(NEXP):
                ins = dve.tensor_scalar(hit[:, e, :], chosen, float(e), None, ALU.is_equal)
            link(ins)
            for e in range(NEXP):
                ins = dve.tensor_tensor_scan(rank[:, e, :], hit[:, e, :], zeros[:, :], 0.0, ALU.add, ALU.add)
            link(ins)
            dve.tensor_copy(small[:, 0, :], rank[:, :, 2 * G - 1]).then_inc(S["totals2"], 1)
            dve.wait_ge(S["exp2_ready"], 1)
            link(dve.tensor_scalar(gap[:, 2, :], gap[:, 1, :], 1.0, None, ALU.add))
            link(dve.reciprocal(plan["weight"][:, 0, :], gap[:, 2, :]))
            link(dve.tensor_tensor(plan["weight"][:, 1, :], gap[:, 1, :], plan["weight"][:, 0, :], ALU.mult))
            dve.wait_ge(S["prefixed2"], 1)
            link(dve.tensor_scalar(cnt_i[:, 0, :], ps_cnt[:, 1, :], float(TILE - 1), None, ALU.add))
            link(dve.tensor_scalar(cnt_i[:, 1, :], cnt_i[:, 0, :], TILE_BITS, TILE_BITS,
                                   ALU.logical_shift_right, ALU.logical_shift_left))
            link(dve.tensor_copy(small[:, 1, :], cnt_i[:, 1, :]))
            link(dve.tensor_tensor_scan(small[:, 2, :], small[:, 1, :], zeros[:, 0:NEXP], 0.0, ALU.add, ALU.add))
            link(dve.tensor_tensor(small[:, 3, :], small[:, 2, :], small[:, 1, :], ALU.subtract))
            link(dve.scalar_tensor_tensor(small[:, 4, :], small[:, 3, :], -1.0, ps_cnt[:, 0, :], ALU.add, ALU.add))
            for e in range(NEXP):
                link(dve.scalar_tensor_tensor(rank[:, e, :], rank[:, e, :], small[:, 4, e:e + 1], hit[:, e, :],
                                              ALU.add, ALU.mult))
                if e:
                    link(dve.tensor_tensor(pos[:, :], pos[:, :], rank[:, e, :], ALU.add))
                else:
                    link(dve.tensor_copy(pos[:, :], rank[:, 0, :]))
            dve.tensor_copy(plan["slot"][:, :, :], pos[:, :].rearrange("p (i g) -> p i g", i=2)
                            ).then_inc(S["slots_ready"], 1)
            link(dve.tensor_scalar(tile_f[:, :], tile_no[:, :], small[0:1, 3, 1:2], None, ALU.is_ge))
            for e in range(2, NEXP):
                link(dve.scalar_tensor_tensor(tile_f[:, :], tile_no[:, :], small[0:1, 3, e:e + 1], tile_f[:, :],
                                              ALU.is_ge, ALU.add))
            link(dve.tensor_copy(plan["tile_expert"][:, :], tile_f[:, :]))

        @block.scalar
        def _(act):
            def linear(t):
                act.wait_ge(S["accT_ps"], t + 1)
                wait(act, S["o_ps"], t)
                act.activation(accT[:, :, :], ps_T[:, :, :], ACT.Copy).then_inc(S["accT_ready"], 1)
            linear(0)
            with act.Fori(1, G) as t:
                linear(t)
            act.wait_ge(S["set2"], 5)
            act.wait_ge(S["var2"], 1)
            act.activation(std[:, :], mv[:, :, 1], ACT.Sqrt, bias=eps_t[:, :]).then_inc(S["std2_done"], 1)

            def router(t):
                act.wait_ge(S["x3T_ps"], t + 1)
                wait(act, S["l_ps"], t)
                act.activation(x3Ts[:, :, :], ps_T3[:, :, :], ACT.Copy).then_inc(S["x3T_ready"], 1)
            router(0)
            with act.Fori(1, G) as t:
                router(t)
            act.wait_ge(S["gap_ready"], 1)
            act.activation(gap[:, 1, :], gap[:, 0, :], ACT.Exp).then_inc(S["exp2_ready"], 1)

        @block.tensor
        def _(pe):
            pe.wait_ge(S["params_in"], 16 * 5)
            pe.wait_ge(S["set2"], 5)

            def linear(t):
                pe.wait_ge(S["s1_ready"], t + 1)
                wait(pe, S["accT_ready"], t)
                for c in range(4):
                    ins = pe.transpose(ps_T[:, c, :], s1[:, c * 128:(c + 1) * 128], keep["ident"][0:NG, 0:NG])
                ins.then_inc(S["accT_ps"], 1)
                pe.wait_ge(S["accT_ready"], t + 1)
                wait(pe, S["x2_ready"], 2 * t)
                pe.matmul(ps_o[:, 0, :], accT[:, 0, :], wo0[:, :], start=True, stop=False)
                pe.matmul(ps_o[:, 0, :], ones_row[:, :], bo0[:, :], start=False, stop=True)
                for m in range(3):
                    ins = pe.matmul(ps_o[:, 1 + m, :], accT[:, 1 + m, :], wo1[:, :], start=True, stop=True)
                ins.then_inc(S["o_ps"], 1)
            linear(0)
            with pe.Fori(1, G) as t:
                linear(t)

            def router(t):
                pe.wait_ge(S["x3s_ready"], t + 1)
                wait(pe, S["x3T_ready"], t)
                for c in range(4):
                    ins = pe.transpose(ps_T3[:, c, :], x3s[:, c * 128:(c + 1) * 128], keep["ident"][0:NG, 0:NG])
                ins.then_inc(S["x3T_ps"], 1)
                pe.wait_ge(S["x3T_ready"], t + 1)
                wait(pe, S["l_ready"], t)
                for c in range(4):
                    pe.matmul(ps_l[:, :], x3Ts[:, c, :], rw[:, c, :], start=(c == 0), stop=False)
                pe.matmul(ps_l[:, :], ones_row[:, :], rb[:, :], start=False, stop=True).then_inc(S["l_ps"], 1)
            router(0)
            with pe.Fori(1, G) as t:
                router(t)
            pe.wait_ge(S["tri_set"], 1)
            pe.wait_ge(S["totals2"], 1)
            pe.matmul(ps_cnt[:, 0, :], tri[:, :], small[:, 0, :], start=True, stop=True)
            pe.matmul(ps_cnt[:, 1, :], onesq[:, :], small[:, 0, :], start=True, stop=True).then_inc(S["prefixed2"], 1)


def experts(nc, a, keep, scratch, plan, out):
    FC = FF // 128
    J = TILE // 128
    U = 2
    ROUNDS = (TILES - 1) // U
    with ExitStack() as ctx:
        def sb(name, shape, dt=F32):
            return ctx.enter_context(nc.sbuf_tensor(name, shape, dt))

        def ps(name, shape, dt=F32):
            return ctx.enter_context(nc.psum_tensor(name, shape, dt))

        def sem(name):
            return ctx.enter_context(nc.semaphore(name))

        w1 = [sb(f"w1_{i}", [128, 4, 2 * FF]) for i in range(U)]
        w2 = [sb(f"w2_{i}", [128, FC, D]) for i in range(U)]
        b1 = [sb(f"b1_{i}", [128, 2 * FC]) for i in range(U)]
        b2 = [sb(f"b2_{i}", [1, D]) for i in range(U)]
        xs = [sb(f"xs_{i}", [128, J, D]) for i in range(U)]
        xT = [sb(f"xT_{i}", [128, 4, TILE]) for i in range(U)]
        ones_row = sb("ones_row3", [1, 128])
        gate = sb("gate", [128, 2, TILE])
        act_a = sb("act_a", [128, FC, TILE])
        y = sb("y", [128, J, D])
        yg = [sb(f"yg{i}", [NG, 2, D]) for i in range(4)]
        ps_h = [ps(f"ps_h{i}", [128, 2, TILE]) for i in range(4)]
        ps_y = [ps(f"ps_y{i}", [128, D]) for i in range(J)]
        ps_x = [ps(f"ps_x{i}", [128, 4, 128]) for i in range(J)]
        names = ("set3 xT_ps xT_ready gate_ready h_ps a_ready y_ps y_ready x4_first x4_done")
        S = {n: sem(n) for n in names.split()}
        w1_in = [sem(f"w1_in{i}") for i in range(U)]
        w2_in = [sem(f"w2_in{i}") for i in range(U)]
        xs_in = [sem(f"xs_in{i}") for i in range(U)]
        y_out = sem("y_out")
        yg_in = [sem(f"yg_in{i}") for i in range(4)]
        stored = sem("stored")
        block = ctx.enter_context(nc.Block())

        def has(s):
            return not isinstance(s, int) or 0 <= s < TILES

        def tiles(eng, body):
            for s in range(U):
                body(s, s, 0)
            with eng.Fori(1, ROUNDS) as r:
                for k in range(U):
                    body(r * U + k, k, r)
            for s in range(ROUNDS * U, TILES):
                body(s, s % U, s // U)

        @block.sync
        def _(sp):
            def load(s, k, rnd):
                e = sp.value_load(plan["tile_expert"][0:1, bass.ds(s, 1)], min_val=0, max_val=NEXP - 1)
                wait(sp, S["y_ps"], J * (s - U + 1))
                sp.dma_start(xs[k][:, :, :], scratch["x_slots"][bass.ds(s * TILE, TILE), :].rearrange("(j p) d -> p j d", p=128)
                             ).then_inc(xs_in[k], 16)
                sp.dma_start(w1[k][:, :, :], a["w1t"][bass.ds(e, 1)].rearrange("e (c p) f -> p (e c) f", p=128)).then_inc(w1_in[k], 16)
                sp.dma_start(b1[k][:, :], a["b1"][bass.ds(e, 1)].rearrange("e p f -> p (e f)")).then_inc(w1_in[k], 16)
                sp.dma_start(w2[k][:, :, :], a["w2t"][bass.ds(e, 1)].rearrange("e (c p) d -> p (e c) d", p=128)).then_inc(w2_in[k], 16)
                sp.dma_start(b2[k][:, :], a["L0_ffn_fc2_b"][bass.ds(e, 1), :]).then_inc(w2_in[k], 16)
            tiles(sp, load)
            for t in range(G):
                sp.wait_ge(S["x4_done"], t + 1)
                sp.dma_start(out[t * NG:(t + 1) * NG, :], keep["x"][:, t, :]).then_inc(stored, 16)
            sp.wait_ge(stored, 16 * G)

        @block.gpsimd
        def _(pool):
            pool.memset(ones_row[:, :], 1.0).then_inc(S["set3"], 1)
            pool.wait_ge(y_out, 16 * TILES)
            for t in range(G):
                if t >= 4:
                    pool.wait_ge(S["x4_done"], t - 3)
                for i in range(2):
                    pool.indirect_dma_start(
                        out=yg[t % 4][:, i, :], out_offset=None, in_=scratch["y_slots"],
                        in_offset=bass.IndirectOffsetOnAxis(ap=plan["slot"][:, i, t:t + 1], axis=0)
                    ).then_inc(yg_in[t % 4], 16)

        @block.scalar
        def _(act):
            def transposed(s, k):
                for j in range(J):
                    act.wait_ge(S["xT_ps"], J * s + j + 1)
                    if j == 0:
                        wait(act, S["h_ps"], FC * (s - U + 1))
                    act.activation(xT[k][:, :, j * 128:(j + 1) * 128], ps_x[j][:, :, :], ACT.Copy).then_inc(S["xT_ready"], 1)

            def results(s):
                wait(act, y_out, 16 * s)
                for j in range(J):
                    act.wait_ge(S["y_ps"], J * s + j + 1)
                    act.activation(y[:, j, :], ps_y[j][:, :], ACT.Copy).then_inc(S["y_ready"], 1)
                act.wait_ge(S["y_ready"], J * s + J)
                act.dma_start(scratch["y_slots"][bass.ds(s * TILE, TILE), :].rearrange("(j p) d -> p j d", p=128),
                              y[:, :, :]).then_inc(y_out, 16)

            def body(s, k, rnd):
                act.wait_ge(w1_in[k], 32 * rnd + 32)
                for f in range(FC):
                    act.wait_ge(S["h_ps"], s * FC + f + 1)
                    wait(act, S["a_ready"], s * FC + f - 1)
                    act.activation(gate[:, f % 2, :], ps_h[f % 4][:, 0, :], ACT.Silu, bias=b1[k][:, f:f + 1]
                                   ).then_inc(S["gate_ready"], 1)
                    if f == 1 and has(s - 1):
                        results(s - 1)
                if has(s + 1):
                    transposed(s + 1, (k + 1) % U)
            transposed(0, 0)
            tiles(act, body)
            results(TILES - 1)
            act.wait_ge(y_out, 16 * TILES)

        @block.vector
        def _(dve):
            def body(s, k, rnd):
                dve.wait_ge(w1_in[k], 32 * rnd + 32)
                for f in range(FC):
                    dve.wait_ge(S["gate_ready"], s * FC + f + 1)
                    if f == 0:
                        wait(dve, S["y_ps"], J * s)
                    dve.scalar_tensor_tensor(act_a[:, f, :], ps_h[f % 4][:, 1, :], b1[k][:, FC + f:FC + f + 1],
                                             gate[:, f % 2, :], ALU.add, ALU.mult).then_inc(S["a_ready"], 1)
            tiles(dve, body)
            for t in range(G):
                dve.wait_ge(yg_in[t % 4], 32 * (t // 4 + 1))
                x_t = keep["x"][:, t, :]
                dve.scalar_tensor_tensor(x_t, yg[t % 4][:, 0, :], plan["weight"][:, 0, t:t + 1], x_t,
                                         ALU.mult, ALU.add).then_inc(S["x4_first"], 1)
                dve.wait_ge(S["x4_first"], t + 1)
                dve.scalar_tensor_tensor(x_t, yg[t % 4][:, 1, :], plan["weight"][:, 1, t:t + 1], x_t,
                                         ALU.mult, ALU.add).then_inc(S["x4_done"], 1)

        @block.tensor
        def _(pe):
            def transposes(s, k, rnd):
                pe.wait_ge(xs_in[k], 16 * rnd + 16)
                wait(pe, S["xT_ready"], J * s)
                for j in range(J):
                    for c in range(4):
                        ins = pe.transpose(ps_x[j][:, c, :], xs[k][:, j, c * 128:(c + 1) * 128], keep["ident"][:, :])
                    ins.then_inc(S["xT_ps"], 1)

            def body(s, k, rnd):
                pe.wait_ge(S["xT_ready"], J * s + J)
                pe.wait_ge(w1_in[k], 32 * rnd + 32)
                for f in range(FC):
                    wait(pe, S["a_ready"], s * FC + f - 3)
                    for h in range(2):
                        for c in range(4):
                            col = h * FF + f * 128
                            ins = pe.matmul(ps_h[f % 4][:, h, :], w1[k][:, c, col:col + 128], xT[k][:, c, :],
                                            start=(c == 0), stop=(c == 3))
                    ins.then_inc(S["h_ps"], 1)
                if has(s + 1):
                    transposes(s + 1, (k + 1) % U, rnd + (k + 1) // U)
                pe.wait_ge(w2_in[k], 32 * rnd + 32)
                pe.wait_ge(S["a_ready"], s * FC + FC)
                wait(pe, S["y_ready"], J * s)
                for j in range(J):
                    for f in range(FC):
                        pe.matmul(ps_y[j][:, :], act_a[:, f, j * 128:(j + 1) * 128], w2[k][:, f, :],
                                  start=(f == 0), stop=False)
                    pe.matmul(ps_y[j][:, :], ones_row[:, :], b2[k][:, :], start=False, stop=True).then_inc(S["y_ps"], 1)
            pe.wait_ge(S["set3"], 1)
            transposes(0, 0, 0)
            tiles(pe, body)


_INS = ["x", "src", "dst", "rec", "L0_gnn_W_pre0", "L0_gnn_b_pre0", "L0_gnn_W_pre1", "L0_gnn_W_nd0", "L0_gnn_b_nd0",
        "L0_gnn_W_nd1", "L0_gnn_W_g1", "bg1", "L0_gnn_W_g2", "bg2", "L0_gnn_W_f1", "wf2",
        "L0_gnn_W_s1", "ws2", "L0_gnn_W_o0", "L0_gnn_b_o0", "L0_gnn_W_o1", "rw", "L0_ffn_router_b", "w1t", "b1",
        "w2t", "L0_ffn_fc2_b"]


def program(nc, a, out):
    with ExitStack() as ctx:
        keep = {}

        def sb(name, shape, dt=F32):
            keep[name] = ctx.enter_context(nc.sbuf_tensor(name, shape, dt))
        scratch = {"sorted": nc.dram_tensor("sorted_recs", (STEPS * STEP, REC), F32, kind="Internal").ap(),
                   "x_slots": nc.dram_tensor("x_slots", (TILES * TILE, D), F32, kind="Internal").ap(),
                   "y_slots": nc.dram_tensor("y_slots", (TILES * TILE, D), F32, kind="Internal").ap(),
                   "rows": nc.dram_tensor("node_rows", (N, ROW), F32, kind="Internal").ap()}
        sb("x", [NG, G, D])
        sb("acc", [NG, G, D])
        sb("ident", [128, 128])
        sb("half", [128, 1])
        with ExitStack() as gnn:
            ctx_, ctx = ctx, gnn
            sb("iota", [128, NG])
            sb("step_group", [1, STEPS], I32)
            sb("tab", [NG, G, 2, 4 * MUL], F32R)
            sb("wf1", [RECK, 4, HID])
            sb("ws1c", [128, 4, HID])
            sb("w2", [128, 2, 4 * MUL], F32R)
            prepare(nc, a, keep, scratch)
            edges(nc, keep, scratch)
            ctx = ctx_
        ffn(nc, a, keep, scratch, out)


def kernel(**inputs):
    import concourse.bacc as _bacc
    from concourse.bass_utils import run_bass_kernel_spmd as _run

    i = {k: np.ascontiguousarray(v) for k, v in inputs.items()}
    rec = np.zeros((E, REC), np.float32)
    rec[:, SH:SH + 4] = i["edge_attr_4"]
    rec[:, ATTR:RECK] = i["edge_attr_32"]
    i["rec"] = rec

    def by_path(w):
        return np.ascontiguousarray(w.reshape(HID, 4, MUL)[:, [0, 2, 1, 3], :].reshape(HID, 4 * MUL))
    i["wf2"], i["ws2"] = by_path(i["L0_gnn_W_f2"]), by_path(i["L0_gnn_W_s2"])
    for n in ("1", "2"):
        i["bg" + n] = np.ascontiguousarray(i["L0_gnn_b_g" + n].reshape(2, 128).T)
    i["rw"] = np.ascontiguousarray(i["L0_ffn_router_w"].T)
    i["w1t"] = np.ascontiguousarray(i["L0_ffn_fc1_w"].transpose(0, 2, 1))
    i["b1"] = np.ascontiguousarray(i["L0_ffn_fc1_b"].reshape(NEXP, 2 * FF // 128, 128).transpose(0, 2, 1))
    i["w2t"] = np.ascontiguousarray(i["L0_ffn_fc2_w"].transpose(0, 2, 1))
    nc = _bacc.Bacc("TRN2", target_bir_lowering=False, num_devices=1)
    arrays = {"in_" + n: i[n] for n in _INS}
    a = {n: nc.dram_tensor("in_" + n, i[n].shape, mybir.dt.from_np(i[n].dtype), kind="ExternalInput").ap() for n in _INS}
    out = nc.dram_tensor("out_x", (N, D), F32, kind="ExternalOutput").ap()
    program(nc, a, out)
    return _run(nc, [arrays], core_ids=[0]).results[0]["out_x"]
```

```python
from contextlib import ExitStack

import numpy as np
import concourse.bass as bass
from concourse import mybir

F32 = mybir.dt.float32
F32R = mybir.dt.float32r
I32 = mybir.dt.int32
ALU = mybir.AluOpType
ACT = mybir.ActivationFunctionType

N, D, E = 1250, 512, 40000
MUL = 128
G = 10
NG = N // G
EP = 125
EC = E // EP
STEP = 256
STEPS = (E - G) // STEP + G
REC = 38
A_LOC, B_ID, SH, ATTR = 0, 1, 2, 6
RECK = ATTR + 32
HID = 32
ROW = 3 * MUL + 4 * MUL
REC_COLS = 64
CH = 8
FILLS = 4
NEXP = 8
FF = 1024
EPS = 1e-5
TILE = 256
TILE_BITS = 8
CHUNK = 3 * D + 2
TILES = (2 * N - NEXP) // TILE + NEXP


def wait(eng, sem, value):
    if isinstance(value, int) and value <= 0:
        return
    eng.wait_ge(sem, value)


def prepare(nc, a, keep, scratch):
    with ExitStack() as ctx:
        def sb(name, shape, dt=F32):
            return ctx.enter_context(nc.sbuf_tensor(name, shape, dt))

        def ps(name, shape, dt=F32):
            return ctx.enter_context(nc.psum_tensor(name, shape, dt))

        def sem(name):
            return ctx.enter_context(nc.semaphore(name))

        rec_all = sb("rec_all", [EP, EC, REC])
        stage = [sb(f"stage{i}", [EP, CH, REC]) for i in range(2)]
        stage_pos = [sb(f"stage_pos{i}", [EP, CH], I32) for i in range(2)]
        a_int = sb("a_int", [EP, EC], I32)
        b_int = sb("b_int", [EP, EC], I32)
        a_f = sb("a_f", [EP, EC])
        grp = sb("grp", [EP, EC])
        zeros_e = sb("zeros_e", [EP, EC])
        rank = sb("rank", [EP, G, EC])
        pos_i = sb("pos_i", [EP, EC], I32)
        small = sb("small", [EP, 5, G])
        cnt_i = sb("cnt_i", [EP, 2, G], I32)
        step_no = sb("step_no", [1, STEPS])
        step_f = sb("step_f", [1, STEPS])
        zero_fill = sb("zero_fill", [128, STEPS * STEP * REC // (FILLS * 128)])
        tri = sb("tri", [EP, EP])
        onesq = sb("onesq", [EP, EP])
        stats = sb("stats", [NG, G, 6])
        mv = sb("mv", [NG, G, 2])
        std = sb("std", [NG, G])
        rstd = sb("rstd", [NG, G])
        eps_t = sb("eps_t", [NG, 1])
        wpre0 = sb("wpre0", [128, MUL])
        wpre1 = sb("wpre1", [128, MUL])
        wnd0 = sb("wnd0", [128, MUL])
        wnd1 = sb("wnd1", [128, MUL])
        wg1 = sb("wg1", [128, 2, 2 * MUL])
        wg2 = sb("wg2", [128, 2, 2 * MUL])
        bpre0 = sb("bpre0", [128, 1])
        bg1 = sb("bg1", [128, 2])
        bg2 = sb("bg2", [128, 2])
        bnd0 = sb("bnd0", [1, MUL])
        ones_row = sb("ones_row", [1, NG])
        ws1ab = sb("ws1ab", [128, 2, 4, HID])
        w2_raw = sb("w2_raw", [128, 4 * MUL])
        xs = sb("xs", [NG, 4, MUL])
        xT = sb("xT", [128, 4, NG])
        sq = sb("sq", [128, 3, NG])
        n1s = sb("n1s", [128, 2, NG])
        n1T = sb("n1T", [128, NG])
        p0T = sb("p0T", [128, NG])
        hT = sb("hT", [128, 2, NG])
        gT = sb("gT", [128, 2, NG])
        xgT = sb("xgT", [128, 3, NG])
        brow = sb("brow", [NG, ROW])
        ps_prefix = ps("ps_prefix", [EP, 2, G])
        ps_xT = ps("ps_xT", [128, 4, NG])
        ps_p0 = ps("ps_p0", [128, NG])
        ps_pre = ps("ps_pre", [NG, 4, MUL])
        ps_g1 = ps("ps_g1", [128, 2, NG])
        ps_g2 = ps("ps_g2", [128, 2, NG])
        ps_nd = ps("ps_nd", [NG, 4, MUL])

        rec_in = [sem(f"rec_in{i}") for i in range(2)]
        ab_in = sem("ab_in")
        x_in = sem("x_in")
        w_in = sem("w_in")
        w4_in = sem("w4_in")
        zeros_set = sem("zeros_set")
        filled = sem("filled")
        consts = sem("consts")
        wide_consts = sem("wide_consts")
        dve_step = sem("dve_step")
        rec_done = sem("rec_done")
        totals = sem("totals")
        prefixed = sem("prefixed")
        pos_done = sem("pos_done")
        stage_seen = sem("stage_seen")
        staged = [sem(f"staged{i}") for i in range(2)]
        scattered = [sem(f"scattered{i}") for i in range(2)]
        var_done = sem("var_done")
        std_done = sem("std_done")
        split_hi = sem("split_hi")
        xs_ready = sem("xs_ready")
        xT_ps = sem("xT_ps")
        xT_ready = sem("xT_ready")
        sq_ready = sem("sq_ready")
        sq_sum = sem("sq_sum")
        n1_sum = sem("n1_sum")
        n1_ready = sem("n1_ready")
        p0_ps = sem("p0_ps")
        p0_ready = sem("p0_ready")
        pre_ps = sem("pre_ps")
        tab_hi = sem("tab_hi")
        tab_done = sem("tab_done")
        g1_ps = sem("g1_ps")
        h_ready = sem("h_ready")
        g2_ps = sem("g2_ps")
        g_ready = sem("g_ready")
        xg_ready = sem("xg_ready")
        nd_ps = sem("nd_ps")
        acc_ready = sem("acc_ready")
        row_pre = sem("row_pre")
        row_ready = sem("row_ready")
        row_out = sem("row_out")
        block = ctx.enter_context(nc.Block())

        WDMA = 16 * 19

        @block.sync
        def _(sp):
            sp.dma_start(a_int[:, :], a["src"].rearrange("(p c) -> p c", p=EP)).then_inc(ab_in, 16)
            sp.dma_start(b_int[:, :], a["dst"].rearrange("(p c) -> p c", p=EP)).then_inc(ab_in, 16)
            records = a["rec"].rearrange("(p c) r -> p c r", p=EP)
            sp.dma_start(rec_all[:, 0:REC_COLS, :], records[:, 0:REC_COLS, :]).then_inc(rec_in[0], 16)
            sp.wait_ge(zeros_set, 1)
            fill = scratch["sorted"].rearrange("(k p f) r -> k p (f r)", k=FILLS, p=128)
            for i in range(FILLS):
                sp.dma_start(fill[i], zero_fill[:, :]).then_inc(filled, 16)
            sp.wait_ge(pos_done, 1)

            def stage_pair(r):
                for i in range(2):
                    wait(sp, scattered[i], r * 16 * CH)
                    col = (2 * r + i) * CH
                    sp.dma_start(stage[i][:, :, :], rec_all[:, bass.ds(col, CH), :]).then_inc(staged[i], 16)
                    sp.dma_start(stage_pos[i][:, :], pos_i[:, bass.ds(col, CH)]).then_inc(staged[i], 16)
            pairs = REC_COLS // (2 * CH)
            sp.wait_ge(rec_done, 2)
            stage_pair(0)
            sp.dma_start(rec_all[:, REC_COLS:EC, :], records[:, REC_COLS:EC, :]).then_inc(rec_in[1], 16)
            stage_pair(1)
            sp.dma_start(keep["x"][:, :, :], a["x"].rearrange("(g p) d -> p g d", p=NG)).then_inc(x_in, 16)
            with sp.Fori(2, pairs) as r:
                stage_pair(r)
            sp.wait_ge(rec_done, 4)
            with sp.Fori(pairs, EC // (2 * CH)) as r:
                stage_pair(r)

        @block.gpsimd
        def _(pool):
            pool.memset(zero_fill[:, :], 0.0).then_inc(zeros_set, 1)
            pool.memset(keep["half"][:, :], 0.5).then_inc(zeros_set, 1)
            pool.memset(keep["ident"][:, :], 0.0).then_inc(wide_consts, 1)
            pool.memset(onesq[:, :], 1.0).then_inc(wide_consts, 1)
            pool.memset(zeros_e[:, :], 0.0).then_inc(wide_consts, 1)
            pool.memset(ones_row[:, :], 1.0).then_inc(wide_consts, 1)
            pool.memset(eps_t[:, :], EPS).then_inc(wide_consts, 1)
            pool.memset(keep["wf1"][:, :, :], 0.0).then_inc(wide_consts, 1)
            pool.memset(keep["ws1c"][:, :, :], 0.0).then_inc(wide_consts, 1)
            pool.memset(ws1ab[:, :, :, :], 0.0).then_inc(wide_consts, 1)
            pool.iota(keep["iota"][:, :], [[1, NG]], base=0, channel_multiplier=0,
                      allow_small_or_imprecise_dtypes=True).then_inc(wide_consts, 1)
            pool.iota(step_no[:, :], [[STEP, STEPS]], base=0, channel_multiplier=0,
                      allow_small_or_imprecise_dtypes=True).then_inc(wide_consts, 1)
            pool.wait_ge(wide_consts, 10)
            pool.affine_select(out=keep["ident"][:, :], in_=keep["ident"][:, :], compare_op=ALU.not_equal,
                               fill=1.0, base=0, pattern=[[-1, 128]], channel_multiplier=1).then_inc(consts, 1)
            pool.affine_select(out=tri[:, :], in_=onesq[:, :], compare_op=ALU.is_ge,
                               fill=0.0, base=-1, pattern=[[1, EP]], channel_multiplier=-1).then_inc(consts, 1)
            pool.wait_ge(filled, 16 * FILLS)

            def scatter_pair(r):
                for i in range(2):
                    pool.wait_ge(staged[i], 32 * (r + 1))
                    pool.sem_inc(stage_seen, 1)
                    for c in range(CH):
                        pool.indirect_dma_start(
                            out=scratch["sorted"], out_offset=bass.IndirectOffsetOnAxis(ap=stage_pos[i][:, c:c + 1], axis=0),
                            in_=stage[i][:, c, :], in_offset=None).then_inc(scattered[i], 16)
            with pool.Fori(0, EC // (2 * CH)) as r:
                scatter_pair(r)
            for i in range(2):
                pool.wait_ge(scattered[i], 8 * EC)

        @block.vector
        def _(dve):
            done = [0]

            def link(ins):
                done[0] += 1
                ins.then_inc(dve_step, 1)
                dve.wait_ge(dve_step, done[0])

            dve.wait_ge(ab_in, 32)
            link(dve.tensor_copy(a_f[:, :], a_int[:, :]))
            link(dve.tensor_scalar(grp[:, :], a_f[:, :], float(NG), None, ALU.is_ge))
            for g in range(2, G):
                link(dve.scalar_tensor_tensor(grp[:, :], a_f[:, :], float(NG * g), grp[:, :], ALU.is_ge, ALU.add))
            dve.wait_ge(wide_consts, 10)
            for g in range(G):
                ins = dve.tensor_scalar(rank[:, g, :], grp[:, :], float(g), None, ALU.is_equal)
            link(ins)
            for g in range(G):
                ins = dve.tensor_tensor_scan(rank[:, g, :], rank[:, g, :], zeros_e[:, :], 0.0, ALU.add, ALU.add)
            link(ins)
            dve.tensor_copy(small[:, 0, :], rank[:, :, EC - 1]).then_inc(totals, 1)
            dve.wait_ge(prefixed, 1)
            link(dve.tensor_scalar(cnt_i[:, 0, :], ps_prefix[:, 1, :], float(STEP - 1), None, ALU.add))
            link(dve.tensor_scalar(cnt_i[:, 1, :], cnt_i[:, 0, :], 8, 8, ALU.logical_shift_right, ALU.logical_shift_left))
            link(dve.tensor_copy(small[:, 1, :], cnt_i[:, 1, :]))
            link(dve.tensor_tensor_scan(small[:, 2, :], small[:, 1, :], zeros_e[:, 0:G], 0.0, ALU.add, ALU.add))
            link(dve.tensor_tensor(small[:, 3, :], small[:, 2, :], small[:, 1, :], ALU.subtract))
            link(dve.scalar_tensor_tensor(small[:, 4, :], small[:, 3, :], -1.0, ps_prefix[:, 0, :], ALU.add, ALU.add))
            for g in range(G):
                ins = dve.tensor_scalar(rank[:, g, :], rank[:, g, :], small[:, 4, g:g + 1], None, ALU.add)
            link(ins)
            for g in range(G):
                ins = dve.scalar_tensor_tensor(rank[:, g, :], grp[:, :], float(g), rank[:, g, :], ALU.is_equal, ALU.mult)
            link(ins)
            link(dve.tensor_tensor(rank[:, 0:5, :], rank[:, 0:5, :], rank[:, 5:10, :], ALU.add))
            link(dve.tensor_tensor(rank[:, 0:2, :], rank[:, 0:2, :], rank[:, 2:4, :], ALU.add))
            link(dve.tensor_tensor(rank[:, 0, :], rank[:, 0, :], rank[:, 1, :], ALU.add))
            dve.tensor_tensor(pos_i[:, :], rank[:, 0, :], rank[:, 4, :], ALU.add).then_inc(pos_done, 1)
            for i, at in enumerate((slice(0, REC_COLS), slice(REC_COLS, EC))):
                dve.wait_ge(rec_in[i], 16)
                dve.scalar_tensor_tensor(rec_all[:, at, A_LOC], grp[:, at], float(-NG), a_f[:, at],
                                         ALU.mult, ALU.add).then_inc(rec_done, 1)
                dve.tensor_copy(rec_all[:, at, B_ID], b_int[:, at]).then_inc(rec_done, 1)
            link(dve.tensor_scalar(step_f[:, :], step_no[:, :], small[0:1, 3, 1:2], None, ALU.is_ge))
            for g in range(2, G):
                link(dve.scalar_tensor_tensor(step_f[:, :], step_no[:, :], small[0:1, 3, g:g + 1], step_f[:, :],
                                              ALU.is_ge, ALU.add))
            link(dve.tensor_copy(keep["step_group"][:, :], step_f[:, :]))
            dve.wait_ge(w4_in, 16 * 4)
            dve.tensor_copy(keep["w2"][:, 0, :], w2_raw[:, :]).then_inc(split_hi, 1)
            dve.wait_ge(split_hi, 1)
            link(dve.tensor_tensor(keep["w2"][:, 1, :], w2_raw[:, :], keep["w2"][:, 0, :].bitcast(F32), ALU.subtract))
            dve.wait_ge(x_in, 16)
            for t in range(G):
                ins = dve.bn_stats(stats[:, t, :], keep["x"][:, t, :])
            link(ins)
            for t in range(G):
                ins = dve.bn_aggr(mv[:, t, :], stats[:, t, :])
            ins.then_inc(var_done, 1)
            dve.wait_ge(std_done, 1)
            link(dve.reciprocal(rstd[:, :], std[:, :]))
            for t in range(G):
                ins = dve.tensor_scalar(keep["acc"][:, t, :], keep["x"][:, t, :], mv[:, t, 0:1], rstd[:, t:t + 1],
                                        ALU.subtract, ALU.mult)
            link(ins)
            link(dve.tensor_tensor(keep["x"][:, :, :], keep["x"][:, :, :], keep["acc"][:, :, :], ALU.add))

            def tile(t):
                xn_t = keep["acc"][:, bass.ds(t, 1), :]
                wait(dve, xT_ps, t)
                dve.tensor_scalar(xs[:, 0:1, :], xn_t[:, :, 0:MUL], 1.0, None, ALU.mult).then_inc(xs_ready, 1)
                dve.tensor_scalar(xs[:, 1:4, :], xn_t[:, :, MUL:D].rearrange("p g (u m) -> p (g m) u", m=3),
                                  1.0, None, ALU.mult).then_inc(xs_ready, 1)
                dve.wait_ge(sq_ready, t + 1)
                dve.tensor_tensor(n1s[:, 0, :], sq[:, 0, :], sq[:, 1, :], ALU.add).then_inc(sq_sum, 1)
                dve.wait_ge(sq_sum, t + 1)
                dve.tensor_tensor(n1s[:, 1, :], n1s[:, 0, :], sq[:, 2, :], ALU.add).then_inc(n1_sum, 1)
                dve.wait_ge(pre_ps, t + 1)
                pre = ps_pre[:, :, :].rearrange("p a b -> p (a b)").unsqueeze(1)
                tab_t = keep["tab"][:, bass.ds(t, 1), :, :]
                dve.tensor_scalar(tab_t[:, :, 0, :], pre, 1.0, None, ALU.mult).then_inc(tab_hi, 1)
                dve.wait_ge(tab_hi, t + 1)
                dve.tensor_tensor(tab_t[:, :, 1, :], pre, tab_t[:, :, 0, :].bitcast(F32), ALU.subtract).then_inc(tab_done, 1)
                dve.wait_ge(g_ready, 2 * t + 2)
                dve.tensor_tensor(xgT[:, :, :], xT[:, 1:4, :], gT[:, 1:2, :].to_broadcast([128, 3, NG]),
                                  ALU.mult).then_inc(xg_ready, 1)
                dve.wait_ge(nd_ps, t + 1)
                dve.tensor_scalar(keep["acc"][:, bass.ds(t, 1), :], ps_nd[:, :, :].rearrange("p a b -> p (a b)").unsqueeze(1),
                                  1.0, None, ALU.mult).then_inc(acc_ready, 1)
            tile(0)
            with dve.Fori(1, G) as t:
                tile(t)

        @block.scalar
        def _(act):
            for dst, src in ((wpre0[:, :], a["L0_gnn_W_pre0"]), (wpre1[:, :], a["L0_gnn_W_pre1"]),
                             (wnd0[:, :], a["L0_gnn_W_nd0"]), (wnd1[:, :], a["L0_gnn_W_nd1"]),
                             (wg1[:, :, :], a["L0_gnn_W_g1"].rearrange("(c p) j -> p c j", p=128)),
                             (wg2[:, :, :], a["L0_gnn_W_g2"].rearrange("(c p) j -> p c j", p=128)),
                             (bpre0[:, :], a["L0_gnn_b_pre0"].rearrange("(p c) -> p c", c=1)),
                             (bg1[:, :], a["bg1"]),
                             (bg2[:, :], a["bg2"]),
                             (bnd0[:, :], a["L0_gnn_b_nd0"].rearrange("(c p) -> c p", c=1))):
                act.dma_start(dst, src).then_inc(w_in, 16)
            w_s1 = a["L0_gnn_W_s1"].rearrange("(c p) k -> c p k", p=MUL)
            act.wait_ge(wide_consts, 10)
            for q in range(2):
                for c in range(2):
                    act.dma_start(ws1ab[:, c, 2 + q, :], w_s1[c]).then_inc(w_in, 16)
                act.dma_start(keep["ws1c"][:, 2 + q, :], w_s1[2]).then_inc(w_in, 16)
                act.dma_start(keep["wf1"][ATTR:RECK, q, :], a["L0_gnn_W_f1"]).then_inc(w_in, 16)
                act.dma_start(w2_raw[32 * q:32 * q + 32, :], a["wf2"]).then_inc(w4_in, 16)
                act.dma_start(w2_raw[64 + 32 * q:96 + 32 * q, :], a["ws2"]).then_inc(w4_in, 16)
            act.wait_ge(var_done, 1)
            act.activation(std[:, :], mv[:, :, 1], ACT.Sqrt, bias=eps_t[:, :]).then_inc(std_done, 1)
            act.wait_ge(w_in, 16 * 18)

            def tile(t):
                act.wait_ge(xT_ps, t + 1)
                wait(act, nd_ps, t)
                act.activation(xT[:, :, :], ps_xT[:, :, :], ACT.Copy).then_inc(xT_ready, 1)
                act.activation(sq[:, :, :], ps_xT[:, 1:4, :], ACT.Square).then_inc(sq_ready, 1)
                act.wait_ge(n1_sum, t + 1)
                act.activation(n1T[:, :], n1s[:, 1, :], ACT.Sqrt, scale=1.0 / 3.0).then_inc(n1_ready, 1)
                act.wait_ge(p0_ps, t + 1)
                act.activation(p0T[:, :], ps_p0[:, :], ACT.Identity, bias=bpre0[:, :]).then_inc(p0_ready, 1)
                act.wait_ge(g1_ps, t + 1)
                for c in range(2):
                    act.activation(hT[:, c, :], ps_g1[:, c, :], ACT.Silu, bias=bg1[:, c:c + 1]).then_inc(h_ready, 1)
                act.wait_ge(tab_done, t + 1)
                wait(act, row_out, 16 * t)
                act.activation(brow[:, 0:3 * MUL], ps_pre[:, 0:3, :].rearrange("p a b -> p (a b)"), ACT.Copy).then_inc(row_pre, 1)
                act.wait_ge(g2_ps, t + 1)
                for c in range(2):
                    act.activation(gT[:, c, :], ps_g2[:, c, :], ACT.Identity, bias=bg2[:, c:c + 1]).then_inc(g_ready, 1)
                act.wait_ge(acc_ready, t + 1)
                act.activation(brow[:, 3 * MUL:ROW], ps_nd[:, :, :].rearrange("p a b -> p (a b)"), ACT.Copy).then_inc(row_ready, 1)
                act.wait_ge(row_ready, t + 1)
                act.wait_ge(row_pre, t + 1)
                act.dma_start(scratch["rows"][bass.ds(t * NG, NG), :], brow[:, :]).then_inc(row_out, 16)
            tile(0)
            with act.Fori(1, G) as t:
                tile(t)
            act.wait_ge(row_out, 16 * G)

        @block.tensor
        def _(pe):
            pe.wait_ge(consts, 2)
            pe.wait_ge(totals, 1)
            pe.matmul(ps_prefix[:, 0, :], tri[:, :], small[:, 0, :], start=True, stop=True)
            pe.matmul(ps_prefix[:, 1, :], onesq[:, :], small[:, 0, :], start=True, stop=True).then_inc(prefixed, 1)
            pe.wait_ge(w_in, 16 * 18)

            def tile(t):
                pe.wait_ge(xs_ready, 2 * t + 2)
                wait(pe, xT_ready, t)
                wait(pe, sq_ready, t)
                for c in range(4):
                    ins = pe.transpose(ps_xT[:, c, :], xs[:, c, :], keep["ident"][0:NG, 0:NG])
                ins.then_inc(xT_ps, 1)
                pe.wait_ge(xT_ready, t + 1)
                wait(pe, p0_ready, t)
                pe.matmul(ps_p0[:, :], wpre0[:, :], xT[:, 0, :], start=True, stop=True).then_inc(p0_ps, 1)
                wait(pe, tab_done, t)
                wait(pe, row_pre, t)
                for m in range(3):
                    pe.matmul(ps_pre[:, m, :], xT[:, 1 + m, :], wpre1[:, :], start=True, stop=True)
                pe.wait_ge(p0_ready, t + 1)
                for c in range(2):
                    ins = pe.matmul(ps_pre[:, 3, :], p0T[:, :], ws1ab[:, c, :, :].rearrange("p q k -> p (q k)"),
                                    start=(c == 0), stop=(c == 1))
                ins.then_inc(pre_ps, 1)
                pe.wait_ge(n1_ready, t + 1)
                for c in range(2):
                    pe.matmul(ps_g1[:, c, :], wg1[:, 0, c * 128:(c + 1) * 128], xT[:, 0, :], start=True, stop=False)
                    ins = pe.matmul(ps_g1[:, c, :], wg1[:, 1, c * 128:(c + 1) * 128], n1T[:, :], start=False, stop=True)
                ins.then_inc(g1_ps, 1)
                pe.wait_ge(h_ready, 2 * t + 2)
                for c in range(2):
                    for k in range(2):
                        ins = pe.matmul(ps_g2[:, c, :], wg2[:, k, c * 128:(c + 1) * 128], hT[:, k, :],
                                        start=(k == 0), stop=(k == 1))
                ins.then_inc(g2_ps, 1)
                pe.wait_ge(g_ready, 2 * t + 2)
                wait(pe, acc_ready, t)
                wait(pe, row_ready, t)
                pe.matmul(ps_nd[:, 0, :], gT[:, 0, :], wnd0[:, :], start=True, stop=False)
                pe.matmul(ps_nd[:, 0, :], ones_row[:, :], bnd0[:, :], start=False, stop=True)
                pe.wait_ge(xg_ready, t + 1)
                for m in range(3):
                    ins = pe.matmul(ps_nd[:, 1 + m, :], xgT[:, m, :], wnd1[:, :], start=True, stop=True)
                ins.then_inc(nd_ps, 1)
            tile(0)
            with pe.Fori(1, G) as t:
                tile(t)


def edges(nc, keep, scratch):
    U = 5
    BODY = 2 * U
    BODIES = (STEPS - 4 - U) // BODY
    with ExitStack() as ctx:
        def sb(name, shape, dt=F32):
            return ctx.enter_context(nc.sbuf_tensor(name, shape, dt))

        def ps(name, shape, dt=F32):
            return ctx.enter_context(nc.psum_tensor(name, shape, dt))

        def sem(name):
            return ctx.enter_context(nc.semaphore(name))

        rec = [sb(f"rec{k}", [128, 2, REC]) for k in range(U)]
        rows = [sb(f"rows{k}", [128, 2, ROW]) for k in range(U)]
        bidx = [sb(f"bidx{k}", [128, 2], I32) for k in range(U)]
        shs = [sb(f"shs{k}", [128, 2, 4]) for k in range(U)]
        sht = [sb(f"sht{k}", [128, 2, 3]) for k in range(U)]
        oh = [sb(f"oh{k}", [128, 2, NG]) for k in range(U)]
        q0s = [sb(f"q0s{k}", [NG, 2, MUL], F32R) for k in range(U)]
        recT = [sb(f"recT{k}", [RECK, 2, 128]) for k in range(U)]
        ohT = [sb(f"ohT{k}", [NG, 2, 128], F32R) for k in range(U)]
        z = [sb(f"z{k}", [128, 2, 128], F32R) for k in range(U)]
        prod = sb("prod", [128, 2, 3 * MUL])
        ipT = sb("ipT", [128, 2, 128])
        soft = sb("soft", [128, 256])
        ssp = sb("ssp", [128, 256])
        zc = sb("zc", [128, 256], F32R)
        fs = sb("fs", [128, 2, 4 * MUL])
        w = sb("w", [128, 2, 4 * MUL])
        u = sb("u", [128, 2, 2, MUL])
        dot = sb("dot", [128, 2, 3, MUL])
        v3 = sb("v3", [128, 2, 3, MUL])
        feat = sb("feat", [128, 2, 4 * MUL])
        off = sb("off", [128, 2, NG])
        sqrt3 = sb("inv_sqrt3", [128, 3])
        one4 = sb("one4", [128, 4])
        is_lo = sb("is_lo", [128, 1])
        sign = sb("sign", [128, 1])
        ps_tr = ps("ps_tr", [128, 4, 128])
        ps_a = [ps(f"ps_a{t}", [128, 3 * MUL]) for t in range(2)]
        ps_ip = ps("ps_ip", [128, 128])
        ps_hid = ps("ps_hid", [128, 256])
        ps_f = ps("ps_f", [128, 4 * MUL])
        ps_s = ps("ps_s", [128, 4 * MUL])
        ps_sum = ps("ps_sum", [NG, 4 * MUL])

        rec_landed = [sem(f"rec_landed{k}") for k in range(U)]
        rows_landed = [[sem(f"rows_landed{k}_{t}") for t in range(2)] for k in range(U)]
        names = ("const_set rows_set bidx_ready sh_ready oh_ready q0_ready v3_ready z_ready tr_done recT_ready ohT_ready "
                 "a_ready prod_ready ip_ps ip_ready hid_done abs_ready exp_ready ln_ready ssp_ready zc_ready f_ps "
                 "fs_ready s_ps w_ready u_ready x0s_ready dot1_ready dot2_ready w4_ready out1_done feat0_ready off_ready "
                 "tile_summed acc_done")
        S = {n: sem(n) for n in names.split()}
        block = ctx.enter_context(nc.Block())

        def has(s):
            return not isinstance(s, int) or 0 <= s < STEPS

        def steps(eng, body):
            for s in range(U):
                body(s, s, 0)
            with eng.Fori(0, BODIES) as r:
                for i in range(U, U + BODY):
                    body(r * BODY + i, i % U, r * 2 + i // U)
            for s in range(U + BODIES * BODY, STEPS):
                body(s, s % U, s // U)

        def ahead(k, rnd, n):
            return (k + n) % U, rnd + (k + n) // U

        @block.sync
        def _(sp):
            def load(s, k, rnd):
                wait(sp, S["tr_done"], s - U + 1)
                sp.dma_start(rec[k][:, :, :],
                             scratch["sorted"][bass.ds(s * STEP, STEP), :].rearrange("(t p) r -> p t r", p=128)
                             ).then_inc(rec_landed[k], 16)
            steps(sp, load)

        @block.gpsimd
        def _(pool):
            pool.memset(sqrt3[:, :], 3.0 ** -0.5).then_inc(S["const_set"], 1)
            pool.memset(one4[:, :], 1.0).then_inc(S["const_set"], 1)
            pool.wait_ge(S["const_set"], 2)

            def first(s, k, rnd):
                pool.wait_ge(rec_landed[k], 16 * (rnd + 1))
                wait(pool, S["tile_summed"], 2 * (s - U + 1))
                pool.tensor_tensor(shs[k][:, :, :], rec[k][:, :, SH:SH + 4],
                                   one4[:, :].unsqueeze(1).to_broadcast([128, 2, 4]), ALU.mult).then_inc(S["sh_ready"], 1)
                pool.tensor_copy(bidx[k][:, :], rec[k][:, :, B_ID]).then_inc(S["bidx_ready"], 1)
                pool.wait_ge(S["bidx_ready"], s + 1)
                pool.tensor_tensor(sht[k][:, :, :], rec[k][:, :, SH + 1:SH + 4],
                                   sqrt3[:, :].unsqueeze(1).to_broadcast([128, 2, 3]), ALU.mult).then_inc(S["sh_ready"], 1)
                gather(k, 0)

            def gather(k, t):
                pool.indirect_dma_start(
                    out=rows[k][:, t, :], out_offset=None, in_=scratch["rows"],
                    in_offset=bass.IndirectOffsetOnAxis(ap=bidx[k][:, t:t + 1], axis=0)
                ).then_inc(rows_landed[k][t], 16)

            def scalars(s, t):
                n = 2 * s + t
                pool.wait_ge(S["dot2_ready"], n + 1)
                pool.tensor_tensor(dot[:, t, 0, :], dot[:, t, 2, :], w[:, t, 3 * MUL:4 * MUL],
                                   ALU.mult).then_inc(S["w4_ready"], 1)
                pool.wait_ge(S["w4_ready"], n + 1)
                wait(pool, S["tile_summed"], n - 1)
                pool.tensor_tensor(feat[:, t, 0:MUL], u[:, t, 0, :], dot[:, t, 0, :], ALU.add
                                   ).then_inc(S["feat0_ready"], 1)

            def second(k):
                gather(k, 1)

            def vectors(s, k, t):
                pool.wait_ge(S["w_ready"], 2 * s + t + 1)
                wait(pool, S["out1_done"], 3 * (2 * s + t - 1))
                pool.tensor_tensor(v3[:, t, :, :], rows[k][:, t, 4 * MUL:ROW].rearrange("p (m u) -> p m u", m=3),
                                   w[:, t, MUL:2 * MUL].unsqueeze(1).to_broadcast([128, 3, MUL]),
                                   ALU.mult).then_inc(S["v3_ready"], 1)

            def body(s, k, rnd):
                vectors(s, k, 0)
                if has(s + 4):
                    first(s + 4, *ahead(k, rnd, 4))
                scalars(s, 0)
                vectors(s, k, 1)
                if has(s + 4):
                    second(ahead(k, rnd, 4)[0])
                scalars(s, 1)
            for s in range(4):
                first(s, s, 0)
                second(s)
            steps(pool, body)

        @block.vector
        def _(dve):
            for q in range(4):
                lo = q % 2 == 0
                dve.memset(is_lo[32 * q:32 * q + 32, :], 1.0 if lo else 0.0).then_inc(S["rows_set"], 1)
                dve.memset(sign[32 * q:32 * q + 32, :], -1.0 if lo else 1.0).then_inc(S["rows_set"], 1)
            dve.wait_ge(S["rows_set"], 8)

            def products(s, k, rnd, t):
                dve.wait_ge(rows_landed[k][t], 16 * (rnd + 1))
                dve.wait_ge(S["a_ready"], 2 * s + t + 1)
                wait(dve, S["ip_ps"], 2 * s + t - 1)
                dve.tensor_tensor(prod[:, t, :], ps_a[t][:, :], rows[k][:, t, 0:3 * MUL],
                                  ALU.mult).then_inc(S["prod_ready"], 1)

            def softplus(s):
                dve.wait_ge(S["ln_ready"], s + 1)
                wait(dve, S["z_ready"], s)
                dve.scalar_tensor_tensor(ssp[:, :], ps_hid[:, :], 0.0, soft[:, :], ALU.max, ALU.add
                                         ).then_inc(S["ssp_ready"], 1)

            def split(s, k):
                dve.wait_ge(S["zc_ready"], s + 1)
                wait(dve, S["s_ps"], 2 * (s - U + 1))
                dve.scalar_tensor_tensor(z[k][:, :, :].rearrange("p a b -> p (a b)"), ssp[:, :], is_lo[:, :],
                                         zc[:, :].bitcast(F32), ALU.mult, ALU.add).then_inc(S["z_ready"], 1)

            def head(s, k, t):
                n = 2 * s + t
                x0 = rows[k][:, t, 3 * MUL:4 * MUL]
                x1 = rows[k][:, t, 4 * MUL:ROW].rearrange("p (m u) -> p m u", m=3)
                dve.wait_ge(S["fs_ready"], 2 * n + 2)
                dve.wait_ge(S["s_ps"], n + 1)
                wait(dve, S["feat0_ready"], n - 1)
                dve.tensor_tensor(w[:, t, :], ps_s[:, :], fs[:, t, :], ALU.mult).then_inc(S["w_ready"], 1)
                dve.wait_ge(S["x0s_ready"], n + 1)
                dve.scalar_tensor_tensor(dot[:, t, 1, :], x1[:, 1, :], sht[k][:, t, 1:2], dot[:, t, 0, :],
                                         ALU.mult, ALU.add).then_inc(S["dot1_ready"], 1)
                dve.wait_ge(S["w_ready"], n + 1)
                wv = w[:, t, :].rearrange("p (a b u) -> p a b u", a=2, b=2)[:, :, 0, :]
                dve.tensor_tensor(u[:, t, :, :], wv, x0.unsqueeze(1).to_broadcast([128, 2, MUL]),
                                  ALU.mult).then_inc(S["u_ready"], 1)
                dve.wait_ge(S["dot1_ready"], n + 1)
                dve.scalar_tensor_tensor(dot[:, t, 2, :], x1[:, 2, :], sht[k][:, t, 2:3], dot[:, t, 1, :],
                                         ALU.mult, ALU.add).then_inc(S["dot2_ready"], 1)

            def tail(s, k, t):
                n = 2 * s + t
                wait(dve, S["tile_summed"], n - 1)
                dve.wait_ge(S["v3_ready"], n + 1)
                dve.wait_ge(S["u_ready"], n + 1)
                for m in range(3):
                    dve.scalar_tensor_tensor(feat[:, t, (1 + m) * MUL:(2 + m) * MUL], u[:, t, 1, :],
                                             shs[k][:, t, 1 + m:2 + m], v3[:, t, m, :], ALU.mult, ALU.add
                                             ).then_inc(S["out1_done"], 1)

            def total(s, g):
                dve.wait_ge(S["tile_summed"], 2 * s + 2)
                wait(dve, S["acc_done"], s)
                dve.tensor_tensor(keep["acc"][:, bass.ds(g, 1), :], ps_sum[:, :].unsqueeze(1),
                                  keep["acc"][:, bass.ds(g, 1), :], ALU.add).then_inc(S["acc_done"], 1)

            def group(s):
                return dve.value_load(keep["step_group"][0:1, bass.ds(s, 1)], min_val=0, max_val=G - 1)

            def body(s, k, rnd):
                g = group(s - 1) if has(s - 1) else None
                head(s, k, 0)
                if has(s + 1):
                    softplus(s + 1)
                tail(s, k, 0)
                if has(s - 1):
                    total(s - 1, g)
                if has(s + 1):
                    split(s + 1, ahead(k, rnd, 1)[0])
                head(s, k, 1)
                if has(s + 3):
                    products(s + 3, *ahead(k, rnd, 3), 0)
                tail(s, k, 1)
                if has(s + 3):
                    products(s + 3, *ahead(k, rnd, 3), 1)
            for t in range(2):
                products(0, 0, 0, t)
            softplus(0)
            split(0, 0)
            for s in range(1, 3):
                for t in range(2):
                    products(s, s, 0, t)
            steps(dve, body)
            total(STEPS - 1, group(STEPS - 1))

        @block.scalar
        def _(act):
            act.preload_act_table_set("natural_log_exp_and_others")
            act.wait_ge(S["rows_set"], 8)

            def group(s):
                return act.value_load(keep["step_group"][0:1, bass.ds(s, 1)], min_val=0, max_val=G - 1)

            def transposed(s, k, g):
                act.wait_ge(S["tr_done"], s + 1)
                wait(act, S["hid_done"], s - U + 1)
                act.activation(ohT[k][:, :, :], ps_tr[0:NG, 2:4, :], ACT.Copy).then_inc(S["ohT_ready"], 1)
                act.activation(recT[k][:, :, :], ps_tr[0:RECK, 0:2, :], ACT.Copy).then_inc(S["recT_ready"], 1)
                act.activation(q0s[k][:, :, :].unsqueeze(1),
                               keep["tab"][:, bass.ds(g, 1), :, 3 * MUL:4 * MUL].bitcast(F32), ACT.Copy
                               ).then_inc(S["q0_ready"], 1)

            def onehots(s, k, rnd):
                act.wait_ge(rec_landed[k], 16 * (rnd + 1))
                wait(act, S["oh_ready"], s)
                for t in range(2):
                    act.activation(off[:, t, :], keep["iota"][:, :], ACT.Abs, scale=-1.0,
                                   bias=rec[k][:, t, A_LOC:A_LOC + 1]).then_inc(S["off_ready"], 1)
                act.wait_ge(S["off_ready"], 2 * s + 2)
                wait(act, S["tile_summed"], 2 * (s - U + 1))
                act.activation(oh[k][:, :, :], off[:, :, :], ACT.Relu, scale=-1.0, bias=1.0).then_inc(S["oh_ready"], 1)

            def inner(s, t):
                act.wait_ge(S["ip_ps"], 2 * s + t + 1)
                wait(act, S["hid_done"], s)
                act.activation(ipT[:, t, :], ps_ip[:, :], ACT.Copy, scale=1.0 / 3.0).then_inc(S["ip_ready"], 1)

            def softplus(s):
                act.wait_ge(S["hid_done"], s + 1)
                wait(act, S["ssp_ready"], s)
                act.activation(soft[:, :], ps_hid[:, :], ACT.Abs).then_inc(S["abs_ready"], 1)
                act.wait_ge(S["abs_ready"], s + 1)
                act.activation(soft[:, :], soft[:, :], ACT.Exp, scale=-1.0).then_inc(S["exp_ready"], 1)
                act.wait_ge(S["exp_ready"], s + 1)
                act.activation(soft[:, :], soft[:, :], ACT.Ln, bias=keep["half"][:, :], scale=0.5).then_inc(S["ln_ready"], 1)

            def rounded(s):
                act.wait_ge(S["ssp_ready"], s + 1)
                wait(act, S["z_ready"], s)
                act.activation(zc[:, :], ssp[:, :], ACT.Copy, scale=sign[:, :]).then_inc(S["zc_ready"], 1)

            def filters(s, k, rnd, t):
                n = 2 * s + t
                act.wait_ge(S["sh_ready"], 2 * s + 2)
                wait(act, S["feat0_ready"], n - 1)
                act.wait_ge(S["f_ps"], n + 1)
                act.activation(fs[:, t, 0:2 * MUL], ps_f[:, 0:2 * MUL], ACT.Copy,
                               scale=shs[k][:, t, 0:1]).then_inc(S["fs_ready"], 1)
                act.activation(fs[:, t, 2 * MUL:4 * MUL], ps_f[:, 2 * MUL:4 * MUL], ACT.Copy).then_inc(S["fs_ready"], 1)
                act.wait_ge(rows_landed[k][t], 16 * (rnd + 1))
                act.activation(dot[:, t, 0, :], rows[k][:, t, 4 * MUL:5 * MUL], ACT.Copy,
                               scale=sht[k][:, t, 0:1]).then_inc(S["x0s_ready"], 1)

            def body(s, k, rnd):
                g = group(s + 3) if has(s + 3) else None
                filters(s, k, rnd, 0)
                if has(s + 1):
                    softplus(s + 1)
                if has(s + 2):
                    inner(s + 2, 0)
                if has(s + 1):
                    rounded(s + 1)
                filters(s, k, rnd, 1)
                if has(s + 2):
                    inner(s + 2, 1)
                if has(s + 3):
                    transposed(s + 3, ahead(k, rnd, 3)[0], g)
                if has(s + 4):
                    onehots(s + 4, *ahead(k, rnd, 4))
            for s in range(4):
                onehots(s, s, 0)
            for s in range(2):
                transposed(s, s, group(s))
                inner(s, 0)
                inner(s, 1)
                if s == 0:
                    softplus(0)
                    rounded(0)
            transposed(2, 2, group(2))
            steps(act, body)

        @block.tensor
        def _(pe):
            def transposes(s, k, rnd):
                pe.wait_ge(rec_landed[k], 16 * (rnd + 1))
                pe.wait_ge(S["sh_ready"], 2 * s + 2)
                pe.wait_ge(S["oh_ready"], s + 1)
                wait(pe, S["recT_ready"], s)
                for t in range(2):
                    pe.transpose(ps_tr[0:NG, 2 + t, :], oh[k][:, t, :], keep["ident"][:, :])
                for t in range(2):
                    ins = pe.transpose(ps_tr[0:RECK, t, :], rec[k][:, t, 0:RECK], keep["ident"][:, :])
                ins.then_inc(S["tr_done"], 1)

            def group(s):
                return pe.value_load(keep["step_group"][0:1, bass.ds(s, 1)], min_val=0, max_val=G - 1)

            def gathers(s, k, g):
                pe.wait_ge(S["ohT_ready"], s + 1)
                for t in range(2):
                    wait(pe, S["prod_ready"], 2 * s + t - 1)
                    for i in range(2):
                        ins = pe.matmul(ps_a[t][:, :].unsqueeze(1).unsqueeze(1), ohT[k][:, t, :],
                                        keep["tab"][:, bass.ds(g, 1), i:i + 1, 0:3 * MUL], start=(i == 0), stop=(i == 1))
                    ins.then_inc(S["a_ready"], 1)

            def inner(s, t):
                pe.wait_ge(S["prod_ready"], 2 * s + t + 1)
                wait(pe, S["ip_ready"], 2 * s + t)
                for m in range(3):
                    ins = pe.matmul(ps_ip[:, :], prod[:, t, m * MUL:(m + 1) * MUL], keep["ident"][:, :],
                                    start=(m == 0), stop=(m == 2))
                ins.then_inc(S["ip_ps"], 1)

            def hidden(s, k):
                pe.wait_ge(S["recT_ready"], s + 1)
                wait(pe, S["ssp_ready"], s)
                pe.matmul(ps_hid[:, :], keep["wf1"][:, :, :].rearrange("p q k -> p (q k)"),
                          recT[k][:, :, :].rearrange("p a b -> p (a b)"), start=True, stop=False)
                pe.wait_ge(S["q0_ready"], s + 1)
                for i in range(2):
                    pe.matmul(ps_hid[:, :], q0s[k][:, i, :], ohT[k][:, :, :].rearrange("p a b -> p (a b)"),
                              start=False, stop=False)
                pe.wait_ge(S["ip_ready"], 2 * s + 2)
                pe.matmul(ps_hid[:, :], keep["ws1c"][:, :, :].rearrange("p q k -> p (q k)"),
                          ipT[:, :, :].rearrange("p a b -> p (a b)"), start=False, stop=True).then_inc(S["hid_done"], 1)

            def weights(s, k, t):
                n = 2 * s + t
                pe.wait_ge(S["z_ready"], s + 1)
                wait(pe, S["fs_ready"], 2 * n)
                wait(pe, S["w_ready"], n)
                for i in range(2):
                    f = pe.matmul(ps_f[:, :], z[k][0:64, t, :], keep["w2"][0:64, i, :], start=(i == 0), stop=(i == 1))
                    if i == 1:
                        f.then_inc(S["f_ps"], 1)
                    g = pe.matmul(ps_s[:, :], z[k][64:128, t, :], keep["w2"][64:128, i, :], start=(i == 0), stop=(i == 1))
                g.then_inc(S["s_ps"], 1)

            def sums(s, k, t):
                if t == 0:
                    wait(pe, S["acc_done"], s)
                pe.wait_ge(S["feat0_ready"], 2 * s + t + 1)
                pe.wait_ge(S["out1_done"], 3 * (2 * s + t + 1))
                pe.matmul(ps_sum[:, :], oh[k][:, t, :], feat[:, t, :], start=(t == 0), stop=(t == 1)
                          ).then_inc(S["tile_summed"], 1)

            def body(s, k, rnd):
                g = group(s + 3) if has(s + 3) else None
                if has(s + 2):
                    inner(s + 2, 0)
                if has(s - 1):
                    sums(s - 1, (k - 1) % U, 1)
                weights(s, k, 1)
                if has(s + 2):
                    inner(s + 2, 1)
                if has(s + 3):
                    transposes(s + 3, *ahead(k, rnd, 3))
                if has(s + 2):
                    hidden(s + 2, ahead(k, rnd, 2)[0])
                if has(s + 3):
                    gathers(s + 3, ahead(k, rnd, 3)[0], g)
                if has(s + 1):
                    weights(s + 1, ahead(k, rnd, 1)[0], 0)
                sums(s, k, 0)
            for s in range(2):
                transposes(s, s, 0)
                gathers(s, s, group(s))
                inner(s, 0)
                inner(s, 1)
                hidden(s, s)
            transposes(2, 2, 0)
            gathers(2, 2, group(2))
            weights(0, 0, 0)
            steps(pe, body)
            sums(STEPS - 1, (STEPS - 1) % U, 1)


def ffn(nc, a, keep, scratch, out):
    with ExitStack() as ctx:
        def sb(name, shape, dt=F32):
            return ctx.enter_context(nc.sbuf_tensor(name, shape, dt))
        plan = {"weight": sb("weight", [NG, 2, G]),
                "slot": sb("slot", [NG, 2, G], I32),
                "tile_expert": sb("tile_expert", [1, TILES], I32)}
        route(nc, a, keep, scratch, plan)
        experts(nc, a, keep, scratch, plan, out)


def route(nc, a, keep, scratch, plan):
    with ExitStack() as ctx:
        def sb(name, shape, dt=F32):
            return ctx.enter_context(nc.sbuf_tensor(name, shape, dt))

        def ps(name, shape, dt=F32):
            return ctx.enter_context(nc.psum_tensor(name, shape, dt))

        wo0 = sb("wo0", [128, MUL])
        wo1 = sb("wo1", [128, MUL])
        bo0 = sb("bo0", [1, MUL])
        ones_row = sb("ones_row2", [1, NG])
        rw = sb("rw_s", [128, 4, NEXP])
        rb = sb("rb_s", [1, NEXP])
        eps_t = sb("eps_t2", [NG, 1])
        tri = sb("tri2", [NG, NG])
        onesq = sb("onesq2", [NG, NG])
        tile_no = sb("tile_no", [1, TILES])
        tile_f = sb("tile_f", [1, TILES])
        s1 = [sb(f"s1_{k}", [NG, D]) for k in range(2)]
        accT = [sb(f"accT{k}", [128, 4, NG]) for k in range(2)]
        x3 = sb("x3", [NG, G, D])
        stats = sb("stats2", [NG, G, 6])
        mv = sb("mv2", [NG, G, 2])
        mean = sb("mean2", [NG, G])
        std = sb("std2", [NG, G])
        rstd = sb("rstd2", [NG, G])
        x3s = [sb(f"x3s{k}", [NG, D]) for k in range(2)]
        x3Ts = [sb(f"x3Ts{k}", [128, 4, NG]) for k in range(2)]
        logit = sb("logit", [NG, G, NEXP])
        top = sb("top", [NG, G, 8])
        topi = sb("topi", [NG, G, 8], mybir.dt.uint32)
        choice = sb("choice", [NG, 2, G])
        gap = sb("gap", [NG, 3, G])
        hit = sb("hit", [NG, NEXP, 2 * G])
        rank = sb("rank2", [NG, NEXP, 2 * G])
        small = sb("small2", [NG, 5, NEXP])
        zeros = sb("zeros2", [NG, 2 * G])
        zero_slots = sb("zero_slots", [128, TILE * D // 128])
        cnt_i = sb("cnt_i2", [NG, 2, NEXP], I32)
        pos = sb("pos2", [NG, 2 * G])
        ps_T = [ps(f"ps_T{k}", [128, 4, NG]) for k in range(2)]
        ps_o = [ps(f"ps_o{k}", [NG, 4, MUL]) for k in range(2)]
        ps_l = [ps(f"ps_l{k}", [NG, NEXP]) for k in range(2)]
        ps_cnt = ps("ps_cnt", [NG, 2, NEXP])
        names = ("params_in zeros_set2 filled2 set2 tri_set dve2_step s1_ready accT_ps accT_ready o_ps x2_ready var2 std2_done x3s_ready "
                 "x3_done x3T_ps x3T_ready l_ps l_ready gap_ready exp2_ready totals2 prefixed2 slots_ready sent")
        S = {n: ctx.enter_context(nc.semaphore(n)) for n in names.split()}
        block = ctx.enter_context(nc.Block())

        def has(t):
            return not isinstance(t, int) or t < G

        def groups(eng, body):
            for t in range(2):
                body(t, t)
            with eng.Fori(1, G // 2 - 1) as r:
                for k in range(2):
                    body(r * 2 + k, k)
            for t in range(G - 2, G):
                body(t, t % 2)

        @block.sync
        def _(sp):
            for dst, src in ((wo0[:, :], a["L0_gnn_W_o0"]), (wo1[:, :], a["L0_gnn_W_o1"]),
                             (bo0[:, :], a["L0_gnn_b_o0"].rearrange("(c p) -> c p", c=1)),
                             (rw[:, :, :], a["rw"].rearrange("(c p) e -> p c e", p=128)),
                             (rb[:, :], a["L0_ffn_router_b"].rearrange("(c p) -> c p", c=1))):
                sp.dma_start(dst, src).then_inc(S["params_in"], 16)
            sp.wait_ge(S["zeros_set2"], 1)
            slots = scratch["x_slots"].rearrange("(k p f) d -> k p (f d)", p=128, k=TILES)
            for i in range(TILES):
                sp.dma_start(slots[i], zero_slots[:, :]).then_inc(S["filled2"], 16)

        @block.gpsimd
        def _(pool):
            pool.memset(zero_slots[:, :], 0.0).then_inc(S["zeros_set2"], 1)
            pool.memset(ones_row[:, :], 1.0).then_inc(S["set2"], 1)
            pool.memset(eps_t[:, :], EPS).then_inc(S["set2"], 1)
            pool.memset(onesq[:, :], 1.0).then_inc(S["set2"], 1)
            pool.memset(zeros[:, :], 0.0).then_inc(S["set2"], 1)
            pool.iota(tile_no[:, :], [[TILE, TILES]], base=0, channel_multiplier=0,
                      allow_small_or_imprecise_dtypes=True).then_inc(S["set2"], 1)
            pool.wait_ge(S["set2"], 5)
            pool.affine_select(out=tri[:, :], in_=onesq[:, :], compare_op=ALU.is_ge,
                               fill=0.0, base=-1, pattern=[[1, NG]], channel_multiplier=-1).then_inc(S["tri_set"], 1)
            pool.wait_ge(S["filled2"], 16 * TILES)
            pool.wait_ge(S["x3_done"], G)
            pool.wait_ge(S["slots_ready"], 1)
            for i in range(2):
                for t in range(G):
                    pool.indirect_dma_start(
                        out=scratch["x_slots"], out_offset=bass.IndirectOffsetOnAxis(ap=plan["slot"][:, i, t:t + 1], axis=0),
                        in_=x3[:, t, :], in_offset=None).then_inc(S["sent"], 16)
            pool.wait_ge(S["sent"], 16 * 2 * G)

        @block.vector
        def _(dve):
            done = [0]

            def link(ins):
                done[0] += 1
                ins.then_inc(S["dve2_step"], 1)
                dve.wait_ge(S["dve2_step"], done[0])

            def sums(t, k):
                wait(dve, S["accT_ps"], t - 1)
                dve.tensor_scalar(s1[k][:, :].unsqueeze(1), keep["acc"][:, bass.ds(t, 1), :], 1.0, None, ALU.mult
                                  ).then_inc(S["s1_ready"], 1)

            def linear(t, k):
                wait(dve, S["x2_ready"], 2 * t)
                if has(t + 2):
                    sums(t + 2, k)
                if not isinstance(t, int) or t > 0:
                    dve.bn_stats(stats[:, bass.ds(t - 1, 1), :].rearrange("p g s -> p (g s)"),
                                 keep["x"][:, bass.ds(t - 1, 1), :].rearrange("p g d -> p (g d)"))
                x_t = keep["x"][:, bass.ds(t, 1), :]
                dve.wait_ge(S["o_ps"], t + 1)
                dve.tensor_tensor(x_t[:, :, 0:MUL], ps_o[k][:, 0:1, :], x_t[:, :, 0:MUL], ALU.add).then_inc(S["x2_ready"], 1)
                x_v = x_t[:, :, MUL:D].rearrange("p g (u m) -> p (g m) u", m=3)
                dve.tensor_tensor(x_v, ps_o[k][:, 1:4, :], x_v, ALU.add).then_inc(S["x2_ready"], 1)
            sums(0, 0)
            sums(1, 1)
            groups(dve, linear)
            dve.wait_ge(S["x2_ready"], 2 * G)
            link(dve.bn_stats(stats[:, G - 1, :], keep["x"][:, G - 1, :]))
            for t in range(G):
                ins = dve.bn_aggr(mv[:, t, :], stats[:, t, :])
            ins.then_inc(S["var2"], 1)
            dve.wait_ge(S["var2"], 1)
            link(dve.tensor_copy(mean[:, :], mv[:, :, 0]))
            dve.wait_ge(S["std2_done"], 1)
            link(dve.reciprocal(rstd[:, :], std[:, :]))

            def normed(t, k):
                wait(dve, S["x3T_ps"], t - 1)
                wait(dve, S["x3_done"], t - 1)
                dve.tensor_scalar(x3s[k][:, :].unsqueeze(1), keep["x"][:, bass.ds(t, 1), :], mean[:, bass.ds(t, 1)],
                                  rstd[:, bass.ds(t, 1)], ALU.subtract, ALU.mult).then_inc(S["x3s_ready"], 1)

            def router(t, k):
                dve.wait_ge(S["x3s_ready"], t + 1)
                dve.tensor_scalar(x3[:, bass.ds(t, 1), :], x3s[k][:, :].unsqueeze(1), 1.0, None, ALU.mult
                                  ).then_inc(S["x3_done"], 1)
                if has(t + 2):
                    normed(t + 2, k)
                dve.wait_ge(S["l_ps"], t + 1)
                dve.tensor_scalar(logit[:, bass.ds(t, 1), :], ps_l[k][:, :].unsqueeze(1), 1.0, None, ALU.mult
                                  ).then_inc(S["l_ready"], 1)
            normed(0, 0)
            normed(1, 1)
            groups(dve, router)
            dve.wait_ge(S["l_ready"], G)
            for t in range(G):
                ins = dve.max(top[:, t, :], logit[:, t, :])
            link(ins)
            dve.tensor_tensor(gap[:, 0, :], top[:, :, 1], top[:, :, 0], ALU.subtract).then_inc(S["gap_ready"], 1)
            for t in range(G):
                ins = dve.max_index(topi[:, t, :], top[:, t, :], logit[:, t, :])
            link(ins)
            link(dve.tensor_copy(choice[:, :, :], topi[:, :, 0:2].rearrange("p g i -> p i g")))
            dve.wait_ge(S["set2"], 5)
            chosen = choice[:, :, :].rearrange("p i g -> p (i g)")
            for e in range(NEXP):
                ins = dve.tensor_scalar(hit[:, e, :], chosen, float(e), None, ALU.is_equal)
            link(ins)
            for e in range(NEXP):
                ins = dve.tensor_tensor_scan(rank[:, e, :], hit[:, e, :], zeros[:, :], 0.0, ALU.add, ALU.add)
            link(ins)
            dve.tensor_copy(small[:, 0, :], rank[:, :, 2 * G - 1]).then_inc(S["totals2"], 1)
            dve.wait_ge(S["exp2_ready"], 1)
            link(dve.tensor_scalar(gap[:, 2, :], gap[:, 1, :], 1.0, None, ALU.add))
            link(dve.reciprocal(plan["weight"][:, 0, :], gap[:, 2, :]))
            link(dve.tensor_tensor(plan["weight"][:, 1, :], gap[:, 1, :], plan["weight"][:, 0, :], ALU.mult))
            dve.wait_ge(S["prefixed2"], 1)
            link(dve.tensor_scalar(cnt_i[:, 0, :], ps_cnt[:, 1, :], float(TILE - 1), None, ALU.add))
            link(dve.tensor_scalar(cnt_i[:, 1, :], cnt_i[:, 0, :], TILE_BITS, TILE_BITS,
                                   ALU.logical_shift_right, ALU.logical_shift_left))
            link(dve.tensor_copy(small[:, 1, :], cnt_i[:, 1, :]))
            link(dve.tensor_tensor_scan(small[:, 2, :], small[:, 1, :], zeros[:, 0:NEXP], 0.0, ALU.add, ALU.add))
            link(dve.tensor_tensor(small[:, 3, :], small[:, 2, :], small[:, 1, :], ALU.subtract))
            link(dve.scalar_tensor_tensor(small[:, 4, :], small[:, 3, :], -1.0, ps_cnt[:, 0, :], ALU.add, ALU.add))
            for e in range(NEXP):
                ins = dve.scalar_tensor_tensor(rank[:, e, :], rank[:, e, :], small[:, 4, e:e + 1], hit[:, e, :],
                                               ALU.add, ALU.mult)
            link(ins)
            link(dve.tensor_tensor(rank[:, 0:4, :], rank[:, 0:4, :], rank[:, 4:8, :], ALU.add))
            link(dve.tensor_tensor(rank[:, 0:2, :], rank[:, 0:2, :], rank[:, 2:4, :], ALU.add))
            link(dve.tensor_tensor(pos[:, :], rank[:, 0, :], rank[:, 1, :], ALU.add))
            dve.tensor_copy(plan["slot"][:, :, :], pos[:, :].rearrange("p (i g) -> p i g", i=2)
                            ).then_inc(S["slots_ready"], 1)
            link(dve.tensor_scalar(tile_f[:, :], tile_no[:, :], small[0:1, 3, 1:2], None, ALU.is_ge))
            for e in range(2, NEXP):
                link(dve.scalar_tensor_tensor(tile_f[:, :], tile_no[:, :], small[0:1, 3, e:e + 1], tile_f[:, :],
                                              ALU.is_ge, ALU.add))
            link(dve.tensor_copy(plan["tile_expert"][:, :], tile_f[:, :]))

        @block.scalar
        def _(act):
            def linear(t, k):
                act.wait_ge(S["accT_ps"], t + 1)
                wait(act, S["o_ps"], t - 1)
                act.activation(accT[k][:, :, :], ps_T[k][:, :, :], ACT.Copy).then_inc(S["accT_ready"], 1)
            groups(act, linear)
            act.wait_ge(S["set2"], 5)
            act.wait_ge(S["var2"], 1)
            act.activation(std[:, :], mv[:, :, 1], ACT.Sqrt, bias=eps_t[:, :]).then_inc(S["std2_done"], 1)

            def router(t, k):
                act.wait_ge(S["x3T_ps"], t + 1)
                wait(act, S["l_ps"], t - 1)
                act.activation(x3Ts[k][:, :, :], ps_T[k][:, :, :], ACT.Copy).then_inc(S["x3T_ready"], 1)
            groups(act, router)
            act.wait_ge(S["gap_ready"], 1)
            act.activation(gap[:, 1, :], gap[:, 0, :], ACT.Exp).then_inc(S["exp2_ready"], 1)

        @block.tensor
        def _(pe):
            def transposes(t, k):
                pe.wait_ge(S["s1_ready"], t + 1)
                wait(pe, S["accT_ready"], t - 1)
                for c in range(4):
                    ins = pe.transpose(ps_T[k][:, c, :], s1[k][:, c * 128:(c + 1) * 128], keep["ident"][0:NG, 0:NG])
                ins.then_inc(S["accT_ps"], 1)

            def linear(t, k):
                if has(t + 1):
                    transposes(t + 1, 1 - k)
                pe.wait_ge(S["accT_ready"], t + 1)
                wait(pe, S["x2_ready"], 2 * t - 2)
                pe.matmul(ps_o[k][:, 0, :], accT[k][:, 0, :], wo0[:, :], start=True, stop=False)
                pe.matmul(ps_o[k][:, 0, :], ones_row[:, :], bo0[:, :], start=False, stop=True)
                for m in range(3):
                    ins = pe.matmul(ps_o[k][:, 1 + m, :], accT[k][:, 1 + m, :], wo1[:, :], start=True, stop=True)
                ins.then_inc(S["o_ps"], 1)
            transposes(0, 0)
            pe.wait_ge(S["params_in"], 16 * 5)
            pe.wait_ge(S["set2"], 5)
            groups(pe, linear)

            def normed(t, k):
                pe.wait_ge(S["x3s_ready"], t + 1)
                wait(pe, S["x3T_ready"], t - 1)
                for c in range(4):
                    ins = pe.transpose(ps_T[k][:, c, :], x3s[k][:, c * 128:(c + 1) * 128], keep["ident"][0:NG, 0:NG])
                ins.then_inc(S["x3T_ps"], 1)

            def router(t, k):
                if has(t + 1):
                    normed(t + 1, 1 - k)
                pe.wait_ge(S["x3T_ready"], t + 1)
                wait(pe, S["l_ready"], t - 1)
                for c in range(4):
                    pe.matmul(ps_l[k][:, :], x3Ts[k][:, c, :], rw[:, c, :], start=(c == 0), stop=False)
                pe.matmul(ps_l[k][:, :], ones_row[:, :], rb[:, :], start=False, stop=True).then_inc(S["l_ps"], 1)
            pe.wait_ge(S["accT_ready"], G)
            normed(0, 0)
            groups(pe, router)
            pe.wait_ge(S["tri_set"], 1)
            pe.wait_ge(S["totals2"], 1)
            pe.matmul(ps_cnt[:, 0, :], tri[:, :], small[:, 0, :], start=True, stop=True)
            pe.matmul(ps_cnt[:, 1, :], onesq[:, :], small[:, 0, :], start=True, stop=True).then_inc(S["prefixed2"], 1)


def experts(nc, a, keep, scratch, plan, out):
    FC = FF // 128
    J = TILE // 128
    U = 2
    ROUNDS = (TILES - 1) // U
    LAG = 2
    YG = G // 2
    HI, LO = 0, 1
    with ExitStack() as ctx:
        def sb(name, shape, dt=F32):
            return ctx.enter_context(nc.sbuf_tensor(name, shape, dt))

        def ps(name, shape, dt=F32):
            return ctx.enter_context(nc.psum_tensor(name, shape, dt))

        def sem(name):
            return ctx.enter_context(nc.semaphore(name))

        raw = [sb(f"raw{i}", [128, CHUNK]) for i in range(FC)]
        w1 = [sb(f"w1_{i}", [128, 2, 2 * D], F32R) for i in range(4)]
        w2 = [sb(f"w2_{i}", [128, 2, D], F32R) for i in range(FC)]
        xs = sb("xs_tile", [128, J, D])
        xT = [sb(f"xT_{i}", [128, 2, 4, TILE], F32R) for i in range(U)]
        b2_in = [sb(f"b2_in{i}", [2, D]) for i in range(U)]
        b2c = sb("b2c", [2, D], F32R)
        b2 = [sb(f"b2_{i}", [2, D], F32R) for i in range(U)]
        is_lo = sb("is_lo3", [2, 1])
        sign = sb("sign3", [2, 1])
        ones_f = sb("ones_f3", [2, 128])
        ones2 = sb("ones2", [2, 128], F32R)
        gate = sb("gate", [128, 2, TILE])
        act_f = sb("act_f", [128, 2, TILE])
        act_a = [sb(f"act_a{i}", [128, 2, TILE], F32R) for i in range(4)]
        y = sb("y", [128, J, D])
        yg = [keep["acc"][:, 2 * i:2 * i + 2, :] for i in range(YG)]
        ps_h = [ps(f"ps_h{i}", [128, 2, TILE]) for i in range(4)]
        ps_y = [ps(f"ps_y{i}", [128, D]) for i in range(J)]
        ps_x = [ps(f"ps_x{i}", [128, 4, 128]) for i in range(J)]
        names = ("set3 ones_ready xT_ps xT_hi xT_ready b2c_ready b2_ready w1_hi w1_ready w2_hi w2_ready gate_ready h_ps "
                 "a_ready a_hi a_split y_ps y_ready x4_first x4_done xs_in")
        S = {n: sem(n) for n in names.split()}
        raw_in = [sem(f"raw_in{i}") for i in range(FC)]
        y_out = sem("y_out")
        yg_in = [sem(f"yg_in{i}") for i in range(YG)]
        stored = sem("stored")
        block = ctx.enter_context(nc.Block())

        def has(s):
            return not isinstance(s, int) or 0 <= s < TILES

        def tiles(eng, body):
            for s in range(U):
                body(s, s)
            with eng.Fori(1, ROUNDS) as r:
                for k in range(U):
                    body(r * U + k, k)
            for s in range(ROUNDS * U, TILES):
                body(s, s % U)

        def chunk(s, f):
            return s + f // FC, f % FC, s * FC + f

        @block.sync
        def _(sp):
            def load(s, k):
                e = sp.value_load(plan["tile_expert"][0:1, bass.ds(s, 1)], min_val=0, max_val=NEXP - 1)
                wait(sp, S["xT_ps"], J * s)
                sp.dma_start(xs[:, :, :], scratch["x_slots"][bass.ds(s * TILE, TILE), :].rearrange("(j p) d -> p j d", p=128)
                             ).then_inc(S["xs_in"], 16)
                sp.dma_start(b2_in[k][:, :], a["b2"][bass.ds(e, 1)].rearrange("e p d -> p (e d)")).then_inc(S["xs_in"], 16)
                for f in range(FC):
                    wait(sp, S["a_ready"], s * FC + f - FC + 1)
                    sp.dma_start(raw[f][:, :], a["wc"][bass.ds(e, 1), f:f + 1].rearrange("e f p w -> p (e f w)")
                                 ).then_inc(raw_in[f], 16)
            tiles(sp, load)
            for t in range(G):
                sp.wait_ge(S["x4_done"], t + 1)
                sp.dma_start(out[t * NG:(t + 1) * NG, :], keep["x"][:, t, :]).then_inc(stored, 16)
            sp.wait_ge(stored, 16 * G)

        @block.gpsimd
        def _(pool):
            pool.wait_ge(y_out, 16 * TILES)
            for t in range(G):
                if t >= YG:
                    pool.wait_ge(S["x4_done"], t - YG + 1)
                for i in range(2):
                    pool.indirect_dma_start(
                        out=yg[t % YG][:, i, :], out_offset=None, in_=scratch["y_slots"],
                        in_offset=bass.IndirectOffsetOnAxis(ap=plan["slot"][:, i, t:t + 1], axis=0)
                    ).then_inc(yg_in[t % YG], 16)

        @block.scalar
        def _(act):
            def w1_hi(s, f):
                s, f, _ = chunk(s, f)
                if has(s):
                    act.wait_ge(raw_in[f], 16 * s + 16)
                    act.activation(w1[f % 4][:, HI, :], raw[f][:, 0:2 * D], ACT.Copy).then_inc(S["w1_hi"], 1)

            def w2_hi(s, f):
                s, f, _ = chunk(s, f)
                if has(s):
                    act.activation(w2[f][:, HI, :], raw[f][:, 2 * D:3 * D], ACT.Copy).then_inc(S["w2_hi"], 1)

            def tokens(s, k):
                for j in range(J):
                    act.wait_ge(S["xT_ps"], J * s + j + 1)
                    act.activation(xT[k][:, HI, :, j * 128:(j + 1) * 128], ps_x[j][:, :, :], ACT.Copy).then_inc(S["xT_hi"], 1)
                wait(act, S["b2_ready"], s)
                act.wait_ge(S["xs_in"], 32 * s + 32)
                act.activation(b2c[:, :], b2_in[k][:, :], ACT.Copy, scale=sign[:, :]).then_inc(S["b2c_ready"], 1)

            def results(s):
                wait(act, y_out, 16 * s)
                for j in range(J):
                    act.wait_ge(S["y_ps"], J * s + j + 1)
                    act.activation(y[:, j, :], ps_y[j][:, :], ACT.Copy).then_inc(S["y_ready"], 1)
                act.wait_ge(S["y_ready"], J * s + J)
                act.dma_start(scratch["y_slots"][bass.ds(s * TILE, TILE), :].rearrange("(j p) d -> p j d", p=128),
                              y[:, :, :]).then_inc(y_out, 16)

            def body(s, k):
                for f in range(FC):
                    n = s * FC + f
                    act.wait_ge(S["h_ps"], n + 1)
                    act.activation(gate[:, f % 2, :], ps_h[f % 4][:, 0, :], ACT.Silu,
                                   bias=raw[f][:, 3 * D:3 * D + 1]).then_inc(S["gate_ready"], 1)
                    w1_hi(s, f + LAG)
                    act.wait_ge(S["a_ready"], n + 1)
                    act.activation(act_a[f % 4][:, HI, :], act_f[:, f % 2, :], ACT.Copy).then_inc(S["a_hi"], 1)
                    w2_hi(s, f + LAG)
                    if f == LAG - 1 and has(s - 1):
                        results(s - 1)
                    if f == 5 and has(s + 1):
                        tokens(s + 1, (k + 1) % U)
            act.wait_ge(S["set3"], 5)
            act.activation(ones2[:, :], ones_f[:, :], ACT.Copy).then_inc(S["ones_ready"], 1)
            tokens(0, 0)
            for f in range(LAG):
                w1_hi(0, f)
                w2_hi(0, f)
            tiles(act, body)
            results(TILES - 1)
            act.wait_ge(y_out, 16 * TILES)

        @block.vector
        def _(dve):
            dve.memset(is_lo[:, :], 1.0).then_inc(S["set3"], 1)
            dve.memset(sign[:, :], -1.0).then_inc(S["set3"], 1)
            dve.memset(ones_f[:, :], 1.0).then_inc(S["set3"], 1)
            dve.wait_ge(S["set3"], 3)
            dve.memset(is_lo[0:1, :], 0.0).then_inc(S["set3"], 1)
            dve.memset(sign[0:1, :], 1.0).then_inc(S["set3"], 1)
            dve.wait_ge(S["set3"], 5)

            def w_lo(s, f):
                s, f, n = chunk(s, f)
                if has(s):
                    dve.wait_ge(S["w1_hi"], n + 1)
                    dve.tensor_tensor(w1[f % 4][:, LO, :], raw[f][:, 0:2 * D], w1[f % 4][:, HI, :].bitcast(F32),
                                      ALU.subtract).then_inc(S["w1_ready"], 1)
                    dve.wait_ge(S["w2_hi"], n + 1)
                    dve.tensor_tensor(w2[f][:, LO, :], raw[f][:, 2 * D:3 * D], w2[f][:, HI, :].bitcast(F32),
                                      ALU.subtract).then_inc(S["w2_ready"], 1)

            def tokens(s, k):
                for j in range(J):
                    dve.wait_ge(S["xT_hi"], J * s + j + 1)
                    at = slice(j * 128, (j + 1) * 128)
                    dve.tensor_tensor(xT[k][:, LO, :, at], ps_x[j][:, :, :], xT[k][:, HI, :, at].bitcast(F32),
                                      ALU.subtract).then_inc(S["xT_ready"], 1)
                dve.wait_ge(S["b2c_ready"], s + 1)
                dve.scalar_tensor_tensor(b2[k][:, :], b2_in[k][:, :], is_lo[:, :], b2c[:, :].bitcast(F32),
                                         ALU.mult, ALU.add).then_inc(S["b2_ready"], 1)

            def body(s, k):
                for f in range(FC):
                    n = s * FC + f
                    dve.wait_ge(S["gate_ready"], n + 1)
                    dve.scalar_tensor_tensor(act_f[:, f % 2, :], ps_h[f % 4][:, 1, :], raw[f][:, 3 * D + 1:3 * D + 2],
                                             gate[:, f % 2, :], ALU.add, ALU.mult).then_inc(S["a_ready"], 1)
                    dve.wait_ge(S["a_hi"], n + 1)
                    dve.tensor_tensor(act_a[f % 4][:, LO, :], act_f[:, f % 2, :], act_a[f % 4][:, HI, :].bitcast(F32),
                                      ALU.subtract).then_inc(S["a_split"], 1)
                    w_lo(s, f + LAG)
                    if f == 5 and has(s + 1):
                        tokens(s + 1, (k + 1) % U)
            tokens(0, 0)
            for f in range(LAG):
                w_lo(0, f)
            tiles(dve, body)
            for t in range(G):
                dve.wait_ge(yg_in[t % YG], 32 * (t // YG + 1))
                x_t = keep["x"][:, t, :]
                dve.scalar_tensor_tensor(x_t, yg[t % YG][:, 0, :], plan["weight"][:, 0, t:t + 1], x_t,
                                         ALU.mult, ALU.add).then_inc(S["x4_first"], 1)
                dve.wait_ge(S["x4_first"], t + 1)
                dve.scalar_tensor_tensor(x_t, yg[t % YG][:, 1, :], plan["weight"][:, 1, t:t + 1], x_t,
                                         ALU.mult, ALU.add).then_inc(S["x4_done"], 1)

        @block.tensor
        def _(pe):
            def transposes(s):
                pe.wait_ge(S["xs_in"], 32 * s + 32)
                wait(pe, S["xT_ready"], J * s)
                for j in range(J):
                    for c in range(4):
                        ins = pe.transpose(ps_x[j][:, c, :], xs[:, j, c * 128:(c + 1) * 128], keep["ident"][:, :])
                    ins.then_inc(S["xT_ps"], 1)

            def up(s, k, f):
                n = s * FC + f
                if f == 0:
                    pe.wait_ge(S["xT_ready"], J * s + J)
                pe.wait_ge(S["w1_ready"], n + 1)
                wait(pe, S["a_ready"], n - 3)
                for h in range(2):
                    for c in range(4):
                        at = (2 * c + h) * 128
                        for i, x in ((HI, HI), (HI, LO), (LO, HI)):
                            ins = pe.matmul(ps_h[f % 4][:, h, :], w1[f % 4][:, i, at:at + 128], xT[k][:, x, c, :],
                                            start=(c == 0 and i == x), stop=(c == 3 and i == LO))
                ins.then_inc(S["h_ps"], 1)

            def down(s, k, f):
                s, f, n = chunk(s, f)
                if not has(s):
                    return
                if f == 0:
                    wait(pe, S["y_ready"], J * s)
                    pe.wait_ge(S["b2_ready"], s + 1)
                    for j in range(J):
                        pe.matmul(ps_y[j][:, :], ones2[:, :], b2[k][:, :], start=True, stop=False)
                pe.wait_ge(S["w2_ready"], n + 1)
                pe.wait_ge(S["a_split"], n + 1)
                for j in range(J):
                    for i, v in ((HI, HI), (HI, LO), (LO, HI)):
                        ins = pe.matmul(ps_y[j][:, :], act_a[f % 4][:, i, j * 128:(j + 1) * 128], w2[f][:, v, :],
                                        start=False, stop=(f == FC - 1 and i == LO))
                    if f == FC - 1:
                        ins.then_inc(S["y_ps"], 1)

            def body(s, k):
                for f in range(FC):
                    up(s, k, f)
                    down(s, k if f >= LAG else (k + 1) % U, f - LAG)
                    if f == 4 and has(s + 1):
                        transposes(s + 1)
            pe.wait_ge(S["ones_ready"], 1)
            transposes(0)
            tiles(pe, body)
            for f in range(LAG):
                down(TILES, (TILES - 1) % U, f - LAG)


_INS = ["x", "src", "dst", "rec", "L0_gnn_W_pre0", "L0_gnn_b_pre0", "L0_gnn_W_pre1", "L0_gnn_W_nd0", "L0_gnn_b_nd0",
        "L0_gnn_W_nd1", "L0_gnn_W_g1", "bg1", "L0_gnn_W_g2", "bg2", "L0_gnn_W_f1", "wf2",
        "L0_gnn_W_s1", "ws2", "L0_gnn_W_o0", "L0_gnn_b_o0", "L0_gnn_W_o1", "rw", "L0_ffn_router_b", "wc", "b2"]


def program(nc, a, out):
    with ExitStack() as ctx:
        keep = {}

        def sb(name, shape, dt=F32):
            keep[name] = ctx.enter_context(nc.sbuf_tensor(name, shape, dt))
        scratch = {"sorted": nc.dram_tensor("sorted_recs", (STEPS * STEP, REC), F32, kind="Internal").ap(),
                   "x_slots": nc.dram_tensor("x_slots", (TILES * TILE, D), F32, kind="Internal").ap(),
                   "y_slots": nc.dram_tensor("y_slots", (TILES * TILE, D), F32, kind="Internal").ap(),
                   "rows": nc.dram_tensor("node_rows", (N, ROW), F32, kind="Internal").ap()}
        sb("x", [NG, G, D])
        sb("acc", [NG, G, D])
        sb("ident", [128, 128])
        sb("half", [128, 1])
        with ExitStack() as gnn:
            ctx_, ctx = ctx, gnn
            sb("iota", [128, NG])
            sb("step_group", [1, STEPS], I32)
            sb("tab", [NG, G, 2, 4 * MUL], F32R)
            sb("wf1", [RECK, 4, HID])
            sb("ws1c", [128, 4, HID])
            sb("w2", [128, 2, 4 * MUL], F32R)
            prepare(nc, a, keep, scratch)
            edges(nc, keep, scratch)
            ctx = ctx_
        ffn(nc, a, keep, scratch, out)


def kernel(**inputs):
    import concourse.bacc as _bacc
    from concourse.bass_utils import run_bass_kernel_spmd as _run

    i = {k: np.ascontiguousarray(v) for k, v in inputs.items()}
    rec = np.zeros((E, REC), np.float32)
    rec[:, SH:SH + 4] = i["edge_attr_4"]
    rec[:, ATTR:RECK] = i["edge_attr_32"]
    i["rec"] = rec

    def by_path(w):
        return np.ascontiguousarray(w.reshape(HID, 4, MUL)[:, [0, 2, 1, 3], :].reshape(HID, 4 * MUL))
    i["wf2"], i["ws2"] = by_path(i["L0_gnn_W_f2"]), by_path(i["L0_gnn_W_s2"])
    for n in ("1", "2"):
        i["bg" + n] = np.ascontiguousarray(i["L0_gnn_b_g" + n].reshape(2, 128).T)
    i["rw"] = np.ascontiguousarray(i["L0_ffn_router_w"].T)
    fc = FF // 128
    w1 = i["L0_ffn_fc1_w"].reshape(NEXP, 2, fc, 128, 4, 128).transpose(0, 2, 5, 4, 1, 3).reshape(NEXP, fc, 128, 2 * D)
    w2 = i["L0_ffn_fc2_w"].reshape(NEXP, D, fc, 128).transpose(0, 2, 3, 1)
    b1 = i["L0_ffn_fc1_b"].reshape(NEXP, 2, fc, 128).transpose(0, 2, 3, 1)
    i["wc"] = np.ascontiguousarray(np.concatenate([w1, w2, b1], axis=-1))
    i["b2"] = np.ascontiguousarray(np.stack([i["L0_ffn_fc2_b"]] * 2, axis=1))
    nc = _bacc.Bacc("TRN2", target_bir_lowering=False, num_devices=1)
    arrays = {"in_" + n: i[n] for n in _INS}
    a = {n: nc.dram_tensor("in_" + n, i[n].shape, mybir.dt.from_np(i[n].dtype), kind="ExternalInput").ap() for n in _INS}
    out = nc.dram_tensor("out_x", (N, D), F32, kind="ExternalOutput").ap()
    program(nc, a, out)
    return _run(nc, [arrays], core_ids=[0]).results[0]["out_x"]
```
